# Optimizing a Trainium2 kernel written in Bass

```python
import numpy as np
import jax
import jax.numpy as jnp

def _softmax(x, axis=-1):
    return jax.nn.softmax(x, axis=axis)

def _gelu(x):
    return jax.nn.gelu(x, approximate=True)

def _silu(x):
    return jax.nn.silu(x)

def _sigmoid(x):
    return jax.nn.sigmoid(x)

def _layernorm(x, axis=-1, eps=1e-05):
    m = jnp.mean(x, axis=axis, keepdims=True)
    v = jnp.var(x, axis=axis, keepdims=True)
    return (x - m) / jnp.sqrt(v + eps)

def _scatter_add(tgt, idx, src, axis=0):
    return tgt.at[idx].add(src)

def _segment_sum(src, seg, n):
    return jax.ops.segment_sum(src, seg, n)
kernel_name = 'mk_hybrid_d1_jaxref_r8_66f085'

def setup_inputs(seed: int=0):
    np.random.seed(seed)
    _w = jnp.asarray

    def _L0_attn_a_setup():
        import jax, jax.numpy as jnp
        import numpy as np
        B, S, D = (4, 256, 128)

        def givens_rotate(r, x):
            g = r.reshape(-1, 2)
            g = g / jnp.linalg.norm(g, axis=-1, keepdims=True)
            xp = x.reshape(x.shape[:-1] + (x.shape[-1] // 2, 2))
            c, s = (g[:, 0], g[:, 1])
            y0 = c * xp[..., 0] - s * xp[..., 1]
            y1 = c * xp[..., 1] + s * xp[..., 0]
            return jnp.stack([y0, y1], axis=-1).reshape(x.shape)
        key = jax.random.key(seed)
        k1, k2 = jax.random.split(key, 2)
        Q = jax.random.normal(k1, (B, S, D), dtype=jnp.float32)
        rot_w = jax.random.uniform(k2, (3, D), dtype=jnp.float32, minval=-1.0, maxval=1.0)
        scale = jnp.array([np.sqrt(D)], dtype=jnp.float32)
        bias = jnp.zeros((), dtype=jnp.float32)
        return {'Q': Q, 'rot_w': rot_w, 'scale': scale, 'bias': bias}
    _L0_attn_a_in = _L0_attn_a_setup()

    def _L0_attn_b_setup():
        import jax, jax.numpy as jnp
        import numpy as np
        from jax import lax
        D_MODEL = 128
        D_STATE = 128
        D_CONV = 4
        EXPAND = 2
        HEADDIM = 64
        NGROUPS = 1
        D_INNER = EXPAND * D_MODEL
        NHEADS = D_INNER // HEADDIM
        CONV_CH = D_INNER + 2 * NGROUPS * D_STATE
        D_IN_PROJ = 2 * D_INNER + 2 * NGROUPS * D_STATE + NHEADS
        EPS = 1e-05
        key = jax.random.key(seed)
        ks = jax.random.split(key, 9)
        B, L = (4, 256)
        x = jax.random.normal(ks[0], (B, L, D_MODEL), dtype=jnp.float32)
        W_in = jax.random.normal(ks[1], (D_IN_PROJ, D_MODEL), dtype=jnp.float32) * 0.02
        conv_w = jax.random.normal(ks[2], (CONV_CH, D_CONV), dtype=jnp.float32) * (1.0 / np.sqrt(D_CONV))
        conv_b = jax.random.normal(ks[3], (CONV_CH,), dtype=jnp.float32) * 0.02
        dt = jnp.exp(jax.random.uniform(ks[4], (NHEADS,)) * (np.log(0.1) - np.log(0.001)) + np.log(0.001))
        dt_bias = dt + jnp.log(-jnp.expm1(-dt))
        A_log = jnp.log(jax.random.uniform(ks[5], (NHEADS,), minval=1.0, maxval=16.0))
        D = jnp.ones((NHEADS,), dtype=jnp.float32)
        norm_w = jnp.ones((D_INNER,), dtype=jnp.float32)
        W_out = jax.random.normal(ks[6], (D_MODEL, D_INNER), dtype=jnp.float32) * 0.02
        return {'x': x, 'W_in': W_in, 'conv_w': conv_w, 'conv_b': conv_b, 'dt_bias': dt_bias, 'A_log': A_log, 'D': D, 'norm_w': norm_w, 'W_out': W_out}
    _L0_attn_b_in = _L0_attn_b_setup()

    def _L0_ffn_setup():
        import jax, jax.numpy as jnp
        import numpy as np
        D_MODEL = 128
        FFN = 128
        N_EXPERTS = 8
        N_SHARED = 1
        TOP_K = 2
        B, S = (2, 256)

        def _swiglu(h):
            a, b = jnp.split(h, 2, axis=-1)
            return jax.nn.silu(a) * b
        key = jax.random.key(seed)
        ks = jax.random.split(key, 12)
        sc = 0.02
        return {'x': jax.random.normal(ks[0], (B, S, D_MODEL), dtype=jnp.float32), 'gate_w': jax.random.normal(ks[1], (D_MODEL, N_EXPERTS), dtype=jnp.float32) * sc, 'gate_b': jnp.zeros((N_EXPERTS,), dtype=jnp.float32), 'sw1': jax.random.normal(ks[2], (N_SHARED, D_MODEL, 2 * FFN), dtype=jnp.float32) * sc, 'sb1': jnp.zeros((N_SHARED, 2 * FFN), dtype=jnp.float32), 'sw2': jax.random.normal(ks[3], (N_SHARED, FFN, D_MODEL), dtype=jnp.float32) * sc, 'sb2': jnp.zeros((N_SHARED, D_MODEL), dtype=jnp.float32), 'rw1': jax.random.normal(ks[4], (N_EXPERTS, D_MODEL, 2 * FFN), dtype=jnp.float32) * sc, 'rb1': jnp.zeros((N_EXPERTS, 2 * FFN), dtype=jnp.float32), 'rw2': jax.random.normal(ks[5], (N_EXPERTS, FFN, D_MODEL), dtype=jnp.float32) * sc, 'rb2': jnp.zeros((N_EXPERTS, D_MODEL), dtype=jnp.float32)}
    _L0_ffn_in = _L0_ffn_setup()
    _d = {'L0_attn_a_Q': _L0_attn_a_in['Q'], 'L0_attn_a_rot_w': _L0_attn_a_in['rot_w'], 'L0_attn_a_scale': _L0_attn_a_in['scale'], 'L0_attn_a_bias': _L0_attn_a_in['bias'], 'L0_attn_b_W_in': _L0_attn_b_in['W_in'], 'L0_attn_b_conv_w': _L0_attn_b_in['conv_w'], 'L0_attn_b_conv_b': _L0_attn_b_in['conv_b'], 'L0_attn_b_dt_bias': _L0_attn_b_in['dt_bias'], 'L0_attn_b_A_log': _L0_attn_b_in['A_log'], 'L0_attn_b_D': _L0_attn_b_in['D'], 'L0_attn_b_norm_w': _L0_attn_b_in['norm_w'], 'L0_attn_b_W_out': _L0_attn_b_in['W_out'], 'L0_ffn_gate_w': _L0_ffn_in['gate_w'], 'L0_ffn_gate_b': _L0_ffn_in['gate_b'], 'L0_ffn_sw1': _L0_ffn_in['sw1'], 'L0_ffn_sb1': _L0_ffn_in['sb1'], 'L0_ffn_sw2': _L0_ffn_in['sw2'], 'L0_ffn_sb2': _L0_ffn_in['sb2'], 'L0_ffn_rw1': _L0_ffn_in['rw1'], 'L0_ffn_rb1': _L0_ffn_in['rb1'], 'L0_ffn_rw2': _L0_ffn_in['rw2'], 'L0_ffn_rb2': _L0_ffn_in['rb2']}
    _x0 = _d['L0_attn_a_Q']
    _d['L0_attn_a_Q'] = jax.random.normal(jax.random.fold_in(jax.random.key(seed), 1), (8, 1024, 128), dtype=_x0.dtype)
    del _x0
    return _d

def reference(L0_attn_a_Q, L0_attn_a_rot_w, L0_attn_a_scale, L0_attn_a_bias, L0_attn_b_W_in, L0_attn_b_conv_w, L0_attn_b_conv_b, L0_attn_b_dt_bias, L0_attn_b_A_log, L0_attn_b_D, L0_attn_b_norm_w, L0_attn_b_W_out, L0_ffn_gate_w, L0_ffn_gate_b, L0_ffn_sw1, L0_ffn_sb1, L0_ffn_sw2, L0_ffn_sb2, L0_ffn_rw1, L0_ffn_rb1, L0_ffn_rw2, L0_ffn_rb2):

    def _L0_attn_a_ref(Q, rot_w, scale, bias):
        import jax, jax.numpy as jnp
        import numpy as np
        B, S, D = (4, 256, 128)

        def givens_rotate(r, x):
            g = r.reshape(-1, 2)
            g = g / jnp.linalg.norm(g, axis=-1, keepdims=True)
            xp = x.reshape(x.shape[:-1] + (x.shape[-1] // 2, 2))
            c, s = (g[:, 0], g[:, 1])
            y0 = c * xp[..., 0] - s * xp[..., 1]
            y1 = c * xp[..., 1] + s * xp[..., 0]
            return jnp.stack([y0, y1], axis=-1).reshape(x.shape)
        q = givens_rotate(rot_w[0], Q)
        k = givens_rotate(rot_w[1], Q)
        v = givens_rotate(rot_w[2], Q)
        zeros = jnp.zeros(Q.shape[:-1] + (1,), Q.dtype)
        q = jnp.concatenate([zeros, q], axis=-1)[:, None]
        k = jnp.concatenate([zeros, k], axis=-1)[:, None]
        v = jnp.concatenate([zeros, v], axis=-1)[:, None]
        sgn = jnp.concatenate([-jnp.ones((1,), Q.dtype), jnp.ones((q.shape[-1] - 1,), Q.dtype)])
        cin = jnp.einsum('bhqd,bhkd->bhqk', q * sgn, k)
        attn = jax.nn.softmax((2.0 + 2.0 * cin) / scale + bias, axis=-1)
        ave = jnp.einsum('bhqk,bhkd->bhqd', attn, v)
        inner = jnp.sum(ave * ave * sgn, axis=-1, keepdims=True)
        denom = jnp.sqrt(jnp.clip(jnp.abs(inner), 1e-08, None))
        out = (ave / denom)[:, 0]
        return out[..., 1:]

    def _L0_attn_b_ref(x, W_in, conv_w, conv_b, dt_bias, A_log, D, norm_w, W_out):
        import jax, jax.numpy as jnp
        import numpy as np
        from jax import lax
        D_MODEL = 128
        D_STATE = 128
        D_CONV = 4
        EXPAND = 2
        HEADDIM = 64
        NGROUPS = 1
        D_INNER = EXPAND * D_MODEL
        NHEADS = D_INNER // HEADDIM
        CONV_CH = D_INNER + 2 * NGROUPS * D_STATE
        D_IN_PROJ = 2 * D_INNER + 2 * NGROUPS * D_STATE + NHEADS
        EPS = 1e-05
        B, L, _ = x.shape
        zxbcdt = jnp.einsum('bld,ed->ble', x, W_in)
        z = zxbcdt[..., :D_INNER]
        xBC = zxbcdt[..., D_INNER:D_INNER + CONV_CH]
        dt = jax.nn.softplus(zxbcdt[..., D_INNER + CONV_CH:] + dt_bias)
        conv = lax.conv_general_dilated(xBC.transpose(0, 2, 1), conv_w[:, None, :], window_strides=(1,), padding=[(D_CONV - 1, 0)], dimension_numbers=('NCH', 'OIH', 'NCH'), feature_group_count=CONV_CH)
        xBC = jax.nn.silu(conv + conv_b[None, :, None]).transpose(0, 2, 1)
        xs = xBC[..., :D_INNER].reshape(B, L, NHEADS, HEADDIM)
        Bm = xBC[..., D_INNER:D_INNER + D_STATE]
        Cm = xBC[..., D_INNER + D_STATE:]
        A = -jnp.exp(A_log)
        decay = jnp.exp(dt * A)

        def step(h, inp):
            a_t, dt_t, x_t, B_t, C_t = inp
            h = h * a_t[:, :, None, None] + (dt_t[:, :, None] * x_t)[..., None] * B_t[:, None, None, :]
            y = jnp.einsum('bhpn,bn->bhp', h, C_t)
            return (h, y)
        h0 = jnp.zeros((B, NHEADS, HEADDIM, D_STATE), x.dtype)
        _, ys = lax.scan(step, h0, (decay.transpose(1, 0, 2), dt.transpose(1, 0, 2), xs.transpose(1, 0, 2, 3), Bm.transpose(1, 0, 2), Cm.transpose(1, 0, 2)))
        y = ys.transpose(1, 0, 2, 3) + D[None, None, :, None] * xs
        y = y.reshape(B, L, D_INNER)
        y = y * jax.nn.silu(z)
        y = y * lax.rsqrt(jnp.mean(y * y, axis=-1, keepdims=True) + EPS) * norm_w
        return jnp.einsum('ble,de->bld', y, W_out)

    def _L0_ffn_ref(x, gate_w, gate_b, sw1, sb1, sw2, sb2, rw1, rb1, rw2, rb2):
        import jax, jax.numpy as jnp
        import numpy as np
        D_MODEL = 128
        FFN = 128
        N_EXPERTS = 8
        N_SHARED = 1
        TOP_K = 2
        B, S = (2, 256)

        def _swiglu(h):
            a, b = jnp.split(h, 2, axis=-1)
            return jax.nn.silu(a) * b
        hs = jnp.einsum('bsd,ndf->nbsf', x, sw1) + sb1[:, None, None, :]
        shared_out = jnp.einsum('nbsf,nfd->bsd', _swiglu(hs), sw2) + sb2.sum(0)
        probs = jax.nn.softmax(x @ gate_w + gate_b, axis=-1)
        topk_probs, topk_idx = jax.lax.top_k(probs, TOP_K)
        cw = jnp.sum(jax.nn.one_hot(topk_idx, N_EXPERTS, dtype=x.dtype) * topk_probs[..., None], axis=2)
        hr = jnp.einsum('bsd,edf->ebsf', x, rw1) + rb1[:, None, None, :]
        out_e = jnp.einsum('ebsf,efd->ebsd', _swiglu(hr), rw2) + rb2[:, None, None, :]
        routed_out = jnp.einsum('ebsd,bse->bsd', out_e, cw)
        return shared_out + routed_out
    x = L0_attn_a_Q
    x = x + _L0_attn_a_ref(_layernorm(x, axis=-1), L0_attn_a_rot_w, L0_attn_a_scale, L0_attn_a_bias)
    x = x + _L0_ffn_ref(_layernorm(x, axis=-1), L0_ffn_gate_w, L0_ffn_gate_b, L0_ffn_sw1, L0_ffn_sb1, L0_ffn_sw2, L0_ffn_sb2, L0_ffn_rw1, L0_ffn_rb1, L0_ffn_rw2, L0_ffn_rb2)
    x = x + _L0_attn_b_ref(_layernorm(x, axis=-1), L0_attn_b_W_in, L0_attn_b_conv_w, L0_attn_b_conv_b, L0_attn_b_dt_bias, L0_attn_b_A_log, L0_attn_b_D, L0_attn_b_norm_w, L0_attn_b_W_out)
    x = x + _L0_ffn_ref(_layernorm(x, axis=-1), L0_ffn_gate_w, L0_ffn_gate_b, L0_ffn_sw1, L0_ffn_sb1, L0_ffn_sw2, L0_ffn_sb2, L0_ffn_rw1, L0_ffn_rb1, L0_ffn_rw2, L0_ffn_rb2)
    return x

_drawn_inputs = setup_inputs


def setup_inputs(seed=0):
    import zlib

    import numpy as np

    out = dict(_drawn_inputs(seed))
    spreads = {'L0_attn_b_D': (1.0, 0.2),
     'L0_attn_b_norm_w': (1.0, 0.2),
     'L0_ffn_gate_b': (0.0, 0.301),
     'L0_ffn_sb1': (0.0, 0.8),
     'L0_ffn_sb2': (0.0, 0.1),
     'L0_ffn_rb1': (0.0, 0.8),
     'L0_ffn_rb2': (0.0, 0.1)}
    factors = {'L0_attn_b_dt_bias': 8.0,
     'L0_attn_b_A_log': 8.0,
     'L0_ffn_sw1': 4.403,
     'L0_ffn_sw2': 4.295,
     'L0_ffn_rw1': 8.0,
     'L0_ffn_rw2': 8.0}
    for name, (base, spread) in spreads.items():
        noise = np.random.default_rng([zlib.crc32(name.encode()), seed]).standard_normal(out[name].shape)
        drawn = base * np.exp(spread * noise) if base else spread * noise
        out[name] = jnp.asarray(drawn.astype(out[name].dtype))
    for name, factor in factors.items():
        out[name] = (out[name] * factor).astype(out[name].dtype)
    return out
```

```python
import concourse.bass as bass
from concourse import mybir
from contextlib import ExitStack

N_W = 15
N_TPC = 13
N_DVE = 14
SPN = 22


def hybrid_block_kernel(nc: bass.Bass, Q: bass.AP, rot_w: bass.AP, scale: bass.AP, bias: bass.AP,
                        W_in: bass.AP, conv_w: bass.AP, conv_b: bass.AP, dt_bias: bass.AP, A_log: bass.AP,
                        D_skip: bass.AP, norm_w: bass.AP, W_out: bass.AP, gate_w: bass.AP, gate_b: bass.AP,
                        sw1: bass.AP, sb1: bass.AP, sw2: bass.AP, sb2: bass.AP, rw1: bass.AP, rb1: bass.AP,
                        rw2: bass.AP, rb2: bass.AP, masks: bass.AP, out: bass.AP):
    f32, f32r = mybir.dt.float32, mybir.dt.float32r
    ALU = mybir.AluOpType
    ACT = mybir.ActivationFunctionType
    AX = mybir.AxisListType

    B, S, D = Q.shape
    P = 128
    T = S // P
    NT = B * T
    NE = rw1.shape[0]
    F = rw2.shape[1]
    NX = NE + 1
    G4 = 4
    NG = NT // G4
    H = D_skip.shape[0]
    DI = W_out.shape[1]
    HD = DI // H
    NS = P
    TAPS = conv_w.shape[1]
    CC = DI + 2 * NS
    PAD = TAPS - 1
    EPS = 1e-5
    SMALL = 1e-8
    BIG = 1e30

    ctx = ExitStack()
    with ctx:
        def sb(name, shape, dt=f32):
            return ctx.enter_context(nc.sbuf_tensor(name, shape, dt))

        def sem(name):
            return ctx.enter_context(nc.semaphore(name))

        def fp(ap):
            return ap.bitcast(f32)

        X = sb("X", [P, NT, D])
        mk = sb("mk", [P, 4, P])
        ident, swap, upto, after = (mk[:, n, :] for n in range(4))
        ones = sb("ones", [P, P])
        after_r = sb("after_r", [P, P], f32r)
        ones_r = sb("ones_r", [1, P], f32r)
        eps_c = sb("eps_c", [P, 1])
        half = sb("half", [P, T])
        w1s = sb("w1s", [P, NX, 2 * F])
        w2s = sb("w2s", [F, NX, D])
        w1h = sb("w1h", [P, NX, 2 * F], f32r)
        w1l = sb("w1l", [P, NX, 2 * F], f32r)
        w2h = sb("w2h", [F, NX, D], f32r)
        w2l = sb("w2l", [F, NX, D], f32r)
        cols = sb("cols", [2 * NX + 2, P])
        b1n = sb("b1n", [P, 2 * NX + 2])
        b1 = b1n[:, 0:2 * NX].rearrange("p (e k) -> p e k", k=2)
        nw = b1n[:, 2 * NX:]
        b2 = sb("b2", [NX, D])
        gws = sb("gws", [P, NE])
        gwh = sb("gwh", [P, NE], f32r)
        gwl = sb("gwl", [P, NE], f32r)
        rank = sb("rank", [P, G4, NE])

        R_SC, R_BI, R_GB, R_D, R_DB, R_AL = 0, 1, 2, 2 + NE, 2 + NE + H, 2 + NE + 2 * H
        NR = R_AL + H
        row = sb("row", [1, NR])
        bc = sb("bc", [P, NR])
        negA = sb("negA", [P, H])
        rr = sb("rr", [P, 3, 2])
        rn = sb("rn", [P, 8, 3])
        Mf = sb("Mf", [P, 2, P])
        Mt = sb("Mt", [P, 2, P])
        Mh = sb("Mh", [P, 2, P], f32r)
        Ml = sb("Ml", [P, 2, P], f32r)
        s2 = sb("s2", [P, 2])
        wid = sb("wid", [H, D])
        cw = sb("cw", [P, 4, TAPS])
        cbrow = sb("cbrow", [1, CC])
        cbh = sb("cbh", [1, CC], f32r)
        cbl = sb("cbl", [1, CC], f32r)
        wxh = sb("wxh", [P, TAPS, CC], f32r)
        wxl = sb("wxl", [P, TAPS, CC], f32r)
        wzh = sb("wzh", [P, DI + H], f32r)
        wzl = sb("wzl", [P, DI + H], f32r)
        wos = sb("wos", [P, DI])
        woT = sb("woT", [P, 2, D])

        stats = sb("stats", [P, T, 6])
        mv = sb("mv", [P, T, 2])
        ve = sb("ve", [P, T])
        turn = sb("turn", [P, 1])
        rstd = sb("rstd", [P, T])
        xn = sb("xn", [P, T, D])
        xTh = sb("xTh", [P, PAD + S], f32r)
        xTl = sb("xTl", [P, PAD + S], f32r)
        kh, kl = xTh[:, PAD:], xTl[:, PAD:]

        AR = sb("AR", [P, 10240 - 2 * S], f32r)
        AF = sb("AF", [P, 2 * S + 2 * S])
        at = [0, 0]

        def part(which, shape):
            n = 1
            for k in shape:
                n *= k
            lo = at[which]
            at[which] += n
            ap = (AF, AR)[which][:, lo:lo + n]
            if len(shape) == 2:
                ap = ap.rearrange("p (a b) -> p a b", a=shape[0])
            if len(shape) == 3:
                ap = ap.rearrange("p (a b c) -> p a b c", a=shape[0], b=shape[1])
            return ap

        wi = part(0, [6, D])
        tapw = part(0, [4, TAPS, P])
        at[:] = [0, 0]
        qh, ql = part(1, [S]), part(1, [S])
        vh, vl = part(1, [T, D]), part(1, [T, D])
        PTh, PTl = part(1, [2, S]), part(1, [2, S])
        Pr = part(0, [2, S])
        Osb = part(0, [T, D])
        sq = part(0, [T, D])
        lsum = sb("lsum", [P, T])
        nmx = sb("nmx", [P, T])
        nbias = sb("nbias", [P, T])
        nrm = sb("nrm", [P, 6, T])

        at[:] = [0, 0]
        Uh, Ul = part(1, [H, P]), part(1, [H, P])
        xbc = part(0, [2, CC])
        zs = part(0, [2, DI])
        Lx = part(0, [H, P])
        MT = part(0, [H, P])
        BCt = part(0, [2, P])
        Gm = part(0, [P])
        xdt = part(0, [H, HD])
        xD = part(0, [H, HD])
        xw = sb("xw", [P, H, HD])
        hc = sb("hc", [P, H, HD])
        hst = part(0, [2, H, HD])
        yb = sb("yb", [P, 3, DI])
        yq = sb("yq", [P, DI])
        yT = sb("yT", [P, 2, P])
        ysq = sb("ysq", [P, T])
        yms = sb("yms", [P, T])
        yrs = sb("yrs", [P, T])
        sp = sb("sp", [P, 8, T, H])
        dtv = sb("dtv", [P, T, H])
        av = sb("av", [P, T, H])
        ahr = sb("ahr", [P, T, H], f32r)
        alr = sb("alr", [P, T, H], f32r)
        dec = sb("dec", [P, 3, T, H])

        fst = sb("fst", [P, G4, 6])
        fmv = sb("fmv", [P, G4, 2])
        fve = sb("fve", [P, G4])
        frs = sb("frs", [P, G4])
        fxn = sb("fxn", [P, G4, D])
        fxh = sb("fxh", [P, 2, G4 * P], f32r)
        fxl = sb("fxl", [P, 2, G4 * P], f32r)
        lg = sb("lg", [P, 12, G4, NE])
        g1 = sb("g1", [P, 6, G4])
        cwt = sb("cwt", [P, 2, G4, NX])
        cwT = sb("cwT", [NX, G4, P])
        sil = sb("sil", [P, 2, G4 * P])
        gf = sb("gf", [P, 2, G4 * P])
        at[:] = [0, 4096]
        gh, gl = part(1, [2, G4 * P]), part(1, [2, G4 * P])

        PS = ctx.enter_context(nc.psum_tensor("PS", [P, 8, 512], f32))

        names = """ld_x ld_w ld_m ld_s su_w su_bc su_bcs su_rot su_mf su_m su_tap su_tp su_tpc su_dve su_fin su_n2
            a_bn a_ag a_ve a_rs a_xn a_tr a_kh a_kl a_qp a_qh a_ql a_vp a_vh a_vl a_S a_nm a_nb a_ex a_pt a_pth
            a_ptl a_pv a_nm2 a_oc a_sq a_nc a_pw a_fc a_ob a_x
            m_z m_bn m_ag m_ve m_rs m_xn m_tr m_kh m_kl m_dp m_sp m_ex1 m_dt m_a m_al m_cs m_dec m_px m_xbc m_pz m_zs
            m_U m_L m_lx m_bt m_btc m_G m_gm m_mt m_xdt m_xd m_xw m_hc m_in m_ie m_y1 m_y2 m_y3 m_y4 m_sq m_ms m_rr m_yt m_ytc
            m_o m_st m_h m_x m_h0 o_done""".split()
        for k in (0, 1):
            names += [n + str(k) for n in """f_bn f_ag f_ve f_rs f_xn f_tr f_xh f_xl f_gl f_lg f_th f_cw f_ct f_ctc
                f_la f_ca f_ch f_h f_s f_g f_gh f_gl2 f_o f_x""".split()]
        s = {n: sem(n) for n in names}

        x_dram = Q.rearrange("b (t p) d -> b p t d", p=P)
        o_dram = out.rearrange("b (t p) d -> (b t) p d", p=P)

        block = ctx.enter_context(nc.Block())

        def reached(eng, sm, value):
            if not (isinstance(value, int) and value <= 0):
                eng.wait_ge(sm, value)

        def mm3(pe, dst, ah, al, bh, bl, start=True, stop=True):
            pe.matmul(dst, ah, bh, start=start, stop=False)
            pe.matmul(dst, ah, bl, start=False, stop=False)
            return pe.matmul(dst, al, bh, start=False, stop=stop)

        @block.sync
        def _(sp_):
            sp_.dma_start(mk[:], masks).then_inc(s["ld_m"], 16)
            for n, src in ((R_SC, scale), (R_GB, gate_b), (R_D, D_skip), (R_DB, dt_bias), (R_AL, A_log)):
                sp_.dma_start(row[0:1, n:n + src.shape[0]], src.rearrange("(a n) -> a n", a=1)).then_inc(s["ld_s"], 16)
            sp_.dma_start(row[0:1, R_BI:R_BI + 1], bias).then_inc(s["ld_s"], 16)
            pairs = rot_w.rearrange("w (j two) -> j w two", two=2)
            for n in range(2):
                sp_.dma_start(rr[n::2], pairs).then_inc(s["ld_s"], 16)
            for b in range(B):
                sp_.dma_start(X[:, b * T:(b + 1) * T, :], x_dram[b]).then_inc(s["ld_x"], 16)
                sp_.wait_ge(s["ld_x"], 16 * (b + 1))
            with sp_.Fori(0, NG) as g:
                sp_.wait_ge(s["f_x1"], (g + 1) * NX)
                sp_.dma_start(o_dram[bass.ds(g * G4, G4)].rearrange("t p d -> p t d"),
                              X[:, bass.ds(g * G4, G4), :]).then_inc(s["o_done"], 16)
            sp_.wait_ge(s["o_done"], 16 * NG)

        @block.gpsimd
        def _(pool):
            pool.memset(ones[:], 1.0).then_inc(s["su_dve"], 1)
            pool.memset(eps_c[:], EPS).then_inc(s["su_dve"], 1)
            pool.memset(half[:], -0.5).then_inc(s["su_dve"], 1)
            for e in range(NE):
                pool.memset(rank[:, :, e:e + 1], float(NE - e)).then_inc(s["su_dve"], 1)
            pool.memset(cwt[:], 1.0).then_inc(s["su_dve"], 1)
            pool.memset(fp(xTh[:, 0:PAD]), 0.0).then_inc(s["su_dve"], 1)
            pool.memset(fp(xTl[:, 0:PAD]), 0.0).then_inc(s["su_dve"], 1)
            pool.wait_ge(s["ld_w"], 16 * N_W)
            n = 0
            for full, hi, lo in ((w1s, w1h, w1l), (w2s, w2h, w2l), (gws, gwh, gwl), (cbrow, cbh, cbl)):
                pool.tensor_copy(hi[:], full[:]).then_inc(s["su_w"], 1)
                n += 1
                pool.wait_ge(s["su_w"], n)
                pool.tensor_tensor(lo[:], full[:], fp(hi[:]), ALU.subtract).then_inc(s["su_w"], 1)
                n += 1
            pool.wait_ge(s["su_n2"], 1)
            pool.tensor_tensor(rn[:, 3, :], rn[:, 2, :], half[:, 0:3], ALU.pow).then_inc(s["su_mf"], 1)
            with pool.Fori(0, B) as b:
                pool.wait_ge(s["a_ve"], b + 1)
                pool.tensor_tensor(rstd[:], ve[:], half[:], ALU.pow).then_inc(s["a_rs"], 1)
                pool.wait_ge(s["a_oc"], (b + 1) * T)
                pool.wait_ge(s["a_x"], b)
                pool.tensor_tensor(sq, Osb, Osb, ALU.mult).then_inc(s["a_sq"], 1)
                pool.wait_ge(s["a_nc"], (b + 1) * 4)
                pool.tensor_tensor(nrm[:, 4, :], nrm[:, 3, :], half[:], ALU.pow).then_inc(s["a_pw"], 1)
                pool.wait_ge(s["a_fc"], b + 1)
                pool.tensor_tensor(sq, Osb, nrm[:, 5, :].unsqueeze(2).broadcast_to([P, T, D]),
                                   ALU.mult).then_inc(s["a_ob"], 1)

            def experts(k):
                def power(g):
                    pool.wait_ge(s["f_ve%d" % k], g + 1)
                    pool.tensor_tensor(frs[:], fve[:], half[:, 0:G4], ALU.pow).then_inc(s["f_rs%d" % k], 1)

                power(0)

                def group(g, par, last):
                    for e in range(NX):
                        pool.wait_ge(s["f_gh%d" % k], g * NX + e + 1)
                        o = (par * NX + e) % 2
                        pool.tensor_tensor(gl[:, o, :], gf[:, o, :], fp(gh[:, o, :]),
                                           ALU.subtract).then_inc(s["f_gl2%d" % k], 1)
                        if e == 1 and not last:
                            power(g + 1)

                group(0, 0, False)
                group(1, 1, False)
                with pool.Fori(1, NG // 2 - 1) as i:
                    group(2 * i, 0, False)
                    group(2 * i + 1, 1, False)
                group(NG - 2, 0, False)
                group(NG - 1, 1, True)

            experts(0)

            with pool.Fori(0, B) as b:
                pool.wait_ge(s["m_ve"], b + 1)
                pool.tensor_tensor(rstd[:], ve[:], half[:], ALU.pow).then_inc(s["m_rs"], 1)

                def steps_of_a(c):
                    pool.wait_ge(s["m_L"], b * T + c)
                    up = upto.unsqueeze(1).broadcast_to([P, H, P])
                    pool.tensor_tensor(Uh, up, fp(ahr[:, c, :]).unsqueeze(2).broadcast_to([P, H, P]),
                                       ALU.mult).then_inc(s["m_U"], 1)
                    pool.tensor_tensor(Ul, up, fp(alr[:, c, :]).unsqueeze(2).broadcast_to([P, H, P]),
                                       ALU.mult).then_inc(s["m_U"], 1)

                pool.wait_ge(s["m_al"], b + 1)
                steps_of_a(0)
                for c in range(T):
                    n = b * T + c
                    x4 = xbc[:, c % 2, 0:DI].rearrange("p (h e) -> p h e", h=H)
                    pool.wait_ge(s["m_xbc"], n + 1)
                    pool.wait_ge(s["m_ie"], n)
                    pool.tensor_tensor(xdt, x4, dtv[:, c, :].unsqueeze(2).broadcast_to([P, H, HD]),
                                       ALU.mult).then_inc(s["m_xdt"], 1)
                    pool.wait_ge(s["m_y3"], n)
                    pool.tensor_tensor(xD, x4, bc[:, R_D:R_D + H].unsqueeze(2).broadcast_to([P, H, HD]),
                                       ALU.mult).then_inc(s["m_xd"], 1)
                    pool.wait_ge(s["m_xdt"], n + 1)
                    pool.wait_ge(s["m_dec"], b + 1)
                    pool.wait_ge(s["m_st"], n)
                    pool.tensor_tensor(xw[:], xdt, dec[:, 1, c, :].unsqueeze(2).broadcast_to([P, H, HD]),
                                       ALU.mult).then_inc(s["m_xw"], 1)
                    pool.wait_ge(s["m_h0" if c == 0 else "m_h"], b + 1 if c == 0 else n)
                    pool.wait_ge(s["m_h"], n)
                    pool.tensor_tensor(hc[:], hst[:, c % 2], dec[:, 2, c, :].unsqueeze(2).broadcast_to([P, H, HD]),
                                       ALU.mult).then_inc(s["m_hc"], 1)
                    if c + 1 < T:
                        steps_of_a(c + 1)
                    pool.wait_ge(s["m_ms"], n + 1)
                    pool.tensor_tensor(yrs[:, c:c + 1], yms[:, c:c + 1], half[:, 0:1], ALU.pow).then_inc(s["m_rr"], 1)

            experts(1)

        @block.scalar
        def _(act):
            act.dma_start(wi, W_in[0:6 * P].rearrange("(k p) d -> p k d", p=P)).then_inc(s["ld_w"], 16)
            act.dma_start(wid[:], W_in[6 * P:6 * P + H]).then_inc(s["ld_w"], 16)
            act.dma_start(cw[:], conv_w.rearrange("(k p) w -> p k w", p=P)).then_inc(s["ld_w"], 16)
            act.dma_start(cbrow[:], conv_b.rearrange("(a n) -> a n", a=1)).then_inc(s["ld_w"], 16)
            act.dma_start(wos[:], W_out).then_inc(s["ld_w"], 16)
            act.dma_start(cols[2 * NX:], norm_w.rearrange("(k p) -> k p", p=P)).then_inc(s["ld_w"], 16)
            act.dma_start(w1s[:, 0, :], sw1[0]).then_inc(s["ld_w"], 16)
            act.dma_start(w1s[:, 1:, :], rw1.rearrange("e d f -> d e f")).then_inc(s["ld_w"], 16)
            act.dma_start(w2s[:, 0, :], sw2[0]).then_inc(s["ld_w"], 16)
            act.dma_start(w2s[:, 1:, :], rw2.rearrange("e f d -> f e d")).then_inc(s["ld_w"], 16)
            act.dma_start(cols[0:2], sb1.rearrange("e (k f) -> (e k) f", f=F)).then_inc(s["ld_w"], 16)
            act.dma_start(cols[2:2 * NX], rb1.rearrange("e (k f) -> (e k) f", f=F)).then_inc(s["ld_w"], 16)
            act.dma_start(b2[0:NE, :], rb2).then_inc(s["ld_w"], 16)
            act.dma_start(b2[NE:NX, :], sb2).then_inc(s["ld_w"], 16)
            act.dma_start(gws[:], gate_w).then_inc(s["ld_w"], 16)
            act.wait_ge(s["su_bcs"], 1)
            act.activation(negA[:], bc[:, R_AL:R_AL + H], ACT.Exp).then_inc(s["su_fin"], 1)

            with act.Fori(0, B) as b:
                for h in range(2):
                    act.wait_ge(s["a_tr"], b * 2 + h + 1)
                    act.activation(kh[:, h * 512:(h + 1) * 512], PS[:, h, :], ACT.Copy).then_inc(s["a_kh"], 1)
                for h in range(2):
                    act.wait_ge(s["a_qp"], b * 2 + h + 1)
                    act.activation(qh[:, h * 512:(h + 1) * 512], PS[:, 2 + h, :], ACT.Copy).then_inc(s["a_qh"], 1)
                for h in range(2):
                    act.wait_ge(s["a_vp"], b * 2 + h + 1)
                    act.activation(vh[:, 4 * h:4 * h + 4, :], PS[:, 4 + h, :], ACT.Copy).then_inc(s["a_vh"], 1)

                def exps(t):
                    act.wait_ge(s["a_nb"], b * T + t + 1)
                    act.wait_ge(s["a_pt"], b * T + t - 1) if t >= 2 else act.wait_ge(s["a_pt"], b * T)
                    act.activation(Pr[:, t % 2, :], PS[:, 2 * (t % 2):2 * (t % 2) + 2, :], ACT.Exp,
                                   bias=nbias[:, t:t + 1], accum_out=lsum[:, t:t + 1]).then_inc(s["a_ex"], 1)

                def o_copy(t):
                    act.wait_ge(s["a_pv"], b * T + t + 1)
                    act.activation(Osb[:, t, :], PS[:, 6 + t % 2, 0:D], ACT.Copy).then_inc(s["a_oc"], 1)

                act.wait_ge(s["a_nc"], b * 4)
                exps(0)
                for t in range(T):
                    if t + 1 < T:
                        exps(t + 1)
                    act.wait_ge(s["a_pt"], b * T + t + 1)
                    act.activation(PTh[:, t % 2, :], PS[:, 4:6, :], ACT.Copy).then_inc(s["a_pth"], 1)
                    if t == 1:
                        act.wait_ge(s["a_ob"], b)
                    if t >= 1:
                        o_copy(t - 1)
                o_copy(T - 1)

            def experts(k):
                def rows_t(g, par):
                    act.wait_ge(s["f_tr%d" % k], g + 1)
                    act.activation(fxh[:, par, :], PS[:, 6, :], ACT.Copy).then_inc(s["f_xh%d" % k], 1)

                def gate(g):
                    act.wait_ge(s["f_lg%d" % k], g * 8 + 2)
                    act.activation(lg[:, 2], lg[:, 1], ACT.Tanh, scale=0.5).then_inc(s["f_th%d" % k], 1)

                def gate_t(g):
                    act.wait_ge(s["f_ct%d" % k], g + 1)
                    reached(act, s["f_o%d" % k], (g - 1) * NX + 1)
                    act.activation(cwT[:], PS[0:NX, 7, :].rearrange("e (t p) -> e t p", t=G4),
                                   ACT.Copy).then_inc(s["f_ctc%d" % k], 1)

                def silu(g, e, o):
                    act.wait_ge(s["f_h%d" % k], g * NX + e + 1)
                    act.activation(sil[:, o, :], PS[:, 2 * o, :], ACT.Silu,
                                   bias=b1[:, e, 0:1]).then_inc(s["f_s%d" % k], 1)

                rows_t(0, 0)
                gate(0)
                gate_t(0)
                silu(0, 0, 0)

                def group(g, par, last):
                    for e in range(NX):
                        o = (par * NX + e) % 2
                        if e + 1 < NX:
                            silu(g, e + 1, 1 - o)
                        elif not last:
                            silu(g + 1, 0, 1 - o)
                        act.wait_ge(s["f_g%d" % k], g * NX + e + 1)
                        reached(act, s["f_o%d" % k], g * NX + e - 1)
                        act.activation(gh[:, o, :], gf[:, o, :], ACT.Copy).then_inc(s["f_gh%d" % k], 1)
                        if not last:
                            if e == 3:
                                rows_t(g + 1, 1 - par)
                            if e == 6:
                                gate(g + 1)
                            if e == 7:
                                gate_t(g + 1)

                group(0, 0, False)
                group(1, 1, False)
                with act.Fori(1, NG // 2 - 1) as i:
                    group(2 * i, 0, False)
                    group(2 * i + 1, 1, False)
                group(NG - 2, 0, False)
                group(NG - 1, 1, True)

            experts(0)

            with act.Fori(0, B) as b:
                for h in range(2):
                    act.wait_ge(s["m_tr"], b * 2 + h + 1)
                    act.activation(kh[:, h * 512:(h + 1) * 512], PS[:, h, :], ACT.Copy).then_inc(s["m_kh"], 1)
                act.wait_ge(s["m_sp"], b * SPN + 2)
                act.activation(sp[:, 2], sp[:, 1], ACT.Exp).then_inc(s["m_ex1"], 1)
                act.wait_ge(s["m_cs"], b + 1)
                act.activation(dec[:], PS[:, 7, 0:3 * T * H].rearrange("p (k c h) -> p k c h", k=3, c=T),
                               ACT.Exp).then_inc(s["m_dec"], 1)

                def silus(c):
                    n = b * T + c
                    act.wait_ge(s["m_px"], n + 1)
                    act.wait_ge(s["m_y4"], n - 1) if c >= 2 else act.wait_ge(s["m_y4"], b * T)
                    act.wait_ge(s["m_st"], n - 1) if c >= 2 else act.wait_ge(s["m_st"], b * T)
                    act.activation(xbc[:, c % 2, :], PS[:, 0, :], ACT.Silu).then_inc(s["m_xbc"], 1)
                    act.wait_ge(s["m_pz"], n + 1)
                    act.activation(zs[:, c % 2, :], PS[:, 1, 0:DI], ACT.Silu).then_inc(s["m_zs"], 1)

                silus(0)
                for c in range(T):
                    n = b * T + c
                    act.wait_ge(s["m_bt"], n + 1)
                    act.activation(BCt, PS[:, 3, 0:2 * P].rearrange("p (k n) -> p k n", k=2),
                                   ACT.Copy).then_inc(s["m_btc"], 1)
                    act.wait_ge(s["m_L"], n + 1)
                    act.wait_ge(s["m_mt"], n)
                    act.activation(Lx, PS[:, 2, :].rearrange("p (h t) -> p h t", h=H),
                                   ACT.Exp).then_inc(s["m_lx"], 1)
                    if c + 1 < T:
                        silus(c + 1)
                    act.wait_ge(s["m_y4"], n + 1)
                    act.activation(yq[:], yb[:, 2, :], ACT.Square, accum_out=ysq[:, c:c + 1]).then_inc(s["m_sq"], 1)
                    act.wait_ge(s["m_yt"], n + 1)
                    act.activation(yT[:], PS[:, 7, 0:2 * P].rearrange("p (k n) -> p k n", k=2),
                                   ACT.Copy).then_inc(s["m_ytc"], 1)

            experts(1)

        @block.tensor
        def _(pe):
            pe.wait_ge(s["ld_s"], 16 * 8)
            pe.wait_ge(s["su_dve"], 1)
            pe.matmul(PS[:, 7, 0:NR], ones[0:1, :], row[:], start=True, stop=True).then_inc(s["su_bc"], 1)
            pe.wait_ge(s["ld_m"], 16)
            pe.wait_ge(s["ld_w"], 16 * N_W)
            n = 0
            for k in range(4):
                pe.wait_ge(s["su_tap"], TAPS * (k + 1))
                if k >= 2:
                    pe.wait_ge(s["su_tpc"], 2 * (k - 1))
                for w in range(TAPS):
                    m = pe.transpose(PS[:, k % 2, w * P:(w + 1) * P], tapw[:, k, w, :], ident)
                m.then_inc(s["su_tp"], 1)
            pe.transpose(PS[:, 2, 0:P], wi[:, 0, :], ident)
            pe.transpose(PS[:, 2, P:2 * P], wi[:, 1, :], ident)
            pe.transpose(PS[:, 2, 2 * P:2 * P + H], wid[:], ident[0:H, 0:H]).then_inc(s["su_tp"], 1)
            pe.transpose(PS[:, 3, 0:P], wos[:, 0:P], ident)
            pe.transpose(PS[:, 3, P:2 * P], wos[:, P:2 * P], ident)
            pe.transpose(PS[:, 3, 2 * P:2 * P + 2 * NX + 2], cols[:], ident[0:2 * NX + 2, 0:2 * NX + 2]).then_inc(s["su_tp"], 1)

            pe.wait_ge(s["su_m"], 4)
            pe.wait_ge(s["su_tpc"], N_TPC)
            pe.wait_ge(s["su_bcs"], 1)
            with pe.Fori(0, B) as b:
                for t in range(T):
                    pe.wait_ge(s["a_xn"], b * T + t + 1)
                    if t % 4 == 0:
                        pe.wait_ge(s["a_ex"], b * T)
                    m = pe.transpose(PS[:, t // 4, (t % 4) * P:(t % 4 + 1) * P], xn[:, t, :], ident)
                    if t % 4 == 3:
                        m.then_inc(s["a_tr"], 1)
                for h in range(2):
                    pe.wait_ge(s["a_kh"], b * 2 + h + 1)
                    pe.wait_ge(s["a_kl"], b * 2 + h + 1)
                    c = slice(h * 512, (h + 1) * 512)
                    mm3(pe, PS[:, 2 + h, :], Mh[:, 0, :], Ml[:, 0, :], kh[:, c], kl[:, c]).then_inc(s["a_qp"], 1)
                for t in range(T):
                    c = slice(t * P, (t + 1) * P)
                    if t == 0:
                        pe.wait_ge(s["a_ptl"], b * T)
                        pe.wait_ge(s["a_pth"], b * T)
                    m = mm3(pe, PS[:, 4 + t // 4, (t % 4) * P:(t % 4 + 1) * P], kh[:, c], kl[:, c],
                            Mh[:, 1, :], Ml[:, 1, :])
                    if t % 4 == 3:
                        m.then_inc(s["a_vp"], 1)
                pe.wait_ge(s["a_qh"], b * 2 + 2)
                pe.wait_ge(s["a_ql"], b * 2 + 2)

                def scores(t):
                    q = slice(t * P, (t + 1) * P)
                    for h in range(2):
                        c = slice(h * 512, (h + 1) * 512)
                        m = mm3(pe, PS[:, 2 * (t % 2) + h, :], qh[:, q], ql[:, q], kh[:, c], kl[:, c])
                    m.then_inc(s["a_S"], 1)

                scores(0)
                scores(1)

                def weigh(t):
                    pe.wait_ge(s["a_pth"], b * T + t + 1)
                    pe.wait_ge(s["a_ptl"], b * T + t + 1)
                    if t < 2:
                        pe.wait_ge(s["a_oc"], b * T)
                    else:
                        pe.wait_ge(s["a_oc"], b * T + t - 1)
                    if t == 0:
                        pe.wait_ge(s["a_vh"], b * 2 + 2)
                        pe.wait_ge(s["a_vl"], b * 2 + 2)
                    for k in range(T):
                        c = slice(k * P, (k + 1) * P)
                        m = mm3(pe, PS[:, 6 + t % 2, 0:D], PTh[:, t % 2, c], PTl[:, t % 2, c], vh[:, k, :],
                                vl[:, k, :], start=(k == 0), stop=(k == T - 1))
                    m.then_inc(s["a_pv"], 1)

                for t in range(T):
                    pe.wait_ge(s["a_ex"], b * T + t + 1)
                    if t == 0:
                        pe.wait_ge(s["a_vh"], b * 2 + 2)
                        pe.wait_ge(s["a_vl"], b * 2 + 2)
                    else:
                        pe.wait_ge(s["a_pth"], b * T + t)
                        pe.wait_ge(s["a_ptl"], b * T + t)
                    for k in range(T):
                        m = pe.transpose(PS[:, 4 + k // 4, (k % 4) * P:(k % 4 + 1) * P],
                                         Pr[:, t % 2, k * P:(k + 1) * P], ident)
                    m.then_inc(s["a_pt"], 1)
                    if t + 2 < T:
                        scores(t + 2)
                    if t >= 1:
                        weigh(t - 1)
                weigh(T - 1)

            def experts(k):
                def rows_t(g):
                    for t in range(G4):
                        pe.wait_ge(s["f_xn%d" % k], g * G4 + t + 1)
                        if t == 0:
                            pe.wait_ge(s["f_xh%d" % k], g)
                            pe.wait_ge(s["f_xl%d" % k], g)
                        m = pe.transpose(PS[:, 6, t * P:(t + 1) * P], fxn[:, t, :], ident)
                    m.then_inc(s["f_tr%d" % k], 1)

                def gate(g, par):
                    pe.wait_ge(s["f_xh%d" % k], g + 1)
                    pe.wait_ge(s["f_xl%d" % k], g + 1)
                    pe.wait_ge(s["f_ctc%d" % k], g)
                    for t in range(G4):
                        c = slice(t * P, (t + 1) * P)
                        m = mm3(pe, PS[:, 7, t * NE:(t + 1) * NE], fxh[:, par, c], fxl[:, par, c], gwh[:], gwl[:])
                    m.then_inc(s["f_gl%d" % k], 1)

                def gate_t(g, par):
                    pe.wait_ge(s["f_cw%d" % k], g + 1)
                    for t in range(G4):
                        m = pe.transpose(PS[0:NX, 7, t * P:(t + 1) * P], cwt[:, par, t, :], ident)
                    m.then_inc(s["f_ct%d" % k], 1)

                def hidden(g, e, par, o):
                    if e == 0:
                        pe.wait_ge(s["f_xh%d" % k], g + 1)
                        pe.wait_ge(s["f_xl%d" % k], g + 1)
                    for j in range(2):
                        w = slice(j * F, (j + 1) * F)
                        m = mm3(pe, PS[:, 2 * o + j, :], w1h[:, e, w], w1l[:, e, w], fxh[:, par, :], fxl[:, par, :])
                    m.then_inc(s["f_h%d" % k], 1)

                def output(g, e, o):
                    pe.wait_ge(s["f_gh%d" % k], g * NX + e + 1)
                    pe.wait_ge(s["f_gl2%d" % k], g * NX + e + 1)
                    reached(pe, s["f_x%d" % k], g * NX + e - 1)
                    if e == 0:
                        pe.wait_ge(s["f_ctc%d" % k], g + 1)
                    for t in range(G4):
                        c = slice(t * P, (t + 1) * P)
                        if e == 0:
                            pe.matmul(PS[:, 4 + o, c], cwT[:, t, :], b2[:], start=True, stop=False)
                        m = mm3(pe, PS[:, 4 + o, c], gh[:, o, c], gl[:, o, c], w2h[:, e, :], w2l[:, e, :],
                                start=(e != 0))
                    m.then_inc(s["f_o%d" % k], 1)

                if k == 0:
                    pe.wait_ge(s["su_w"], 8)
                    pe.wait_ge(s["a_x"], B)
                else:
                    pe.wait_ge(s["m_x"], NT)
                rows_t(0)
                gate(0, 0)
                gate_t(0, 0)
                hidden(0, 0, 0, 0)

                def group(g, par, last):
                    for e in range(NX):
                        o = (par * NX + e) % 2
                        if e + 1 < NX:
                            reached(pe, s["f_g%d" % k], g * NX + e)
                            hidden(g, e + 1, par, 1 - o)
                        elif not last:
                            pe.wait_ge(s["f_g%d" % k], g * NX + e)
                            hidden(g + 1, 0, 1 - par, 1 - o)
                        output(g, e, o)
                        if not last:
                            if e == 2:
                                rows_t(g + 1)
                            if e == 4:
                                gate(g + 1, 1 - par)
                            if e == 6:
                                gate_t(g + 1, 1 - par)

                group(0, 0, False)
                group(1, 1, False)
                with pe.Fori(1, NG // 2 - 1) as i:
                    group(2 * i, 0, False)
                    group(2 * i + 1, 1, False)
                group(NG - 2, 0, False)
                group(NG - 1, 1, True)

            experts(0)

            pe.wait_ge(s["f_x0"], NG * NX)
            with pe.Fori(0, B) as b:
                for t in range(T):
                    pe.wait_ge(s["m_xn"], b * T + t + 1)
                    if t == 0:
                        pe.wait_ge(s["m_x"], b * T)
                    m = pe.transpose(PS[:, t // 4, (t % 4) * P:(t % 4 + 1) * P], xn[:, t, :], ident)
                    if t % 4 == 3:
                        m.then_inc(s["m_tr"], 1)
                pe.wait_ge(s["m_kh"], b * 2 + 2)
                pe.wait_ge(s["m_kl"], b * 2 + 2)
                for c in range(T):
                    q = slice(PAD + c * P, PAD + (c + 1) * P)
                    m = mm3(pe, PS[:, 6, c * H:(c + 1) * H], xTh[:, q], xTl[:, q], wzh[:, DI:], wzl[:, DI:])
                m.then_inc(s["m_dp"], 1)
                pe.wait_ge(s["m_dt"], b * 2 + 2)
                a_all = av[:].rearrange("p c h -> p (c h)")
                for j, w in enumerate((upto, after, ones[:])):
                    m = pe.matmul(PS[:, 7, j * T * H:(j + 1) * T * H], w, a_all, start=True, stop=True)
                m.then_inc(s["m_cs"], 1)

                def project(c):
                    n = b * T + c
                    if c >= 1:
                        pe.wait_ge(s["m_xbc"], n)
                        pe.wait_ge(s["m_zs"], n)
                    pe.matmul(PS[:, 0, :], ones_r[:], cbh[:], start=True, stop=False)
                    pe.matmul(PS[:, 0, :], ones_r[:], cbl[:], start=False, stop=False)
                    for w in range(TAPS):
                        q = slice(c * P + w, c * P + w + P)
                        m = mm3(pe, PS[:, 0, :], xTh[:, q], xTl[:, q], wxh[:, w, :], wxl[:, w, :], start=False,
                                stop=(w == TAPS - 1))
                    m.then_inc(s["m_px"], 1)
                    q = slice(PAD + c * P, PAD + (c + 1) * P)
                    mm3(pe, PS[:, 1, 0:DI], xTh[:, q], xTl[:, q], wzh[:, 0:DI], wzl[:, 0:DI]).then_inc(s["m_pz"], 1)

                project(0)
                for c in range(T):
                    n = b * T + c
                    par = c % 2
                    pe.wait_ge(s["m_U"], 2 * n + 2)
                    pe.wait_ge(s["m_lx"], n)
                    pe.matmul(PS[:, 2, :], after_r[:], Uh, start=True, stop=False)
                    pe.matmul(PS[:, 2, :], after_r[:], Ul, start=False, stop=True).then_inc(s["m_L"], 1)
                    pe.wait_ge(s["m_xbc"], n + 1)
                    pe.wait_ge(s["m_btc"], n)
                    pe.wait_ge(s["m_h"], n)
                    pe.transpose(PS[:, 3, 0:P], xbc[:, par, DI:DI + P], ident)
                    pe.transpose(PS[:, 3, P:2 * P], xbc[:, par, DI + P:DI + 2 * P], ident).then_inc(s["m_bt"], 1)
                    if c + 1 < T:
                        project(c + 1)
                    pe.wait_ge(s["m_btc"], n + 1)
                    pe.wait_ge(s["m_gm"], n)
                    pe.wait_ge(s["m_h"], n)
                    pe.matmul(PS[:, 4, 0:P], BCt[:, 0, :], BCt[:, 1, :], start=True, stop=True).then_inc(s["m_G"], 1)
                    if c == 0:
                        pe.wait_ge(s["m_h0"], b + 1)
                    pe.wait_ge(s["m_y1"], n)
                    pe.wait_ge(s["m_sp"], b * SPN + 1)
                    pe.matmul(PS[:, 6, 0:DI], BCt[:, 1, :], hst[:, par].rearrange("p h e -> p (h e)"),
                              start=True, stop=True).then_inc(s["m_in"], 1)
                    pe.wait_ge(s["m_xw"], n + 1)
                    pe.wait_ge(s["m_hc"], n + 1)
                    pe.matmul(PS[:, 3, 0:DI], xbc[:, par, DI:DI + P], xw[:].rearrange("p h e -> p (h e)"),
                              start=True, stop=True).then_inc(s["m_st"], 1)
                    pe.wait_ge(s["m_mt"], n + 1)
                    pe.wait_ge(s["m_xdt"], n + 1)
                    pe.wait_ge(s["m_y2"], n)
                    for h in range(H):
                        m = pe.matmul(PS[:, 5, h * HD:(h + 1) * HD], MT[:, h, :], xdt[:, h, :], start=True, stop=True)
                    m.then_inc(s["m_ie"], 1)
                    pe.wait_ge(s["m_y4"], n + 1)
                    pe.wait_ge(s["m_dec"], b + 1)
                    pe.wait_ge(s["m_ytc"], n)
                    pe.wait_ge(s["m_x"], n)
                    pe.transpose(PS[:, 7, 0:P], yb[:, 2, 0:P], ident)
                    pe.transpose(PS[:, 7, P:2 * P], yb[:, 2, P:2 * P], ident).then_inc(s["m_yt"], 1)
                    pe.wait_ge(s["m_ytc"], n + 1)
                    pe.matmul(PS[:, 7, 0:D], yT[:, 0, :], woT[:, 0, :], start=True, stop=False)
                    pe.matmul(PS[:, 7, 0:D], yT[:, 1, :], woT[:, 1, :], start=False, stop=True).then_inc(s["m_o"], 1)

            experts(1)

        @block.vector
        def _(dve):
            dve.wait_ge(s["su_bc"], 1)
            dve.tensor_copy(bc[:], PS[:, 7, 0:NR]).then_inc(s["su_bcs"], 1)
            chain = [0]

            def link(ins):
                chain[0] += 1
                ins.then_inc(s["su_rot"], 1)
                dve.wait_ge(s["su_rot"], chain[0])

            dve.wait_ge(s["su_bcs"], 1)
            dve.wait_ge(s["ld_s"], 16 * 8)
            dve.wait_ge(s["ld_m"], 16)
            link(dve.reciprocal(s2[:, 1:2], bc[:, R_SC:R_SC + 1]))
            link(dve.tensor_scalar(s2[:, 0:1], s2[:, 1:2], 2.0, None, ALU.mult))
            link(dve.tensor_scalar(s2[:, 1:2], s2[:, 0:1], bc[:, R_BI:R_BI + 1], None, ALU.add))
            link(dve.tensor_tensor(rn[:, 0, :], rr[:, :, 0], rr[:, :, 0], ALU.mult))
            link(dve.tensor_tensor(rn[:, 1, :], rr[:, :, 1], rr[:, :, 1], ALU.mult))
            dve.tensor_tensor(rn[:, 2, :], rn[:, 0, :], rn[:, 1, :], ALU.add).then_inc(s["su_n2"], 1)
            dve.wait_ge(s["su_mf"], 1)
            cs, sn = rn[:, 4, :], rn[:, 5, :]
            link(dve.tensor_tensor(cs, rr[:, :, 0], rn[:, 3, :], ALU.mult))
            link(dve.tensor_tensor(sn, rr[:, :, 1], rn[:, 3, :], ALU.mult))
            link(dve.tensor_tensor(rn[:, 6, 0:1], sn[:, 0:1], sn[:, 1:2], ALU.mult))
            link(dve.tensor_tensor(rn[:, 6, 1:2], cs[:, 0:1], sn[:, 1:2], ALU.mult))
            link(dve.scalar_tensor_tensor(rn[:, 7, 0:1], cs[:, 0:1], cs[:, 1:2], rn[:, 6, 0:1], ALU.mult, ALU.add))
            link(dve.scalar_tensor_tensor(rn[:, 7, 1:2], sn[:, 0:1], cs[:, 1:2], rn[:, 6, 1:2], ALU.mult, ALU.subtract))
            link(dve.tensor_scalar(rn[:, 7, 0:2], rn[:, 7, 0:2], s2[:, 0:1], None, ALU.mult))
            for j, (c1, s1) in enumerate(((rn[:, 7, 0:1], rn[:, 7, 1:2]), (cs[:, 2:3], sn[:, 2:3]))):
                link(dve.tensor_scalar(Mt[:, j, :], ident, c1, None, ALU.mult))
                link(dve.scalar_tensor_tensor(Mf[:, j, :], swap, s1, Mt[:, j, :], ALU.mult, ALU.add))
                dve.tensor_copy(Mh[:, j, :], Mf[:, j, :]).then_inc(s["su_m"], 1)
                dve.wait_ge(s["su_m"], 2 * j + 1)
                dve.tensor_tensor(Ml[:, j, :], Mf[:, j, :], fp(Mh[:, j, :]), ALU.subtract).then_inc(s["su_m"], 1)
            dve.tensor_copy(after_r[:], after).then_inc(s["su_rot"], 1)
            chain[0] += 1
            dve.wait_ge(s["su_dve"], 1)
            link(dve.tensor_copy(ones_r[:], ones[0:1, :]))
            dve.wait_ge(s["su_fin"], 1)
            link(dve.tensor_scalar(negA[:], negA[:], -1.0, None, ALU.mult))
            dve.wait_ge(s["ld_w"], 16 * N_W)
            for k in range(4):
                for w in range(TAPS):
                    dve.tensor_scalar(tapw[:, k, w, :], wi[:, 2 + k, :], cw[:, k, w:w + 1], None,
                                      ALU.mult).then_inc(s["su_tap"], 1)
            n = 0
            for k in range(4):
                dve.wait_ge(s["su_tp"], k + 1)
                src = PS[:, k % 2, :].rearrange("p (w c) -> p w c", w=TAPS)
                c = slice(k * P, (k + 1) * P)
                dve.tensor_copy(wxh[:, :, c], src).then_inc(s["su_tpc"], 1)
                n += 1
                dve.wait_ge(s["su_tpc"], n)
                dve.tensor_tensor(wxl[:, :, c], src, fp(wxh[:, :, c]), ALU.subtract).then_inc(s["su_tpc"], 1)
                n += 1
            dve.wait_ge(s["su_tp"], 5)
            dve.tensor_copy(wzh[:], PS[:, 2, 0:DI + H]).then_inc(s["su_tpc"], 1)
            dve.wait_ge(s["su_tpc"], n + 1)
            dve.tensor_tensor(wzl[:], PS[:, 2, 0:DI + H], fp(wzh[:]), ALU.subtract).then_inc(s["su_tpc"], 1)
            dve.wait_ge(s["su_tp"], 6)
            dve.tensor_copy(b1n[:], PS[:, 3, 2 * P:2 * P + 2 * NX + 2]).then_inc(s["su_tpc"], 1)
            dve.wait_ge(s["su_tpc"], n + 3)
            for j in range(2):
                dve.tensor_scalar(woT[:, j, :], PS[:, 3, j * P:(j + 1) * P], nw[:, j:j + 1], None,
                                  ALU.mult).then_inc(s["su_tpc"], 1)
            dve.wait_ge(s["su_dve"], N_DVE)

            def norm_rows(b, k):
                for t in range(T):
                    dve.bn_stats(stats[:, t, :], X[:, b * T + t, :]).then_inc(s[k + "_bn"], 1)
                dve.wait_ge(s[k + "_bn"], b * (T + 1) + T)
                dve.memset(turn[:], 0.0).then_inc(s[k + "_bn"], 1)
                for t in range(T):
                    dve.bn_aggr(mv[:, t, :], stats[:, t, :]).then_inc(s[k + "_ag"], 1)
                dve.wait_ge(s[k + "_ag"], b * T + T)
                dve.tensor_scalar(ve[:], mv[:, :, 1], EPS, None, ALU.add).then_inc(s[k + "_ve"], 1)
                dve.wait_ge(s[k + "_rs"], b + 1)
                for t in range(T):
                    dve.tensor_scalar(xn[:, t, :], X[:, b * T + t, :], mv[:, t, 0:1], rstd[:, t:t + 1],
                                      ALU.subtract, ALU.mult).then_inc(s[k + "_xn"], 1)

            with dve.Fori(0, B) as b:
                dve.wait_ge(s["ld_x"], 16 * (b + 1))
                norm_rows(b, "a")
                for h in range(2):
                    c = slice(h * 512, (h + 1) * 512)
                    dve.wait_ge(s["a_kh"], b * 2 + h + 1)
                    dve.tensor_tensor(kl[:, c], PS[:, h, :], fp(kh[:, c]), ALU.subtract).then_inc(s["a_kl"], 1)
                for h in range(2):
                    c = slice(h * 512, (h + 1) * 512)
                    dve.wait_ge(s["a_qh"], b * 2 + h + 1)
                    dve.tensor_tensor(ql[:, c], PS[:, 2 + h, :], fp(qh[:, c]), ALU.subtract).then_inc(s["a_ql"], 1)
                for h in range(2):
                    dve.wait_ge(s["a_vh"], b * 2 + h + 1)
                    dve.tensor_tensor(vl[:, 4 * h:4 * h + 4, :],
                                      PS[:, 4 + h, :].rearrange("p (t d) -> p t d", t=4),
                                      fp(vh[:, 4 * h:4 * h + 4, :]), ALU.subtract).then_inc(s["a_vl"], 1)

                def row_max(t):
                    dve.wait_ge(s["a_S"], b * T + t + 1)
                    dve.tensor_reduce(nmx[:, t:t + 1], PS[:, 2 * (t % 2):2 * (t % 2) + 2, :], AX.XY, ALU.max,
                                      negate=True).then_inc(s["a_nm"], 1)
                    dve.wait_ge(s["a_nm"], b * T + t + 1)
                    dve.tensor_scalar(nbias[:, t:t + 1], nmx[:, t:t + 1], s2[:, 1:2], s2[:, 1:2],
                                      ALU.subtract, ALU.add).then_inc(s["a_nb"], 1)

                row_max(0)
                row_max(1)
                for t in range(T):
                    dve.wait_ge(s["a_pth"], b * T + t + 1)
                    dve.tensor_tensor(PTl[:, t % 2, :], PS[:, 4:6, :].rearrange("p a n -> p (a n)"),
                                      fp(PTh[:, t % 2, :]), ALU.subtract).then_inc(s["a_ptl"], 1)
                    if t + 2 < T:
                        row_max(t + 2)
                dve.wait_ge(s["a_sq"], b + 1)
                dve.tensor_reduce(nrm[:, 0, :], sq, AX.X, ALU.add).then_inc(s["a_nc"], 1)
                dve.reciprocal(nrm[:, 1, :], lsum[:]).then_inc(s["a_nc"], 1)
                dve.wait_ge(s["a_nc"], b * 4 + 2)
                dve.tensor_tensor(nrm[:, 2, :], nrm[:, 0, :], nrm[:, 1, :], ALU.mult).then_inc(s["a_nc"], 1)
                dve.wait_ge(s["a_nc"], b * 4 + 3)
                dve.tensor_tensor(nrm[:, 2, :], nrm[:, 2, :], nrm[:, 1, :], ALU.mult).then_inc(s["a_nm2"], 1)
                dve.wait_ge(s["a_nm2"], b + 1)
                dve.tensor_scalar(nrm[:, 3, :], nrm[:, 2, :], SMALL, None, ALU.max).then_inc(s["a_nc"], 1)
                dve.wait_ge(s["a_pw"], b + 1)
                dve.tensor_tensor(nrm[:, 5, :], nrm[:, 4, :], nrm[:, 1, :], ALU.mult).then_inc(s["a_fc"], 1)
                dve.wait_ge(s["a_ob"], b + 1)
                xs = X[:, bass.ds(b * T, T), :]
                dve.tensor_tensor(xs, xs, sq, ALU.add).then_inc(s["a_x"], 1)

            def experts(k):
                def rows(g):
                    if isinstance(g, int) and g == 0:
                        dve.wait_ge(s["a_x"], B) if k == 0 else dve.wait_ge(s["m_x"], NT)
                    for t in range(G4):
                        dve.bn_stats(fst[:, t, :], X[:, g * G4 + t, :]).then_inc(s["f_bn%d" % k], 1)
                    dve.wait_ge(s["f_bn%d" % k], g * (G4 + 1) + G4)
                    dve.memset(turn[:], 0.0).then_inc(s["f_bn%d" % k], 1)
                    for t in range(G4):
                        dve.bn_aggr(fmv[:, t, :], fst[:, t, :]).then_inc(s["f_ag%d" % k], 1)
                    dve.wait_ge(s["f_ag%d" % k], (g + 1) * G4)
                    dve.tensor_scalar(fve[:], fmv[:, :, 1], EPS, None, ALU.add).then_inc(s["f_ve%d" % k], 1)
                    dve.wait_ge(s["f_rs%d" % k], g + 1)
                    dve.wait_ge(s["f_tr%d" % k], g)
                    for t in range(G4):
                        dve.tensor_scalar(fxn[:, t, :], X[:, g * G4 + t, :], fmv[:, t, 0:1], frs[:, t:t + 1],
                                          ALU.subtract, ALU.mult).then_inc(s["f_xn%d" % k], 1)

                def rows_lo(g, par):
                    dve.wait_ge(s["f_xh%d" % k], g + 1)
                    dve.tensor_tensor(fxl[:, par, :], PS[:, 6, :], fp(fxh[:, par, :]),
                                      ALU.subtract).then_inc(s["f_xl%d" % k], 1)

                def logits(g):
                    dve.wait_ge(s["f_gl%d" % k], g + 1)
                    gb = bc[:, R_GB:R_GB + NE].unsqueeze(1).broadcast_to([P, G4, NE])
                    n = [g * 8]

                    def step(ins):
                        n[0] = n[0] + 1
                        ins.then_inc(s["f_lg%d" % k], 1)
                        dve.wait_ge(s["f_lg%d" % k], n[0])

                    def each(v):
                        return v.unsqueeze(2).broadcast_to([P, G4, NE])

                    dve.tensor_tensor(lg[:, 0], PS[:, 7, 0:G4 * NE].rearrange("p (t e) -> p t e", t=G4), gb,
                                      ALU.add).then_inc(s["f_la%d" % k], 1)
                    dve.wait_ge(s["f_la%d" % k], g + 1)
                    step(dve.tensor_reduce(g1[:, 0, :], lg[:, 0], AX.X, ALU.max))
                    step(dve.tensor_tensor(lg[:, 1], lg[:, 0], each(g1[:, 0, :]), ALU.subtract))
                    step(dve.scalar_tensor_tensor(lg[:, 3], lg[:, 1], 0.0, rank[:], ALU.is_ge, ALU.mult))
                    step(dve.tensor_reduce(g1[:, 1, :], lg[:, 3], AX.X, ALU.max))
                    step(dve.tensor_tensor(lg[:, 4], lg[:, 3], each(g1[:, 1, :]), ALU.is_equal))
                    step(dve.scalar_tensor_tensor(lg[:, 5], lg[:, 4], -BIG, lg[:, 1], ALU.mult, ALU.add))
                    step(dve.tensor_reduce(g1[:, 2, :], lg[:, 5], AX.X, ALU.max))
                    step(dve.tensor_tensor(lg[:, 6], lg[:, 5], each(g1[:, 2, :]), ALU.is_ge))

                def choose(g, par):
                    n = [g * 8]

                    def step(ins):
                        n[0] = n[0] + 1
                        ins.then_inc(s["f_ch%d" % k], 1)
                        dve.wait_ge(s["f_ch%d" % k], n[0])

                    def each(v):
                        return v.unsqueeze(2).broadcast_to([P, G4, NE])

                    step(dve.tensor_tensor(lg[:, 7], lg[:, 6], rank[:], ALU.mult))
                    step(dve.tensor_reduce(g1[:, 3, :], lg[:, 7], AX.X, ALU.max))
                    step(dve.tensor_tensor(lg[:, 8], lg[:, 7], each(g1[:, 3, :]), ALU.is_equal))
                    step(dve.tensor_tensor(lg[:, 9], lg[:, 8], lg[:, 4], ALU.add))
                    dve.wait_ge(s["f_th%d" % k], g + 1)
                    step(dve.tensor_scalar(lg[:, 10], lg[:, 2], -1.0, 1.0, ALU.mult, ALU.add))
                    step(dve.reciprocal(lg[:, 11], lg[:, 10]))
                    step(dve.scalar_tensor_tensor(lg[:, 10], lg[:, 2], 1.0, lg[:, 11], ALU.add, ALU.mult))
                    step(dve.tensor_reduce(g1[:, 4, :], lg[:, 10], AX.X, ALU.add))
                    dve.reciprocal(g1[:, 5, :], g1[:, 4, :]).then_inc(s["f_ca%d" % k], 1)
                    dve.tensor_tensor(lg[:, 11], lg[:, 10], lg[:, 9], ALU.mult).then_inc(s["f_ca%d" % k], 1)
                    dve.wait_ge(s["f_ca%d" % k], g * 2 + 2)
                    dve.tensor_tensor(cwt[:, par, :, 0:NE], lg[:, 11], each(g1[:, 5, :]),
                                      ALU.mult).then_inc(s["f_cw%d" % k], 1)

                def multiply(g, e, o):
                    dve.wait_ge(s["f_s%d" % k], g * NX + e + 1)
                    reached(dve, s["f_gl2%d" % k], g * NX + e - 1)
                    reached(dve, s["f_gh%d" % k], g * NX + e - 1)
                    dve.scalar_tensor_tensor(gf[:, o, :], PS[:, 2 * o + 1, :], b1[:, e, 1:2], sil[:, o, :],
                                             ALU.add, ALU.mult).then_inc(s["f_g%d" % k], 1)

                def add(g, e, par, o):
                    dve.wait_ge(s["f_o%d" % k], g * NX + e + 1)
                    reached(dve, s["f_x%d" % k], g * NX + e)
                    if e == 0:
                        xg = X[:, bass.ds(g * G4, G4), :]
                        m = dve.tensor_tensor(xg, PS[:, 4 + o, :].rearrange("p (t d) -> p t d", t=G4), xg, ALU.add)
                    else:
                        for t in range(G4):
                            xt = X[:, g * G4 + t, :]
                            m = dve.scalar_tensor_tensor(xt, PS[:, 4 + o, t * P:(t + 1) * P],
                                                         cwt[:, par, t, e - 1:e], xt, ALU.mult, ALU.add)
                    m.then_inc(s["f_x%d" % k], 1)

                rows(0)
                rows_lo(0, 0)
                logits(0)
                choose(0, 0)

                def group(g, par, last):
                    for e in range(NX):
                        o = (par * NX + e) % 2
                        multiply(g, e, o)
                        if e >= 1:
                            add(g, e - 1, par, 1 - o)
                        if not last:
                            if e == 1:
                                rows(g + 1)
                            if e == 4:
                                rows_lo(g + 1, 1 - par)
                            if e == 6:
                                logits(g + 1)
                                choose(g + 1, 1 - par)
                    add(g, NX - 1, par, o)

                group(0, 0, False)
                group(1, 1, False)
                with dve.Fori(1, NG // 2 - 1) as i:
                    group(2 * i, 0, False)
                    group(2 * i + 1, 1, False)
                group(NG - 2, 0, False)
                group(NG - 1, 1, True)

            experts(0)

            with dve.Fori(0, B) as b:
                dve.wait_ge(s["m_x"], b * T)
                dve.memset(hst[:, 0], 0.0).then_inc(s["m_h0"], 1)
                norm_rows(b, "m")
                for h in range(2):
                    c = slice(h * 512, (h + 1) * 512)
                    dve.wait_ge(s["m_kh"], b * 2 + h + 1)
                    dve.tensor_tensor(kl[:, c], PS[:, h, :], fp(kh[:, c]), ALU.subtract).then_inc(s["m_kl"], 1)
                n = [b * SPN]

                def step(ins):
                    n[0] = n[0] + 1
                    ins.then_inc(s["m_sp"], 1)
                    dve.wait_ge(s["m_sp"], n[0])

                dve.wait_ge(s["m_dp"], b + 1)
                step(dve.tensor_tensor(sp[:, 0], PS[:, 6, 0:T * H].rearrange("p (c h) -> p c h", c=T),
                                       bc[:, R_DB:R_DB + H].unsqueeze(1).broadcast_to([P, T, H]), ALU.add))
                step(dve.scalar_tensor_tensor(sp[:, 1], sp[:, 0], -1.0, sp[:, 0], ALU.mult, ALU.min))
                dve.wait_ge(s["m_ex1"], b + 1)
                step(dve.tensor_scalar(sp[:, 3], sp[:, 2], 2.0, None, ALU.add))
                step(dve.reciprocal(sp[:, 4], sp[:, 3]))
                step(dve.tensor_tensor(sp[:, 5], sp[:, 2], sp[:, 4], ALU.mult))
                step(dve.tensor_tensor(sp[:, 6], sp[:, 5], sp[:, 5], ALU.mult))
                step(dve.tensor_scalar(sp[:, 7], sp[:, 6], 2.0 / 17, 2.0 / 15, ALU.mult, ALU.add))
                for odd in (13, 11, 9, 7, 5, 3, 1):
                    step(dve.tensor_tensor(sp[:, 7], sp[:, 7], sp[:, 6], ALU.mult))
                    step(dve.tensor_scalar(sp[:, 7], sp[:, 7], 2.0 / odd, None, ALU.add))
                step(dve.tensor_tensor(sp[:, 7], sp[:, 7], sp[:, 5], ALU.mult))
                assert SPN == 22
                dve.scalar_tensor_tensor(dtv[:], sp[:, 0], 0.0, sp[:, 7], ALU.max, ALU.add).then_inc(s["m_dt"], 1)
                dve.wait_ge(s["m_dt"], b * 2 + 1)
                dve.tensor_tensor(av[:], dtv[:], negA[:].unsqueeze(1).broadcast_to([P, T, H]),
                                  ALU.mult).then_inc(s["m_dt"], 1)
                dve.wait_ge(s["m_dt"], b * 2 + 2)
                dve.tensor_copy(ahr[:], av[:]).then_inc(s["m_a"], 1)
                dve.wait_ge(s["m_a"], b + 1)
                dve.tensor_tensor(alr[:], av[:], fp(ahr[:]), ALU.subtract).then_inc(s["m_al"], 1)

                def heads(v):
                    return v.rearrange("p (h e) -> p h e", h=H)

                for c in range(T):
                    n_ = b * T + c
                    par = c % 2
                    dve.wait_ge(s["m_G"], n_ + 1)
                    dve.wait_ge(s["m_mt"], n_)
                    dve.tensor_tensor(Gm, PS[:, 4, 0:P], upto, ALU.mult).then_inc(s["m_gm"], 1)
                    dve.wait_ge(s["m_gm"], n_ + 1)
                    dve.wait_ge(s["m_lx"], n_ + 1)
                    dve.wait_ge(s["m_ie"], n_)
                    dve.tensor_tensor(MT, Lx, Gm.unsqueeze(1).broadcast_to([P, H, P]), ALU.mult).then_inc(s["m_mt"], 1)
                    dve.wait_ge(s["m_st"], n_ + 1)
                    dve.wait_ge(s["m_hc"], n_ + 1)
                    dve.wait_ge(s["m_in"], n_)
                    dve.tensor_tensor(hst[:, 1 - par], heads(PS[:, 3, 0:DI]), hc[:], ALU.add).then_inc(s["m_h"], 1)
                    dve.wait_ge(s["m_in"], n_ + 1)
                    dve.wait_ge(s["m_dec"], b + 1)
                    dve.tensor_tensor(heads(yb[:, 0, :]), heads(PS[:, 6, 0:DI]),
                                      dec[:, 0, c, :].unsqueeze(2).broadcast_to([P, H, HD]),
                                      ALU.mult).then_inc(s["m_y1"], 1)
                    dve.wait_ge(s["m_y1"], n_ + 1)
                    dve.wait_ge(s["m_ie"], n_ + 1)
                    dve.tensor_tensor(yb[:, 1, :], PS[:, 5, 0:DI], yb[:, 0, :], ALU.add).then_inc(s["m_y2"], 1)
                    dve.wait_ge(s["m_y2"], n_ + 1)
                    dve.wait_ge(s["m_xd"], n_ + 1)
                    dve.tensor_tensor(yb[:, 0, :], yb[:, 1, :], xD.rearrange("p h e -> p (h e)"),
                                      ALU.add).then_inc(s["m_y3"], 1)
                    dve.wait_ge(s["m_y3"], n_ + 1)
                    dve.wait_ge(s["m_zs"], n_ + 1)
                    dve.wait_ge(s["m_yt"], n_)
                    dve.wait_ge(s["m_sq"], n_)
                    dve.tensor_tensor(yb[:, 2, :], yb[:, 0, :], zs[:, par, :], ALU.mult).then_inc(s["m_y4"], 1)
                    dve.wait_ge(s["m_sq"], n_ + 1)
                    dve.tensor_scalar(yms[:, c:c + 1], ysq[:, c:c + 1], 1.0 / DI, EPS, ALU.mult,
                                      ALU.add).then_inc(s["m_ms"], 1)
                    dve.wait_ge(s["m_rr"], n_ + 1)
                    dve.wait_ge(s["m_o"], n_ + 1)
                    xt = X[:, b * T + c, :]
                    dve.scalar_tensor_tensor(xt, PS[:, 7, 0:D], yrs[:, c:c + 1], xt, ALU.mult,
                                             ALU.add).then_inc(s["m_x"], 1)

            experts(1)


_INS = ['L0_attn_a_Q', 'L0_attn_a_rot_w', 'L0_attn_a_scale', 'L0_attn_a_bias', 'L0_attn_b_W_in',
        'L0_attn_b_conv_w', 'L0_attn_b_conv_b', 'L0_attn_b_dt_bias', 'L0_attn_b_A_log', 'L0_attn_b_D',
        'L0_attn_b_norm_w', 'L0_attn_b_W_out', 'L0_ffn_gate_w', 'L0_ffn_gate_b', 'L0_ffn_sw1', 'L0_ffn_sb1',
        'L0_ffn_sw2', 'L0_ffn_sb2', 'L0_ffn_rw1', 'L0_ffn_rb1', 'L0_ffn_rw2', 'L0_ffn_rb2']


def kernel(**inputs):
    import numpy as _np
    import concourse.bacc as _bacc
    from concourse import mybir as _mybir
    from concourse.bass_utils import run_bass_kernel_spmd as _run

    nc = _bacc.Bacc("TRN2", target_bir_lowering=False, num_devices=1)
    arrays, args = {}, []

    def give(name, a):
        arrays[name] = a
        args.append(nc.dram_tensor(name, a.shape, _mybir.dt.from_np(a.dtype), kind="ExternalInput").ap())

    for name in _INS:
        a = _np.ascontiguousarray(inputs[name])
        give(f"in_{name}_dram", a.reshape(1, 1) if a.ndim == 0 else a)
    n = 128
    r, c = _np.arange(n)[:, None], _np.arange(n)[None, :]
    swap = _np.where((r % 2 == 0) & (c == r + 1), 1.0, 0.0) - _np.where((r % 2 == 1) & (c == r - 1), 1.0, 0.0)
    give("in_masks_dram", _np.ascontiguousarray(
        _np.stack([_np.eye(n), swap, r <= c, r > c], axis=1).astype(_np.float32)))
    shape = inputs['L0_attn_a_Q'].shape
    args.append(nc.dram_tensor("out_0_dram", shape, _mybir.dt.float32, kind="ExternalOutput").ap())
    hybrid_block_kernel(nc, *args)
    return _run(nc, [arrays], core_ids=[0]).results[0]["out_0_dram"]
```

```python
import concourse.bass as bass
from concourse import mybir
from contextlib import ExitStack

N_W = 15
N_TPC = 14
N_DVE = 14
SPN = 22


def hybrid_block_kernel(nc: bass.Bass, Q: bass.AP, rot_w: bass.AP, scale: bass.AP, bias: bass.AP,
                        W_in: bass.AP, conv_w: bass.AP, conv_b: bass.AP, dt_bias: bass.AP, A_log: bass.AP,
                        D_skip: bass.AP, norm_w: bass.AP, W_out: bass.AP, gate_w: bass.AP, gate_b: bass.AP,
                        sw1: bass.AP, sb1: bass.AP, sw2: bass.AP, sb2: bass.AP, rw1: bass.AP, rb1: bass.AP,
                        rw2: bass.AP, rb2: bass.AP, masks: bass.AP, out: bass.AP):
    f32, f32r = mybir.dt.float32, mybir.dt.float32r
    ALU = mybir.AluOpType
    ACT = mybir.ActivationFunctionType
    AX = mybir.AxisListType

    B, S, D = Q.shape
    P = 128
    T = S // P
    NT = B * T
    NE = rw1.shape[0]
    F = rw2.shape[1]
    NX = NE + 1
    G4 = 4
    NG = NT // G4
    H = D_skip.shape[0]
    DI = W_out.shape[1]
    HD = DI // H
    NS = P
    TAPS = conv_w.shape[1]
    CC = DI + 2 * NS
    PAD = TAPS - 1
    EPS = 1e-5
    SMALL = 1e-8
    BIG = 1e30

    ctx = ExitStack()
    with ctx:
        def sb(name, shape, dt=f32):
            return ctx.enter_context(nc.sbuf_tensor(name, shape, dt))

        def sem(name):
            return ctx.enter_context(nc.semaphore(name))

        def fp(ap):
            return ap.bitcast(f32)

        X = sb("X", [P, NT, D])
        mk = sb("mk", [P, 4, P])
        ident, swap, upto, after = (mk[:, n, :] for n in range(4))
        ones = sb("ones", [P, P])
        after_r = sb("after_r", [P, P], f32r)
        ones_r = sb("ones_r", [1, P], f32r)
        eps_c = sb("eps_c", [P, 1])
        half = sb("half", [P, T])
        w1s = sb("w1s", [P, NX, 2 * F])
        w2s = sb("w2s", [F, NX, D])
        w1h = sb("w1h", [P, NX, 2 * F], f32r)
        w1l = sb("w1l", [P, NX, 2 * F], f32r)
        w2h = sb("w2h", [F, NX, D], f32r)
        w2l = sb("w2l", [F, NX, D], f32r)
        cols = sb("cols", [2 * NX + 2, P])
        b1n = sb("b1n", [P, 2 * NX + 2])
        b1 = b1n[:, 0:2 * NX].rearrange("p (e k) -> p e k", k=2)
        nw = b1n[:, 2 * NX:]
        b2 = sb("b2", [NX, D])
        gws = sb("gws", [P, NE])
        gwh = sb("gwh", [P, NE], f32r)
        gwl = sb("gwl", [P, NE], f32r)
        rank = sb("rank", [P, G4, NE])

        R_SC, R_BI, R_GB, R_D, R_DB, R_AL = 0, 1, 2, 2 + NE, 2 + NE + H, 2 + NE + 2 * H
        NR = R_AL + H
        row = sb("row", [1, NR])
        bc = sb("bc", [P, NR])
        negA = sb("negA", [P, H])
        rr = sb("rr", [P, 3, 2])
        rn = sb("rn", [P, 8, 3])
        Mf = sb("Mf", [P, 2, P])
        Mt = sb("Mt", [P, 2, P])
        Mh = sb("Mh", [P, P], f32r)
        Ml = sb("Ml", [P, P], f32r)
        s2 = sb("s2", [P, 2])
        wid = sb("wid", [H, D])
        cw = sb("cw", [P, 4, TAPS])
        cbrow = sb("cbrow", [1, CC])
        cbh = sb("cbh", [1, CC], f32r)
        cbl = sb("cbl", [1, CC], f32r)
        wxh = sb("wxh", [P, TAPS, CC], f32r)
        wxl = sb("wxl", [P, TAPS, CC], f32r)
        wzh = sb("wzh", [P, DI], f32r)
        wzl = sb("wzl", [P, DI], f32r)
        wdt = sb("wdt", [P, H])
        wos = sb("wos", [P, DI])
        woT = sb("woT", [P, 2, D])

        stats = sb("stats", [P, T, 6])
        mv = sb("mv", [P, T, 2])
        ve = sb("ve", [P, T])
        turn = sb("turn", [P, 1])
        rstd = sb("rstd", [P, T])
        xn = sb("xn", [P, T, D])
        xTh = sb("xTh", [P, PAD + S], f32r)
        xTl = sb("xTl", [P, PAD + S], f32r)
        kh, kl = xTh[:, PAD:], xTl[:, PAD:]
        xTf = sb("xTf", [P, S])

        AR = sb("AR", [P, 2 * S], f32r)
        AF = sb("AF", [P, 7 * S])
        at = [0, 0]

        def part(which, shape):
            n = 1
            for k in shape:
                n *= k
            lo = at[which]
            at[which] += n
            ap = (AF, AR)[which][:, lo:lo + n]
            if len(shape) == 2:
                ap = ap.rearrange("p (a b) -> p a b", a=shape[0])
            if len(shape) == 3:
                ap = ap.rearrange("p (a b c) -> p a b c", a=shape[0], b=shape[1])
            return ap

        wi = part(0, [6, D])
        tapw = part(0, [4, TAPS, P])
        at[:] = [0, 0]
        qh, ql = part(1, [S]), part(1, [S])
        Pr = part(0, [2, S])
        Osb = part(0, [T, D])
        PT = part(0, [2, S])
        vf = part(0, [T, D])
        osq = sb("osq", [P, D])
        lsum = sb("lsum", [P, T])
        nmx = sb("nmx", [P, T])
        nbias = sb("nbias", [P, T])
        nrm = sb("nrm", [P, 6, T])

        at[:] = [0, 0]
        Uh, Ul = part(1, [H, P]), part(1, [H, P])
        xbc = part(0, [2, CC])
        zs = part(0, [2, DI])
        Lx = part(0, [H, P])
        MT = part(0, [H, P])
        BCt = part(0, [2, P])
        Gm = part(0, [P])
        xdt = part(0, [H, HD])
        xD = part(0, [H, HD])
        xw = sb("xw", [P, H, HD])
        hc = sb("hc", [P, H, HD])
        hst = part(0, [2, H, HD])
        yb = sb("yb", [P, 3, DI])
        yq = sb("yq", [P, DI])
        yT = sb("yT", [P, 2, P])
        ysq = sb("ysq", [P, T])
        yms = sb("yms", [P, T])
        yrs = sb("yrs", [P, T])
        sp = sb("sp", [P, 8, T, H])
        dtv = sb("dtv", [P, T, H])
        av = sb("av", [P, T, H])
        ahr = sb("ahr", [P, T, H], f32r)
        alr = sb("alr", [P, T, H], f32r)
        dec = sb("dec", [P, 3, T, H])

        fst = sb("fst", [P, G4, 6])
        fmv = sb("fmv", [P, G4, 2])
        fve = sb("fve", [P, G4])
        frs = sb("frs", [P, G4])
        fxn = sb("fxn", [P, G4, D])
        fxh = sb("fxh", [P, 2, G4 * P], f32r)
        fxl = sb("fxl", [P, 2, G4 * P], f32r)
        lg = sb("lg", [P, 12, G4, NE])
        g1 = sb("g1", [P, 6, G4])
        cwt = sb("cwt", [P, 2, G4, NX])
        cwT = sb("cwT", [NX, G4, P])
        sil = sb("sil", [P, 2, G4 * P])
        gf = sb("gf", [P, 2, G4 * P])

        PS = ctx.enter_context(nc.psum_tensor("PS", [P, 8, 512], f32))

        names = """ld_x ld_w ld_m ld_s su_w su_bc su_bcs su_rot su_mf su_m su_tap su_tp su_tpc su_dve su_fin su_n2
            a_bn a_ag a_ve a_rs a_xn a_tr a_kh a_kl a_xf a_qp a_qh a_ql a_vp a_vf a_S a_nm a_nb a_ex a_pt a_ptc
            a_pv a_oc a_ss a_nc a_cl a_pw a_fc a_x
            m_z m_bn m_ag m_ve m_rs m_xn m_tr m_kh m_kl m_xf m_dp m_sp m_ex1 m_dt m_a m_al m_cs m_dec m_px m_xbc m_pz
            m_zs m_U m_L m_lx m_bt m_btc m_G m_gm m_mt m_xdt m_xd m_xw m_hc m_in m_ie m_y1 m_y2 m_y3 m_y4 m_sq m_ms
            m_rr m_yt m_ytc m_o m_st m_h m_x m_h0 o_done""".split()
        for k in (0, 1):
            names += [n + str(k) for n in """f_bn f_ag f_ve f_rs f_xn f_tr f_xh f_xl f_gl f_lg f_th f_cw f_ct f_ctc
                f_la f_ca f_ch f_h f_s f_g f_o f_x""".split()]
        s = {n: sem(n) for n in names}

        x_dram = Q.rearrange("b (t p) d -> b p t d", p=P)
        o_dram = out.rearrange("b (t p) d -> (b t) p d", p=P)

        block = ctx.enter_context(nc.Block())

        def reached(eng, sm, value):
            if not (isinstance(value, int) and value <= 0):
                eng.wait_ge(sm, value)

        def mm3(pe, dst, ah, al, bh, bl, start=True, stop=True):
            pe.matmul(dst, ah, bh, start=start, stop=False)
            pe.matmul(dst, ah, bl, start=False, stop=False)
            return pe.matmul(dst, al, bh, start=False, stop=stop)

        @block.sync
        def _(sp_):
            sp_.dma_start(mk[:], masks).then_inc(s["ld_m"], 16)
            for n, src in ((R_SC, scale), (R_GB, gate_b), (R_D, D_skip), (R_DB, dt_bias), (R_AL, A_log)):
                sp_.dma_start(row[0:1, n:n + src.shape[0]], src.rearrange("(a n) -> a n", a=1)).then_inc(s["ld_s"], 16)
            sp_.dma_start(row[0:1, R_BI:R_BI + 1], bias).then_inc(s["ld_s"], 16)
            pairs = rot_w.rearrange("w (j two) -> j w two", two=2)
            for n in range(2):
                sp_.dma_start(rr[n::2], pairs).then_inc(s["ld_s"], 16)
            for b in range(B):
                sp_.dma_start(X[:, b * T:(b + 1) * T, :], x_dram[b]).then_inc(s["ld_x"], 16)
                sp_.wait_ge(s["ld_x"], 16 * (b + 1))
            with sp_.Fori(0, NG) as g:
                sp_.wait_ge(s["f_x1"], (g + 1) * NX)
                sp_.dma_start(o_dram[bass.ds(g * G4, G4)].rearrange("t p d -> p t d"),
                              X[:, bass.ds(g * G4, G4), :]).then_inc(s["o_done"], 16)
            sp_.wait_ge(s["o_done"], 16 * NG)

        @block.gpsimd
        def _(pool):
            pool.memset(ones[:], 1.0).then_inc(s["su_dve"], 1)
            pool.memset(eps_c[:], EPS).then_inc(s["su_dve"], 1)
            pool.memset(half[:], -0.5).then_inc(s["su_dve"], 1)
            for e in range(NE):
                pool.memset(rank[:, :, e:e + 1], float(NE - e)).then_inc(s["su_dve"], 1)
            pool.memset(cwt[:], 1.0).then_inc(s["su_dve"], 1)
            pool.memset(fp(xTh[:, 0:PAD]), 0.0).then_inc(s["su_dve"], 1)
            pool.memset(fp(xTl[:, 0:PAD]), 0.0).then_inc(s["su_dve"], 1)
            pool.wait_ge(s["ld_w"], 16 * N_W)
            n = 0
            for full, hi, lo in ((w1s, w1h, w1l), (w2s, w2h, w2l), (gws, gwh, gwl), (cbrow, cbh, cbl)):
                pool.tensor_copy(hi[:], full[:]).then_inc(s["su_w"], 1)
                n += 1
                pool.wait_ge(s["su_w"], n)
                pool.tensor_tensor(lo[:], full[:], fp(hi[:]), ALU.subtract).then_inc(s["su_w"], 1)
                n += 1
            pool.wait_ge(s["su_n2"], 1)
            pool.tensor_tensor(rn[:, 3, :], rn[:, 2, :], half[:, 0:3], ALU.pow).then_inc(s["su_mf"], 1)
            def rows_power(b, k):
                pool.wait_ge(s[k + "_ve"], b + 1)
                pool.tensor_tensor(rstd[:], ve[:], half[:], ALU.pow).then_inc(s[k + "_rs"], 1)

            def norm_power(b, hf):
                h = slice(4 * hf, 4 * hf + 4)
                pool.wait_ge(s["a_cl"], b * 2 + hf + 1)
                pool.tensor_tensor(nrm[:, 4, h], nrm[:, 3, h], half[:, h], ALU.pow).then_inc(s["a_pw"], 1)

            def attend(b, last):
                if not last:
                    rows_power(b + 1, "a")
                norm_power(b, 0)
                norm_power(b, 1)

            rows_power(0, "a")
            attend(0, False)
            with pool.Fori(1, B - 1) as b:
                attend(b, False)
            attend(B - 1, True)

            def experts(k):
                def power(g):
                    pool.wait_ge(s["f_ve%d" % k], g + 1)
                    pool.tensor_tensor(frs[:], fve[:], half[:, 0:G4], ALU.pow).then_inc(s["f_rs%d" % k], 1)

                power(0)

                for g in range(1):
                    power(g + 1)
                with pool.Fori(1, NG - 1) as g:
                    power(g + 1)

            experts(0)

            def steps_of_a(b, c):
                pool.wait_ge(s["m_al"], b + 1)
                reached(pool, s["m_L"], b * T + c)
                up = upto.unsqueeze(1).broadcast_to([P, H, P])
                pool.tensor_tensor(Uh, up, fp(ahr[:, c, :]).unsqueeze(2).broadcast_to([P, H, P]),
                                   ALU.mult).then_inc(s["m_U"], 1)
                pool.tensor_tensor(Ul, up, fp(alr[:, c, :]).unsqueeze(2).broadcast_to([P, H, P]),
                                   ALU.mult).then_inc(s["m_U"], 1)

            def root(n, c):
                pool.wait_ge(s["m_ms"], n + 1)
                pool.tensor_tensor(yrs[:, c:c + 1], yms[:, c:c + 1], half[:, 0:1], ALU.pow).then_inc(s["m_rr"], 1)

            def sequence(b, first, last):
                steps_of_a(b, 0)
                for c in range(T):
                    n = b * T + c
                    x4 = xbc[:, c % 2, 0:DI].rearrange("p (h e) -> p h e", h=H)
                    pool.wait_ge(s["m_xbc"], n + 1)
                    reached(pool, s["m_ie"], n)
                    pool.tensor_tensor(xdt, x4, dtv[:, c, :].unsqueeze(2).broadcast_to([P, H, HD]),
                                       ALU.mult).then_inc(s["m_xdt"], 1)
                    reached(pool, s["m_y3"], n)
                    pool.tensor_tensor(xD, x4, bc[:, R_D:R_D + H].unsqueeze(2).broadcast_to([P, H, HD]),
                                       ALU.mult).then_inc(s["m_xd"], 1)
                    pool.wait_ge(s["m_xdt"], n + 1)
                    pool.wait_ge(s["m_dec"], b + 1)
                    reached(pool, s["m_st"], n)
                    pool.tensor_tensor(xw[:], xdt, dec[:, 1, c, :].unsqueeze(2).broadcast_to([P, H, HD]),
                                       ALU.mult).then_inc(s["m_xw"], 1)
                    if c == 0:
                        pool.wait_ge(s["m_h0"], b + 1)
                    reached(pool, s["m_h"], n)
                    pool.tensor_tensor(hc[:], hst[:, c % 2], dec[:, 2, c, :].unsqueeze(2).broadcast_to([P, H, HD]),
                                       ALU.mult).then_inc(s["m_hc"], 1)
                    if c + 1 < T:
                        steps_of_a(b, c + 1)
                    if c == 3 and not last:
                        rows_power(b + 1, "m")
                    root(n, c)

            rows_power(0, "m")
            sequence(0, True, False)
            with pool.Fori(1, B - 1) as b:
                sequence(b, False, False)
            sequence(B - 1, False, True)

            experts(1)

        @block.scalar
        def _(act):
            act.dma_start(wi, W_in[0:6 * P].rearrange("(k p) d -> p k d", p=P)).then_inc(s["ld_w"], 16)
            act.dma_start(wid[:], W_in[6 * P:6 * P + H]).then_inc(s["ld_w"], 16)
            act.dma_start(cw[:], conv_w.rearrange("(k p) w -> p k w", p=P)).then_inc(s["ld_w"], 16)
            act.dma_start(cbrow[:], conv_b.rearrange("(a n) -> a n", a=1)).then_inc(s["ld_w"], 16)
            act.dma_start(wos[:], W_out).then_inc(s["ld_w"], 16)
            act.dma_start(cols[2 * NX:], norm_w.rearrange("(k p) -> k p", p=P)).then_inc(s["ld_w"], 16)
            act.dma_start(w1s[:, 0, :], sw1[0]).then_inc(s["ld_w"], 16)
            act.dma_start(w1s[:, 1:, :], rw1.rearrange("e d f -> d e f")).then_inc(s["ld_w"], 16)
            act.dma_start(w2s[:, 0, :], sw2[0]).then_inc(s["ld_w"], 16)
            act.dma_start(w2s[:, 1:, :], rw2.rearrange("e f d -> f e d")).then_inc(s["ld_w"], 16)
            act.dma_start(cols[0:2], sb1.rearrange("e (k f) -> (e k) f", f=F)).then_inc(s["ld_w"], 16)
            act.dma_start(cols[2:2 * NX], rb1.rearrange("e (k f) -> (e k) f", f=F)).then_inc(s["ld_w"], 16)
            act.dma_start(b2[0:NE, :], rb2).then_inc(s["ld_w"], 16)
            act.dma_start(b2[NE:NX, :], sb2).then_inc(s["ld_w"], 16)
            act.dma_start(gws[:], gate_w).then_inc(s["ld_w"], 16)
            act.wait_ge(s["su_bcs"], 1)
            act.activation(negA[:], bc[:, R_AL:R_AL + H], ACT.Exp).then_inc(s["su_fin"], 1)

            def rows_hi(b, k, banks=(0, 1)):
                for h in range(2):
                    act.wait_ge(s[k + "_tr"], b * 2 + h + 1)
                    act.activation(kh[:, h * 512:(h + 1) * 512], PS[:, banks[h], :], ACT.Copy).then_inc(s[k + "_kh"], 1)

            def rows_full(b, k, banks=(0, 1)):
                for h in range(2):
                    act.activation(xTf[:, h * 512:(h + 1) * 512], PS[:, banks[h], :], ACT.Copy).then_inc(s[k + "_xf"], 1)

            def queries(b):
                for h in range(2):
                    act.wait_ge(s["a_qp"], b * 2 + h + 1)
                    act.activation(qh[:, h * 512:(h + 1) * 512], PS[:, 2 + h, :], ACT.Copy).then_inc(s["a_qh"], 1)

            def values(b):
                for h in range(2):
                    act.wait_ge(s["a_vp"], b * 2 + h + 1)
                    act.activation(vf[:, 4 * h:4 * h + 4, :], PS[:, 4 + h, :].rearrange("p (t d) -> p t d", t=4),
                                   ACT.Copy).then_inc(s["a_vf"], 1)

            def exps(b, t):
                act.wait_ge(s["a_nb"], b * T + t + 1)
                reached(act, s["a_pt"], b * T + t - 1)
                reached(act, s["a_cl"], b * 2 - 1 + (t >= 4))
                act.activation(Pr[:, t % 2, :], PS[:, 2 * (t % 2):2 * (t % 2) + 2, :], ACT.Exp,
                               bias=nbias[:, t:t + 1], accum_out=lsum[:, t:t + 1]).then_inc(s["a_ex"], 1)

            def attend(b, last):
                for t in range(T):
                    if t + 1 < T:
                        exps(b, t + 1)
                    act.wait_ge(s["a_pt"], b * T + t + 1)
                    reached(act, s["a_pv"], b * T + t - 1)
                    act.activation(PT[:, t % 2, :], PS[:, 4:6, :].rearrange("p a n -> p (a n)"),
                                   ACT.Copy).then_inc(s["a_ptc"], 1)
                    if t == T - 2 and not last:
                        rows_hi(b + 1, "a")
                        rows_full(b + 1, "a")
                if not last:
                    queries(b + 1)
                    values(b + 1)
                    exps(b + 1, 0)

            rows_hi(0, "a")
            rows_full(0, "a")
            queries(0)
            values(0)
            exps(0, 0)
            attend(0, False)
            with act.Fori(1, B - 1) as b:
                attend(b, False)
            attend(B - 1, True)

            def experts(k):
                def rows_t(g, par):
                    act.wait_ge(s["f_tr%d" % k], g + 1)
                    act.activation(fxh[:, par, :], PS[:, 6, :], ACT.Copy).then_inc(s["f_xh%d" % k], 1)

                def gate(g):
                    act.wait_ge(s["f_lg%d" % k], g * 8 + 2)
                    act.activation(lg[:, 2], lg[:, 1], ACT.Tanh, scale=0.5).then_inc(s["f_th%d" % k], 1)

                def gate_t(g):
                    act.wait_ge(s["f_ct%d" % k], g + 1)
                    reached(act, s["f_o%d" % k], (g - 1) * NX + 1)
                    act.activation(cwT[:], PS[0:NX, 7, :].rearrange("e (t p) -> e t p", t=G4),
                                   ACT.Copy).then_inc(s["f_ctc%d" % k], 1)

                def silu(g, e, o):
                    act.wait_ge(s["f_h%d" % k], g * NX + e + 1)
                    act.activation(sil[:, o, :], PS[:, 2 * o, :], ACT.Silu,
                                   bias=b1[:, e, 0:1]).then_inc(s["f_s%d" % k], 1)

                rows_t(0, 0)
                gate(0)
                gate_t(0)
                silu(0, 0, 0)

                def group(g, par, last):
                    for e in range(NX):
                        o = (par * NX + e) % 2
                        if e + 1 < NX:
                            silu(g, e + 1, 1 - o)
                        elif not last:
                            silu(g + 1, 0, 1 - o)
                        if not last:
                            if e == 3:
                                rows_t(g + 1, 1 - par)
                            if e == 6:
                                gate(g + 1)
                            if e == 7:
                                gate_t(g + 1)

                group(0, 0, False)
                group(1, 1, False)
                with act.Fori(1, NG // 2 - 1) as i:
                    group(2 * i, 0, False)
                    group(2 * i + 1, 1, False)
                group(NG - 2, 0, False)
                group(NG - 1, 1, True)

            experts(0)

            def decays(b):
                act.wait_ge(s["m_sp"], b * SPN + 2)
                act.activation(sp[:, 2], sp[:, 1], ACT.Exp).then_inc(s["m_ex1"], 1)

            def decays_2(b):
                act.wait_ge(s["m_cs"], b + 1)
                act.activation(dec[:], PS[:, 7, 0:3 * T * H].rearrange("p (k c h) -> p k c h", k=3, c=T),
                               ACT.Exp).then_inc(s["m_dec"], 1)

            def silus(b, c):
                n = b * T + c
                act.wait_ge(s["m_px"], n + 1)
                reached(act, s["m_y4"], n - 1)
                reached(act, s["m_st"], n - 1)
                act.activation(xbc[:, c % 2, :], PS[:, 0, :], ACT.Silu).then_inc(s["m_xbc"], 1)
                act.wait_ge(s["m_pz"], n + 1)
                act.activation(zs[:, c % 2, :], PS[:, 1, 0:DI], ACT.Silu).then_inc(s["m_zs"], 1)

            def turned(n):
                act.wait_ge(s["m_yt"], n + 1)
                act.activation(yT[:], PS[:, 7, 0:2 * P].rearrange("p (k n) -> p k n", k=2),
                               ACT.Copy).then_inc(s["m_ytc"], 1)

            def sequence(b, first, last):
                for c in range(T):
                    n = b * T + c
                    act.wait_ge(s["m_bt"], n + 1)
                    act.activation(BCt, PS[:, 3, 0:2 * P].rearrange("p (k n) -> p k n", k=2),
                                   ACT.Copy).then_inc(s["m_btc"], 1)
                    act.wait_ge(s["m_L"], n + 1)
                    reached(act, s["m_mt"], n)
                    act.activation(Lx, PS[:, 2, :].rearrange("p (h t) -> p h t", h=H),
                                   ACT.Exp).then_inc(s["m_lx"], 1)
                    if c == T - 1 and not last:
                        rows_hi(b + 1, "m")
                        rows_full(b + 1, "m")
                    if c > 0:
                        turned(n - 1)
                    if c + 1 < T:
                        silus(b, c + 1)
                    act.wait_ge(s["m_y4"], n + 1)
                    act.activation(yq[:], yb[:, 2, :], ACT.Square, accum_out=ysq[:, c:c + 1]).then_inc(s["m_sq"], 1)
                turned(b * T + T - 1)
                if not last:
                    decays(b + 1)
                    silus(b + 1, 0)
                    decays_2(b + 1)

            rows_hi(0, "m")
            rows_full(0, "m")
            decays(0)
            silus(0, 0)
            decays_2(0)
            sequence(0, True, False)
            with act.Fori(1, B - 1) as b:
                sequence(b, False, False)
            sequence(B - 1, False, True)

            experts(1)

        @block.tensor
        def _(pe):
            pe.wait_ge(s["ld_s"], 16 * 8)
            pe.wait_ge(s["su_dve"], 1)
            pe.matmul(PS[:, 7, 0:NR], ones[0:1, :], row[:], start=True, stop=True).then_inc(s["su_bc"], 1)
            pe.wait_ge(s["ld_m"], 16)
            pe.wait_ge(s["ld_w"], 16 * N_W)
            n = 0
            for k in range(4):
                pe.wait_ge(s["su_tap"], TAPS * (k + 1))
                if k >= 2:
                    pe.wait_ge(s["su_tpc"], 2 * (k - 1))
                for w in range(TAPS):
                    m = pe.transpose(PS[:, k % 2, w * P:(w + 1) * P], tapw[:, k, w, :], ident)
                m.then_inc(s["su_tp"], 1)
            pe.transpose(PS[:, 2, 0:P], wi[:, 0, :], ident)
            pe.transpose(PS[:, 2, P:2 * P], wi[:, 1, :], ident)
            pe.transpose(PS[:, 2, 2 * P:2 * P + H], wid[:], ident[0:H, 0:H]).then_inc(s["su_tp"], 1)
            pe.transpose(PS[:, 3, 0:P], wos[:, 0:P], ident)
            pe.transpose(PS[:, 3, P:2 * P], wos[:, P:2 * P], ident)
            pe.transpose(PS[:, 3, 2 * P:2 * P + 2 * NX + 2], cols[:], ident[0:2 * NX + 2, 0:2 * NX + 2]).then_inc(s["su_tp"], 1)

            pe.wait_ge(s["su_m"], 2)
            pe.wait_ge(s["su_tpc"], N_TPC)
            pe.wait_ge(s["su_bcs"], 1)
            def rows_t(b):
                for t in range(T):
                    pe.wait_ge(s["a_xn"], b * T + t + 1)
                    if t == 0:
                        reached(pe, s["a_ex"], b * T - 1)
                    m = pe.transpose(PS[:, t // 4, (t % 4) * P:(t % 4 + 1) * P], xn[:, t, :], ident)
                    if t % 4 == 3:
                        m.then_inc(s["a_tr"], 1)

            def queries(b):
                reached(pe, s["a_ex"], b * T)
                for h in range(2):
                    pe.wait_ge(s["a_kh"], b * 2 + h + 1)
                    pe.wait_ge(s["a_kl"], b * 2 + h + 1)
                    c = slice(h * 512, (h + 1) * 512)
                    mm3(pe, PS[:, 2 + h, :], Mh[:], Ml[:], kh[:, c], kl[:, c]).then_inc(s["a_qp"], 1)

            def values(b):
                pe.wait_ge(s["a_xf"], b * 2 + 2)
                reached(pe, s["a_ptc"], b * T)
                for t in range(T):
                    m = pe.matmul(PS[:, 4 + t // 4, (t % 4) * P:(t % 4 + 1) * P], xTf[:, t * P:(t + 1) * P],
                                  Mf[:, 1, :], start=True, stop=True)
                    if t % 4 == 3:
                        m.then_inc(s["a_vp"], 1)

            def scores(b, t):
                q = slice(t * P, (t + 1) * P)
                for h in range(2):
                    c = slice(h * 512, (h + 1) * 512)
                    m = mm3(pe, PS[:, 2 * (t % 2) + h, :], qh[:, q], ql[:, q], kh[:, c], kl[:, c])
                m.then_inc(s["a_S"], 1)

            def first_scores(b):
                pe.wait_ge(s["a_qh"], b * 2 + 2)
                pe.wait_ge(s["a_ql"], b * 2 + 2)
                scores(b, 0)
                scores(b, 1)

            def weigh(b, t):
                pe.wait_ge(s["a_ptc"], b * T + t + 1)
                reached(pe, s["a_oc"], b * T + t - 1)
                for k in range(T):
                    m = pe.matmul(PS[:, 6 + t % 2, 0:D], PT[:, t % 2, k * P:(k + 1) * P], vf[:, k, :],
                                  start=(k == 0), stop=(k == T - 1))
                m.then_inc(s["a_pv"], 1)

            def attend(b, last):
                for t in range(T):
                    pe.wait_ge(s["a_ex"], b * T + t + 1)
                    if t == 0:
                        pe.wait_ge(s["a_vf"], b * 2 + 2)
                    else:
                        pe.wait_ge(s["a_ptc"], b * T + t)
                    for k in range(T):
                        m = pe.transpose(PS[:, 4 + k // 4, (k % 4) * P:(k % 4 + 1) * P],
                                         Pr[:, t % 2, k * P:(k + 1) * P], ident)
                    m.then_inc(s["a_pt"], 1)
                    if t + 2 < T:
                        scores(b, t + 2)
                    elif t == T - 2 and not last:
                        rows_t(b + 1)
                    if t >= 1:
                        weigh(b, t - 1)
                if not last:
                    queries(b + 1)
                weigh(b, T - 1)
                if not last:
                    values(b + 1)
                    first_scores(b + 1)

            rows_t(0)
            queries(0)
            values(0)
            first_scores(0)
            attend(0, False)
            with pe.Fori(1, B - 1) as b:
                attend(b, False)
            attend(B - 1, True)

            def experts(k):
                def rows_t(g):
                    for t in range(G4):
                        pe.wait_ge(s["f_xn%d" % k], g * G4 + t + 1)
                        if t == 0:
                            pe.wait_ge(s["f_xh%d" % k], g)
                            pe.wait_ge(s["f_xl%d" % k], g)
                        m = pe.transpose(PS[:, 6, t * P:(t + 1) * P], fxn[:, t, :], ident)
                    m.then_inc(s["f_tr%d" % k], 1)

                def gate(g, par):
                    pe.wait_ge(s["f_xh%d" % k], g + 1)
                    pe.wait_ge(s["f_xl%d" % k], g + 1)
                    pe.wait_ge(s["f_ctc%d" % k], g)
                    for t in range(G4):
                        c = slice(t * P, (t + 1) * P)
                        m = mm3(pe, PS[:, 7, t * NE:(t + 1) * NE], fxh[:, par, c], fxl[:, par, c], gwh[:], gwl[:])
                    m.then_inc(s["f_gl%d" % k], 1)

                def gate_t(g, par):
                    pe.wait_ge(s["f_cw%d" % k], g + 1)
                    for t in range(G4):
                        m = pe.transpose(PS[0:NX, 7, t * P:(t + 1) * P], cwt[:, par, t, :], ident)
                    m.then_inc(s["f_ct%d" % k], 1)

                def hidden(g, e, par, o):
                    if e == 0:
                        pe.wait_ge(s["f_xh%d" % k], g + 1)
                        pe.wait_ge(s["f_xl%d" % k], g + 1)
                    for j in range(2):
                        w = slice(j * F, (j + 1) * F)
                        m = mm3(pe, PS[:, 2 * o + j, :], w1h[:, e, w], w1l[:, e, w], fxh[:, par, :], fxl[:, par, :])
                    m.then_inc(s["f_h%d" % k], 1)

                def output(g, e, o):
                    pe.wait_ge(s["f_g%d" % k], g * NX + e + 1)
                    reached(pe, s["f_x%d" % k], g * NX + e - 1)
                    if e == 0:
                        pe.wait_ge(s["f_ctc%d" % k], g + 1)
                    for t in range(G4):
                        c = slice(t * P, (t + 1) * P)
                        if e == 0:
                            pe.matmul(PS[:, 4 + o, c], cwT[:, t, :], b2[:], start=True, stop=False)
                        m = pe.matmul(PS[:, 4 + o, c], gf[:, o, c], w2s[:, e, :], start=(e != 0), stop=True)
                    m.then_inc(s["f_o%d" % k], 1)

                if k == 0:
                    pe.wait_ge(s["su_w"], 8)
                    pe.wait_ge(s["a_x"], 2 * B)
                else:
                    pe.wait_ge(s["m_x"], NT)
                rows_t(0)
                gate(0, 0)
                gate_t(0, 0)
                hidden(0, 0, 0, 0)

                def group(g, par, last):
                    for e in range(NX):
                        o = (par * NX + e) % 2
                        if e + 1 < NX:
                            reached(pe, s["f_g%d" % k], g * NX + e)
                            hidden(g, e + 1, par, 1 - o)
                        elif not last:
                            pe.wait_ge(s["f_g%d" % k], g * NX + e)
                            hidden(g + 1, 0, 1 - par, 1 - o)
                        output(g, e, o)
                        if not last:
                            if e == 2:
                                rows_t(g + 1)
                            if e == 4:
                                gate(g + 1, 1 - par)
                            if e == 6:
                                gate_t(g + 1, 1 - par)

                group(0, 0, False)
                group(1, 1, False)
                with pe.Fori(1, NG // 2 - 1) as i:
                    group(2 * i, 0, False)
                    group(2 * i + 1, 1, False)
                group(NG - 2, 0, False)
                group(NG - 1, 1, True)

            experts(0)

            pe.wait_ge(s["f_x0"], NG * NX)
            def rows_t2(b):
                for t in range(T):
                    pe.wait_ge(s["m_xn"], b * T + t + 1)
                    if t == 0:
                        reached(pe, s["m_xbc"], b * T)
                        reached(pe, s["m_zs"], b * T)
                    m = pe.transpose(PS[:, t // 4, (t % 4) * P:(t % 4 + 1) * P], xn[:, t, :], ident)
                    if t % 4 == 3:
                        m.then_inc(s["m_tr"], 1)

            def steps(b):
                pe.wait_ge(s["m_xf"], b * 2 + 2)
                reached(pe, s["m_y1"], b * T)
                for c in range(T):
                    m = pe.matmul(PS[:, 6, c * H:(c + 1) * H], xTf[:, c * P:(c + 1) * P], wdt[:],
                                  start=True, stop=True)
                m.then_inc(s["m_dp"], 1)

            def sums(b):
                pe.wait_ge(s["m_dt"], b * 2 + 2)
                reached(pe, s["m_x"], b * T)
                a_all = av[:].rearrange("p c h -> p (c h)")
                for j, w in enumerate((upto, after, ones[:])):
                    m = pe.matmul(PS[:, 7, j * T * H:(j + 1) * T * H], w, a_all, start=True, stop=True)
                m.then_inc(s["m_cs"], 1)

            def project(b, c):
                n = b * T + c
                reached(pe, s["m_xbc"], n)
                reached(pe, s["m_zs"], n)
                if c == 0:
                    pe.wait_ge(s["m_kl"], b * 2 + 2)
                    pe.wait_ge(s["m_kh"], b * 2 + 2)
                pe.matmul(PS[:, 0, :], ones_r[:], cbh[:], start=True, stop=False)
                pe.matmul(PS[:, 0, :], ones_r[:], cbl[:], start=False, stop=False)
                for w in range(TAPS):
                    q = slice(c * P + w, c * P + w + P)
                    m = mm3(pe, PS[:, 0, :], xTh[:, q], xTl[:, q], wxh[:, w, :], wxl[:, w, :], start=False,
                            stop=(w == TAPS - 1))
                m.then_inc(s["m_px"], 1)
                q = slice(PAD + c * P, PAD + (c + 1) * P)
                mm3(pe, PS[:, 1, 0:DI], xTh[:, q], xTl[:, q], wzh[:], wzl[:]).then_inc(s["m_pz"], 1)

            def turn(n):
                pe.wait_ge(s["m_y4"], n + 1)
                pe.transpose(PS[:, 7, 0:P], yb[:, 2, 0:P], ident)
                pe.transpose(PS[:, 7, P:2 * P], yb[:, 2, P:2 * P], ident).then_inc(s["m_yt"], 1)

            def leave(n):
                pe.wait_ge(s["m_ytc"], n + 1)
                pe.matmul(PS[:, 7, 0:D], yT[:, 0, :], woT[:, 0, :], start=True, stop=False)
                pe.matmul(PS[:, 7, 0:D], yT[:, 1, :], woT[:, 1, :], start=False, stop=True).then_inc(s["m_o"], 1)

            def sequence(b, first, last):
                for c in range(T):
                    n = b * T + c
                    par = c % 2
                    pe.wait_ge(s["m_U"], n * 2 + 2)
                    reached(pe, s["m_lx"], n)
                    pe.matmul(PS[:, 2, :], after_r[:], Uh, start=True, stop=False)
                    pe.matmul(PS[:, 2, :], after_r[:], Ul, start=False, stop=True).then_inc(s["m_L"], 1)
                    pe.wait_ge(s["m_xbc"], n + 1)
                    reached(pe, s["m_h"], n)
                    pe.transpose(PS[:, 3, 0:P], xbc[:, par, DI:DI + P], ident)
                    pe.transpose(PS[:, 3, P:2 * P], xbc[:, par, DI + P:DI + 2 * P], ident).then_inc(s["m_bt"], 1)
                    if c + 1 < T:
                        project(b, c + 1)
                    elif not last:
                        rows_t2(b + 1)
                    if c > 0:
                        if c == 1:
                            pe.wait_ge(s["m_dec"], b + 1)
                        reached(pe, s["m_x"], n - 1)
                        turn(n - 1)
                    pe.wait_ge(s["m_btc"], n + 1)
                    reached(pe, s["m_gm"], n)
                    pe.matmul(PS[:, 4, 0:P], BCt[:, 0, :], BCt[:, 1, :], start=True, stop=True).then_inc(s["m_G"], 1)
                    if c == 0:
                        pe.wait_ge(s["m_h0"], b + 1)
                        pe.wait_ge(s["m_sp"], b * SPN + 1)
                    reached(pe, s["m_y1"], n)
                    pe.matmul(PS[:, 6, 0:DI], BCt[:, 1, :], hst[:, par].rearrange("p h e -> p (h e)"),
                              start=True, stop=True).then_inc(s["m_in"], 1)
                    pe.wait_ge(s["m_xw"], n + 1)
                    pe.matmul(PS[:, 3, 0:DI], xbc[:, par, DI:DI + P], xw[:].rearrange("p h e -> p (h e)"),
                              start=True, stop=True).then_inc(s["m_st"], 1)
                    if c > 0:
                        leave(n - 1)
                    pe.wait_ge(s["m_mt"], n + 1)
                    pe.wait_ge(s["m_xdt"], n + 1)
                    reached(pe, s["m_y2"], n)
                    for h in range(H):
                        m = pe.matmul(PS[:, 5, h * HD:(h + 1) * HD], MT[:, h, :], xdt[:, h, :], start=True, stop=True)
                    m.then_inc(s["m_ie"], 1)
                n = b * T + T - 1
                if not last:
                    steps(b + 1)
                reached(pe, s["m_x"], n)
                turn(n)
                if not last:
                    project(b + 1, 0)
                leave(n)
                if not last:
                    sums(b + 1)

            rows_t2(0)
            steps(0)
            project(0, 0)
            sums(0)
            sequence(0, True, False)
            with pe.Fori(1, B - 1) as b:
                sequence(b, False, False)
            sequence(B - 1, False, True)

            experts(1)

        @block.vector
        def _(dve):
            dve.wait_ge(s["su_bc"], 1)
            dve.tensor_copy(bc[:], PS[:, 7, 0:NR]).then_inc(s["su_bcs"], 1)
            chain = [0]

            def link(ins):
                chain[0] += 1
                ins.then_inc(s["su_rot"], 1)
                dve.wait_ge(s["su_rot"], chain[0])

            dve.wait_ge(s["su_bcs"], 1)
            dve.wait_ge(s["ld_s"], 16 * 8)
            dve.wait_ge(s["ld_m"], 16)
            link(dve.reciprocal(s2[:, 1:2], bc[:, R_SC:R_SC + 1]))
            link(dve.tensor_scalar(s2[:, 0:1], s2[:, 1:2], 2.0, None, ALU.mult))
            link(dve.tensor_scalar(s2[:, 1:2], s2[:, 0:1], bc[:, R_BI:R_BI + 1], None, ALU.add))
            link(dve.tensor_tensor(rn[:, 0, :], rr[:, :, 0], rr[:, :, 0], ALU.mult))
            link(dve.tensor_tensor(rn[:, 1, :], rr[:, :, 1], rr[:, :, 1], ALU.mult))
            dve.tensor_tensor(rn[:, 2, :], rn[:, 0, :], rn[:, 1, :], ALU.add).then_inc(s["su_n2"], 1)
            dve.wait_ge(s["su_mf"], 1)
            cs, sn = rn[:, 4, :], rn[:, 5, :]
            link(dve.tensor_tensor(cs, rr[:, :, 0], rn[:, 3, :], ALU.mult))
            link(dve.tensor_tensor(sn, rr[:, :, 1], rn[:, 3, :], ALU.mult))
            link(dve.tensor_tensor(rn[:, 6, 0:1], sn[:, 0:1], sn[:, 1:2], ALU.mult))
            link(dve.tensor_tensor(rn[:, 6, 1:2], cs[:, 0:1], sn[:, 1:2], ALU.mult))
            link(dve.scalar_tensor_tensor(rn[:, 7, 0:1], cs[:, 0:1], cs[:, 1:2], rn[:, 6, 0:1], ALU.mult, ALU.add))
            link(dve.scalar_tensor_tensor(rn[:, 7, 1:2], sn[:, 0:1], cs[:, 1:2], rn[:, 6, 1:2], ALU.mult, ALU.subtract))
            link(dve.tensor_scalar(rn[:, 7, 0:2], rn[:, 7, 0:2], s2[:, 0:1], None, ALU.mult))
            for j, (c1, s1) in enumerate(((rn[:, 7, 0:1], rn[:, 7, 1:2]), (cs[:, 2:3], sn[:, 2:3]))):
                link(dve.tensor_scalar(Mt[:, j, :], ident, c1, None, ALU.mult))
                link(dve.scalar_tensor_tensor(Mf[:, j, :], swap, s1, Mt[:, j, :], ALU.mult, ALU.add))
            dve.tensor_copy(Mh[:], Mf[:, 0, :]).then_inc(s["su_m"], 1)
            dve.wait_ge(s["su_m"], 1)
            dve.tensor_tensor(Ml[:], Mf[:, 0, :], fp(Mh[:]), ALU.subtract).then_inc(s["su_m"], 1)
            dve.tensor_copy(after_r[:], after).then_inc(s["su_rot"], 1)
            chain[0] += 1
            dve.wait_ge(s["su_dve"], 1)
            link(dve.tensor_copy(ones_r[:], ones[0:1, :]))
            dve.wait_ge(s["su_fin"], 1)
            link(dve.tensor_scalar(negA[:], negA[:], -1.0, None, ALU.mult))
            dve.wait_ge(s["ld_w"], 16 * N_W)
            for k in range(4):
                for w in range(TAPS):
                    dve.tensor_scalar(tapw[:, k, w, :], wi[:, 2 + k, :], cw[:, k, w:w + 1], None,
                                      ALU.mult).then_inc(s["su_tap"], 1)
            n = 0
            for k in range(4):
                dve.wait_ge(s["su_tp"], k + 1)
                src = PS[:, k % 2, :].rearrange("p (w c) -> p w c", w=TAPS)
                c = slice(k * P, (k + 1) * P)
                dve.tensor_copy(wxh[:, :, c], src).then_inc(s["su_tpc"], 1)
                n += 1
                dve.wait_ge(s["su_tpc"], n)
                dve.tensor_tensor(wxl[:, :, c], src, fp(wxh[:, :, c]), ALU.subtract).then_inc(s["su_tpc"], 1)
                n += 1
            dve.wait_ge(s["su_tp"], 5)
            dve.tensor_copy(wdt[:], PS[:, 2, DI:DI + H]).then_inc(s["su_tpc"], 1)
            dve.tensor_copy(wzh[:], PS[:, 2, 0:DI]).then_inc(s["su_tpc"], 1)
            dve.wait_ge(s["su_tpc"], n + 2)
            dve.tensor_tensor(wzl[:], PS[:, 2, 0:DI], fp(wzh[:]), ALU.subtract).then_inc(s["su_tpc"], 1)
            dve.wait_ge(s["su_tp"], 6)
            dve.tensor_copy(b1n[:], PS[:, 3, 2 * P:2 * P + 2 * NX + 2]).then_inc(s["su_tpc"], 1)
            dve.wait_ge(s["su_tpc"], n + 4)
            for j in range(2):
                dve.tensor_scalar(woT[:, j, :], PS[:, 3, j * P:(j + 1) * P], nw[:, j:j + 1], None,
                                  ALU.mult).then_inc(s["su_tpc"], 1)
            dve.wait_ge(s["su_dve"], N_DVE)

            def norm_rows(b, k):
                for t in range(T):
                    dve.bn_stats(stats[:, t, :], X[:, b * T + t, :]).then_inc(s[k + "_bn"], 1)
                dve.wait_ge(s[k + "_bn"], b * (T + 1) + T)
                dve.memset(turn[:], 0.0).then_inc(s[k + "_bn"], 1)
                for t in range(T):
                    dve.bn_aggr(mv[:, t, :], stats[:, t, :]).then_inc(s[k + "_ag"], 1)
                dve.wait_ge(s[k + "_ag"], b * T + T)
                dve.tensor_scalar(ve[:], mv[:, :, 1], EPS, None, ALU.add).then_inc(s[k + "_ve"], 1)

            def norm_rows_2(b, k):
                dve.wait_ge(s[k + "_rs"], b + 1)
                reached(dve, s[k + "_tr"], b * 2)
                for t in range(T):
                    dve.tensor_scalar(xn[:, t, :], X[:, b * T + t, :], mv[:, t, 0:1], rstd[:, t:t + 1],
                                      ALU.subtract, ALU.mult).then_inc(s[k + "_xn"], 1)

            def rows_lo(b, k):
                for h in range(2):
                    c = slice(h * 512, (h + 1) * 512)
                    dve.wait_ge(s[k + "_kh"], b * 2 + h + 1)
                    dve.wait_ge(s[k + "_xf"], b * 2 + h + 1)
                    dve.tensor_tensor(kl[:, c], xTf[:, c], fp(kh[:, c]), ALU.subtract).then_inc(s[k + "_kl"], 1)

            def queries_lo(b):
                for h in range(2):
                    c = slice(h * 512, (h + 1) * 512)
                    dve.wait_ge(s["a_qh"], b * 2 + h + 1)
                    dve.tensor_tensor(ql[:, c], PS[:, 2 + h, :], fp(qh[:, c]), ALU.subtract).then_inc(s["a_ql"], 1)

            def row_max(b, t):
                dve.wait_ge(s["a_S"], b * T + t + 1)
                dve.tensor_reduce(nmx[:, t:t + 1], PS[:, 2 * (t % 2):2 * (t % 2) + 2, :], AX.XY, ALU.max,
                                  negate=True).then_inc(s["a_nm"], 1)
                dve.wait_ge(s["a_nm"], b * T + t + 1)
                dve.tensor_scalar(nbias[:, t:t + 1], nmx[:, t:t + 1], s2[:, 1:2], s2[:, 1:2],
                                  ALU.subtract, ALU.add).then_inc(s["a_nb"], 1)

            def o_copy(b, t):
                dve.wait_ge(s["a_pv"], b * T + t + 1)
                reached(dve, s["a_x"], b * 2 - 1 + (t >= 4))
                dve.tensor_copy(Osb[:, t, :], PS[:, 6 + t % 2, 0:D]).then_inc(s["a_oc"], 1)
                dve.wait_ge(s["a_oc"], b * T + t + 1)
                reached(dve, s["a_ss"], b * T + t)
                dve.tensor_tensor_reduce(osq[:], Osb[:, t, :], Osb[:, t, :], 1.0, 0.0, ALU.mult, ALU.add,
                                         nrm[:, 0, t:t + 1]).then_inc(s["a_ss"], 1)

            def norm_1(b, hf):
                h = slice(4 * hf, 4 * hf + 4)
                n = b * 6 + 3 * hf
                dve.reciprocal(nrm[:, 1, h], lsum[:, h]).then_inc(s["a_nc"], 1)
                dve.wait_ge(s["a_nc"], n + 1)
                dve.wait_ge(s["a_ss"], b * T + 4 * hf + 4)
                dve.tensor_tensor(nrm[:, 2, h], nrm[:, 0, h], nrm[:, 1, h], ALU.mult).then_inc(s["a_nc"], 1)
                dve.wait_ge(s["a_nc"], n + 2)
                dve.tensor_tensor(nrm[:, 2, h], nrm[:, 2, h], nrm[:, 1, h], ALU.mult).then_inc(s["a_nc"], 1)
                dve.wait_ge(s["a_nc"], n + 3)
                dve.tensor_scalar(nrm[:, 3, h], nrm[:, 2, h], SMALL, None, ALU.max).then_inc(s["a_cl"], 1)

            def norm_2(b, hf):
                h = slice(4 * hf, 4 * hf + 4)
                dve.wait_ge(s["a_pw"], b * 2 + hf + 1)
                dve.tensor_tensor(nrm[:, 5, h], nrm[:, 4, h], nrm[:, 1, h], ALU.mult).then_inc(s["a_fc"], 1)
                dve.wait_ge(s["a_fc"], b * 2 + hf + 1)
                for t in range(4 * hf, 4 * hf + 4):
                    xt = X[:, b * T + t, :]
                    m = dve.scalar_tensor_tensor(xt, Osb[:, t, :], nrm[:, 5, t:t + 1], xt, ALU.mult, ALU.add)
                m.then_inc(s["a_x"], 1)

            def attend(b, first, last):
                for t in range(T):
                    if t + 2 < T:
                        row_max(b, t + 2)
                    if t >= 1:
                        o_copy(b, t - 1)
                    if t == 1 and not first:
                        norm_2(b - 1, 1)
                    if t == 2 and not last:
                        dve.wait_ge(s["ld_x"], 16 * (b + 2))
                        norm_rows(b + 1, "a")
                    if t == 4 and not last:
                        norm_rows_2(b + 1, "a")
                    if t == 5:
                        norm_1(b, 0)
                    if t == 6:
                        norm_2(b, 0)
                if not last:
                    rows_lo(b + 1, "a")
                    queries_lo(b + 1)
                o_copy(b, T - 1)
                norm_1(b, 1)
                if not last:
                    row_max(b + 1, 0)
                    row_max(b + 1, 1)

            dve.wait_ge(s["ld_x"], 16)
            norm_rows(0, "a")
            norm_rows_2(0, "a")
            rows_lo(0, "a")
            queries_lo(0)
            row_max(0, 0)
            row_max(0, 1)
            attend(0, True, False)
            with dve.Fori(1, B - 1) as b:
                attend(b, False, False)
            attend(B - 1, False, True)
            norm_2(B - 1, 1)

            def experts(k):
                def rows(g):
                    if isinstance(g, int) and g == 0:
                        dve.wait_ge(s["a_x"], 2 * B) if k == 0 else dve.wait_ge(s["m_x"], NT)
                    for t in range(G4):
                        dve.bn_stats(fst[:, t, :], X[:, g * G4 + t, :]).then_inc(s["f_bn%d" % k], 1)
                    dve.wait_ge(s["f_bn%d" % k], g * (G4 + 1) + G4)
                    dve.memset(turn[:], 0.0).then_inc(s["f_bn%d" % k], 1)
                    for t in range(G4):
                        dve.bn_aggr(fmv[:, t, :], fst[:, t, :]).then_inc(s["f_ag%d" % k], 1)
                    dve.wait_ge(s["f_ag%d" % k], (g + 1) * G4)
                    dve.tensor_scalar(fve[:], fmv[:, :, 1], EPS, None, ALU.add).then_inc(s["f_ve%d" % k], 1)
                    dve.wait_ge(s["f_rs%d" % k], g + 1)
                    dve.wait_ge(s["f_tr%d" % k], g)
                    for t in range(G4):
                        dve.tensor_scalar(fxn[:, t, :], X[:, g * G4 + t, :], fmv[:, t, 0:1], frs[:, t:t + 1],
                                          ALU.subtract, ALU.mult).then_inc(s["f_xn%d" % k], 1)

                def rows_lo(g, par):
                    dve.wait_ge(s["f_xh%d" % k], g + 1)
                    dve.tensor_tensor(fxl[:, par, :], PS[:, 6, :], fp(fxh[:, par, :]),
                                      ALU.subtract).then_inc(s["f_xl%d" % k], 1)

                def logits(g):
                    dve.wait_ge(s["f_gl%d" % k], g + 1)
                    gb = bc[:, R_GB:R_GB + NE].unsqueeze(1).broadcast_to([P, G4, NE])
                    n = [g * 8]

                    def step(ins):
                        n[0] = n[0] + 1
                        ins.then_inc(s["f_lg%d" % k], 1)
                        dve.wait_ge(s["f_lg%d" % k], n[0])

                    def each(v):
                        return v.unsqueeze(2).broadcast_to([P, G4, NE])

                    dve.tensor_tensor(lg[:, 0], PS[:, 7, 0:G4 * NE].rearrange("p (t e) -> p t e", t=G4), gb,
                                      ALU.add).then_inc(s["f_la%d" % k], 1)
                    dve.wait_ge(s["f_la%d" % k], g + 1)
                    step(dve.tensor_reduce(g1[:, 0, :], lg[:, 0], AX.X, ALU.max))
                    step(dve.tensor_tensor(lg[:, 1], lg[:, 0], each(g1[:, 0, :]), ALU.subtract))
                    step(dve.scalar_tensor_tensor(lg[:, 3], lg[:, 1], 0.0, rank[:], ALU.is_ge, ALU.mult))
                    step(dve.tensor_reduce(g1[:, 1, :], lg[:, 3], AX.X, ALU.max))
                    step(dve.tensor_tensor(lg[:, 4], lg[:, 3], each(g1[:, 1, :]), ALU.is_equal))
                    step(dve.scalar_tensor_tensor(lg[:, 5], lg[:, 4], -BIG, lg[:, 1], ALU.mult, ALU.add))
                    step(dve.tensor_reduce(g1[:, 2, :], lg[:, 5], AX.X, ALU.max))
                    step(dve.tensor_tensor(lg[:, 6], lg[:, 5], each(g1[:, 2, :]), ALU.is_ge))

                def choose(g, par):
                    n = [g * 8]

                    def step(ins):
                        n[0] = n[0] + 1
                        ins.then_inc(s["f_ch%d" % k], 1)
                        dve.wait_ge(s["f_ch%d" % k], n[0])

                    def each(v):
                        return v.unsqueeze(2).broadcast_to([P, G4, NE])

                    step(dve.tensor_tensor(lg[:, 7], lg[:, 6], rank[:], ALU.mult))
                    step(dve.tensor_reduce(g1[:, 3, :], lg[:, 7], AX.X, ALU.max))
                    step(dve.tensor_tensor(lg[:, 8], lg[:, 7], each(g1[:, 3, :]), ALU.is_equal))
                    step(dve.tensor_tensor(lg[:, 9], lg[:, 8], lg[:, 4], ALU.add))
                    dve.wait_ge(s["f_th%d" % k], g + 1)
                    step(dve.tensor_scalar(lg[:, 10], lg[:, 2], -1.0, 1.0, ALU.mult, ALU.add))
                    step(dve.reciprocal(lg[:, 11], lg[:, 10]))
                    step(dve.scalar_tensor_tensor(lg[:, 10], lg[:, 2], 1.0, lg[:, 11], ALU.add, ALU.mult))
                    step(dve.tensor_reduce(g1[:, 4, :], lg[:, 10], AX.X, ALU.add))
                    dve.reciprocal(g1[:, 5, :], g1[:, 4, :]).then_inc(s["f_ca%d" % k], 1)
                    dve.tensor_tensor(lg[:, 11], lg[:, 10], lg[:, 9], ALU.mult).then_inc(s["f_ca%d" % k], 1)
                    dve.wait_ge(s["f_ca%d" % k], g * 2 + 2)
                    dve.tensor_tensor(cwt[:, par, :, 0:NE], lg[:, 11], each(g1[:, 5, :]),
                                      ALU.mult).then_inc(s["f_cw%d" % k], 1)

                def multiply(g, e, o):
                    dve.wait_ge(s["f_s%d" % k], g * NX + e + 1)
                    reached(dve, s["f_o%d" % k], g * NX + e - 1)
                    dve.scalar_tensor_tensor(gf[:, o, :], PS[:, 2 * o + 1, :], b1[:, e, 1:2], sil[:, o, :],
                                             ALU.add, ALU.mult).then_inc(s["f_g%d" % k], 1)

                def add(g, e, par, o):
                    dve.wait_ge(s["f_o%d" % k], g * NX + e + 1)
                    reached(dve, s["f_x%d" % k], g * NX + e)
                    if e == 0:
                        xg = X[:, bass.ds(g * G4, G4), :]
                        m = dve.tensor_tensor(xg, PS[:, 4 + o, :].rearrange("p (t d) -> p t d", t=G4), xg, ALU.add)
                    else:
                        for t in range(G4):
                            xt = X[:, g * G4 + t, :]
                            m = dve.scalar_tensor_tensor(xt, PS[:, 4 + o, t * P:(t + 1) * P],
                                                         cwt[:, par, t, e - 1:e], xt, ALU.mult, ALU.add)
                    m.then_inc(s["f_x%d" % k], 1)

                rows(0)
                rows_lo(0, 0)
                logits(0)
                choose(0, 0)

                def group(g, par, last):
                    for e in range(NX):
                        o = (par * NX + e) % 2
                        multiply(g, e, o)
                        if e >= 1:
                            add(g, e - 1, par, 1 - o)
                        if not last:
                            if e == 1:
                                rows(g + 1)
                            if e == 4:
                                rows_lo(g + 1, 1 - par)
                            if e == 6:
                                logits(g + 1)
                                choose(g + 1, 1 - par)
                    add(g, NX - 1, par, o)

                group(0, 0, False)
                group(1, 1, False)
                with dve.Fori(1, NG // 2 - 1) as i:
                    group(2 * i, 0, False)
                    group(2 * i + 1, 1, False)
                group(NG - 2, 0, False)
                group(NG - 1, 1, True)

            experts(0)

            def steps(b):
                n = [b * SPN]

                def step(ins):
                    n[0] = n[0] + 1
                    ins.then_inc(s["m_sp"], 1)
                    dve.wait_ge(s["m_sp"], n[0])

                dve.wait_ge(s["m_dp"], b + 1)
                step(dve.tensor_tensor(sp[:, 0], PS[:, 6, 0:T * H].rearrange("p (c h) -> p c h", c=T),
                                       bc[:, R_DB:R_DB + H].unsqueeze(1).broadcast_to([P, T, H]), ALU.add))
                step(dve.scalar_tensor_tensor(sp[:, 1], sp[:, 0], -1.0, sp[:, 0], ALU.mult, ALU.min))
                dve.wait_ge(s["m_ex1"], b + 1)
                step(dve.tensor_scalar(sp[:, 3], sp[:, 2], 2.0, None, ALU.add))
                step(dve.reciprocal(sp[:, 4], sp[:, 3]))
                step(dve.tensor_tensor(sp[:, 5], sp[:, 2], sp[:, 4], ALU.mult))
                step(dve.tensor_tensor(sp[:, 6], sp[:, 5], sp[:, 5], ALU.mult))
                step(dve.tensor_scalar(sp[:, 7], sp[:, 6], 2.0 / 17, 2.0 / 15, ALU.mult, ALU.add))
                for odd in (13, 11, 9, 7, 5, 3, 1):
                    step(dve.tensor_tensor(sp[:, 7], sp[:, 7], sp[:, 6], ALU.mult))
                    step(dve.tensor_scalar(sp[:, 7], sp[:, 7], 2.0 / odd, None, ALU.add))
                step(dve.tensor_tensor(sp[:, 7], sp[:, 7], sp[:, 5], ALU.mult))
                reached(dve, s["m_xdt"], b * T)
                dve.scalar_tensor_tensor(dtv[:], sp[:, 0], 0.0, sp[:, 7], ALU.max, ALU.add).then_inc(s["m_dt"], 1)
                dve.wait_ge(s["m_dt"], b * 2 + 1)
                dve.tensor_tensor(av[:], dtv[:], negA[:].unsqueeze(1).broadcast_to([P, T, H]),
                                  ALU.mult).then_inc(s["m_dt"], 1)
                dve.wait_ge(s["m_dt"], b * 2 + 2)
                dve.tensor_copy(ahr[:], av[:]).then_inc(s["m_a"], 1)
                dve.wait_ge(s["m_a"], b + 1)
                dve.tensor_tensor(alr[:], av[:], fp(ahr[:]), ALU.subtract).then_inc(s["m_al"], 1)

            def heads(v):
                return v.rearrange("p (h e) -> p h e", h=H)

            def state_0(b):
                reached(dve, s["m_hc"], b * T)
                reached(dve, s["m_in"], b * T)
                reached(dve, s["m_h"], b * T)
                dve.memset(hst[:, 0], 0.0).then_inc(s["m_h0"], 1)

            def leave(b, c):
                n = b * T + c
                dve.wait_ge(s["m_rr"], n + 1)
                dve.wait_ge(s["m_o"], n + 1)
                xt = X[:, b * T + c, :]
                dve.scalar_tensor_tensor(xt, PS[:, 7, 0:D], yrs[:, c:c + 1], xt, ALU.mult,
                                         ALU.add).then_inc(s["m_x"], 1)

            def sequence(b, first, last):
                for c in range(T):
                    n = b * T + c
                    par = c % 2
                    dve.wait_ge(s["m_G"], n + 1)
                    reached(dve, s["m_mt"], n)
                    dve.tensor_tensor(Gm, PS[:, 4, 0:P], upto, ALU.mult).then_inc(s["m_gm"], 1)
                    dve.wait_ge(s["m_gm"], n + 1)
                    dve.wait_ge(s["m_lx"], n + 1)
                    reached(dve, s["m_ie"], n)
                    dve.tensor_tensor(MT, Lx, Gm.unsqueeze(1).broadcast_to([P, H, P]), ALU.mult).then_inc(s["m_mt"], 1)
                    dve.wait_ge(s["m_in"], n + 1)
                    dve.wait_ge(s["m_dec"], b + 1)
                    dve.tensor_tensor(heads(yb[:, 0, :]), heads(PS[:, 6, 0:DI]),
                                      dec[:, 0, c, :].unsqueeze(2).broadcast_to([P, H, HD]),
                                      ALU.mult).then_inc(s["m_y1"], 1)
                    dve.wait_ge(s["m_st"], n + 1)
                    dve.wait_ge(s["m_hc"], n + 1)
                    dve.tensor_tensor(hst[:, 1 - par], heads(PS[:, 3, 0:DI]), hc[:], ALU.add).then_inc(s["m_h"], 1)
                    if c > 0:
                        leave(b, c - 1)
                    dve.wait_ge(s["m_y1"], n + 1)
                    dve.wait_ge(s["m_ie"], n + 1)
                    dve.tensor_tensor(yb[:, 1, :], PS[:, 5, 0:DI], yb[:, 0, :], ALU.add).then_inc(s["m_y2"], 1)
                    dve.wait_ge(s["m_y2"], n + 1)
                    dve.wait_ge(s["m_xd"], n + 1)
                    dve.tensor_tensor(yb[:, 0, :], yb[:, 1, :], xD.rearrange("p h e -> p (h e)"),
                                      ALU.add).then_inc(s["m_y3"], 1)
                    dve.wait_ge(s["m_y3"], n + 1)
                    dve.wait_ge(s["m_zs"], n + 1)
                    reached(dve, s["m_yt"], n)
                    reached(dve, s["m_sq"], n)
                    dve.tensor_tensor(yb[:, 2, :], yb[:, 0, :], zs[:, par, :], ALU.mult).then_inc(s["m_y4"], 1)
                    if c == T - 1 and not last:
                        rows_lo(b + 1, "m")
                    dve.wait_ge(s["m_sq"], n + 1)
                    dve.tensor_scalar(yms[:, c:c + 1], ysq[:, c:c + 1], 1.0 / DI, EPS, ALU.mult,
                                      ALU.add).then_inc(s["m_ms"], 1)
                    if c == 2 and not last:
                        norm_rows(b + 1, "m")
                    if c == 4 and not last:
                        norm_rows_2(b + 1, "m")
                if not last:
                    state_0(b + 1)
                    steps(b + 1)
                leave(b, T - 1)

            norm_rows(0, "m")
            norm_rows_2(0, "m")
            rows_lo(0, "m")
            state_0(0)
            steps(0)
            sequence(0, True, False)
            with dve.Fori(1, B - 1) as b:
                sequence(b, False, False)
            sequence(B - 1, False, True)

            experts(1)


_INS = ['L0_attn_a_Q', 'L0_attn_a_rot_w', 'L0_attn_a_scale', 'L0_attn_a_bias', 'L0_attn_b_W_in',
        'L0_attn_b_conv_w', 'L0_attn_b_conv_b', 'L0_attn_b_dt_bias', 'L0_attn_b_A_log', 'L0_attn_b_D',
        'L0_attn_b_norm_w', 'L0_attn_b_W_out', 'L0_ffn_gate_w', 'L0_ffn_gate_b', 'L0_ffn_sw1', 'L0_ffn_sb1',
        'L0_ffn_sw2', 'L0_ffn_sb2', 'L0_ffn_rw1', 'L0_ffn_rb1', 'L0_ffn_rw2', 'L0_ffn_rb2']


def kernel(**inputs):
    import numpy as _np
    import concourse.bacc as _bacc
    from concourse import mybir as _mybir
    from concourse.bass_utils import run_bass_kernel_spmd as _run

    nc = _bacc.Bacc("TRN2", target_bir_lowering=False, num_devices=1)
    arrays, args = {}, []

    def give(name, a):
        arrays[name] = a
        args.append(nc.dram_tensor(name, a.shape, _mybir.dt.from_np(a.dtype), kind="ExternalInput").ap())

    for name in _INS:
        a = _np.ascontiguousarray(inputs[name])
        give(f"in_{name}_dram", a.reshape(1, 1) if a.ndim == 0 else a)
    n = 128
    r, c = _np.arange(n)[:, None], _np.arange(n)[None, :]
    swap = _np.where((r % 2 == 0) & (c == r + 1), 1.0, 0.0) - _np.where((r % 2 == 1) & (c == r - 1), 1.0, 0.0)
    give("in_masks_dram", _np.ascontiguousarray(
        _np.stack([_np.eye(n), swap, r <= c, r > c], axis=1).astype(_np.float32)))
    shape = inputs['L0_attn_a_Q'].shape
    args.append(nc.dram_tensor("out_0_dram", shape, _mybir.dt.float32, kind="ExternalOutput").ap())
    hybrid_block_kernel(nc, *args)
    return _run(nc, [arrays], core_ids=[0]).results[0]["out_0_dram"]
```

```python
import concourse.bass as bass
from concourse import mybir
from contextlib import ExitStack

N_W = 15
N_TPC = 8
N_DVE = 11
SPN = 15


def hybrid_block_kernel(nc: bass.Bass, Q: bass.AP, rot_w: bass.AP, scale: bass.AP, bias: bass.AP,
                        W_in: bass.AP, conv_w: bass.AP, conv_b: bass.AP, dt_bias: bass.AP, A_log: bass.AP,
                        D_skip: bass.AP, norm_w: bass.AP, W_out: bass.AP, gate_w: bass.AP, gate_b: bass.AP,
                        sw1: bass.AP, sb1: bass.AP, sw2: bass.AP, sb2: bass.AP, rw1: bass.AP, rb1: bass.AP,
                        rw2: bass.AP, rb2: bass.AP, masks: bass.AP, out: bass.AP):
    f32, f32r = mybir.dt.float32, mybir.dt.float32r
    ALU = mybir.AluOpType
    ACT = mybir.ActivationFunctionType
    AX = mybir.AxisListType

    B, S, D = Q.shape
    P = 128
    T = S // P
    NT = B * T
    NE = rw1.shape[0]
    F = rw2.shape[1]
    NX = NE + 1
    G4 = 4
    NG = NT // G4
    H = D_skip.shape[0]
    DI = W_out.shape[1]
    HD = DI // H
    NS = P
    TAPS = conv_w.shape[1]
    CC = DI + 2 * NS
    PAD = TAPS - 1
    EPS = 1e-5
    SMALL = 1e-8
    BIG = 1e30

    ctx = ExitStack()
    with ctx:
        def sb(name, shape, dt=f32):
            return ctx.enter_context(nc.sbuf_tensor(name, shape, dt))

        def sem(name):
            return ctx.enter_context(nc.semaphore(name))

        def fp(ap):
            return ap.bitcast(f32)

        X = sb("X", [P, NT, D])
        mk = sb("mk", [P, 4, P])
        ident, swap, upto, after = (mk[:, n, :] for n in range(4))
        ones = sb("ones", [P, P])
        after_r = sb("after_r", [P, P], f32r)
        half = sb("half", [P, T])
        w2s = sb("w2s", [F, NX, D])
        w1h = sb("w1h", [P, NX, 2 * F], f32r)
        w1l = sb("w1l", [P, NX, 2 * F], f32r)
        NC = 2 * NX + 2 + 4
        cols = sb("cols", [NC, P])
        b1n = sb("b1n", [P, NC])
        b1 = b1n[:, 0:2 * NX].rearrange("p (e k) -> p e k", k=2)
        nw = b1n[:, 2 * NX:2 * NX + 2]
        cb = b1n[:, 2 * NX + 2:]
        b2 = sb("b2", [NX, D])
        gws = sb("gws", [P, NE])
        rank = sb("rank", [P, G4, NE])

        R_SC, R_BI, R_GB, R_D, R_DB, R_AL = 0, 1, 2, 2 + NE, 2 + NE + H, 2 + NE + 2 * H
        NR = R_AL + H
        row = sb("row", [1, NR])
        bc = sb("bc", [P, NR])
        negA = sb("negA", [P, H])
        rr = sb("rr", [P, 3, 2])
        rn = sb("rn", [P, 8, 3])
        Mf = sb("Mf", [P, 2, P])
        Mt = sb("Mt", [P, 2, P])
        Mh = sb("Mh", [P, P], f32r)
        Ml = sb("Ml", [P, P], f32r)
        s2 = sb("s2", [P, 2])
        wid = sb("wid", [H, D])
        cw = sb("cw", [P, 4, TAPS])
        wxh = sb("wxh", [P, CC], f32r)
        wxl = sb("wxl", [P, CC], f32r)
        wzh = sb("wzh", [P, DI], f32r)
        wzl = sb("wzl", [P, DI], f32r)
        wdt = sb("wdt", [P, H])
        wos = sb("wos", [P, DI])
        woT = sb("woT", [P, 2, D])

        stats = sb("stats", [P, T, 6])
        mv = sb("mv", [P, T, 2])
        ve = sb("ve", [P, T])
        turn = sb("turn", [P, 1])
        rstd = sb("rstd", [P, T])
        xn = sb("xn", [P, T, D])
        kh = sb("kh", [P, S], f32r)
        kl = sb("kl", [P, S], f32r)
        xTf = sb("xTf", [P, S])

        AR = sb("AR", [P, 2 * S], f32r)
        AF = sb("AF", [P, 13 * S])
        at = [0, 0]

        def part(which, shape):
            n = 1
            for k in shape:
                n *= k
            lo = at[which]
            at[which] += n
            ap = (AF, AR)[which][:, lo:lo + n]
            if len(shape) == 2:
                ap = ap.rearrange("p (a b) -> p a b", a=shape[0])
            if len(shape) == 3:
                ap = ap.rearrange("p (a b c) -> p a b c", a=shape[0], b=shape[1])
            return ap

        at[:] = [7 * S, 0]
        wi = part(0, [6, D])
        w1s = part(0, [NX, 2 * F])
        at[:] = [0, 0]
        qh, ql = part(1, [S]), part(1, [S])
        Pr = part(0, [2, S])
        Osb = part(0, [T, D])
        PT = part(0, [2, S])
        vf = part(0, [T, D])
        osq = sb("osq", [P, D])
        lsum = sb("lsum", [P, T])
        nmx = sb("nmx", [P, T])
        nbias = sb("nbias", [P, T])
        nrm = sb("nrm", [P, 6, T])

        at[:] = [0, 0]
        Uh, Ul = part(1, [2, H, P]), part(1, [2, H, P])
        HT = T // 2
        HS = HT * P
        pj = part(0, [4, PAD + S])
        cv = part(0, [2, 4, HS])
        zs = part(0, [2, HT, DI])
        xb = part(0, [2, 3 * P])
        Lx = part(0, [H, P])
        MT = part(0, [H, P])
        Gm = part(0, [P])
        xdt = part(0, [2, H, HD])
        Ddiag = sb("Ddiag", [P, H, P])
        xw = sb("xw", [P, 2, H, HD])
        hc = sb("hc", [P, H, HD])
        hst = part(0, [2, H, HD])
        yb = sb("yb", [P, 3, DI])
        yq = sb("yq", [P, DI])
        yT = sb("yT", [P, 2, P])
        ysq = sb("ysq", [P, T])
        yms = sb("yms", [P, T])
        yrs = sb("yrs", [P, T])
        sp = sb("sp", [P, 8, HT, H])
        dtv = sb("dtv", [P, 2, HT, H])
        av = sb("av", [P, 2, HT, H])
        ahr = sb("ahr", [P, 2, HT, H], f32r)
        alr = sb("alr", [P, 2, HT, H], f32r)
        dec = sb("dec", [P, 2, 3, HT, H])

        BY_ACT = (1, 3, 5, 7, NE)
        BY_DVE = tuple(e for e in range(NX) if e not in BY_ACT)
        NA = len(BY_ACT)
        NV = len(BY_DVE)
        GN = 19
        at[:] = [0, 0]
        fst = sb("fst", [P, G4, 6])
        fmv = sb("fmv", [P, G4, 2])
        fve = sb("fve", [P, G4])
        frs = sb("frs", [P, G4])
        fxh = part(1, [2, G4 * P])
        fxl = part(1, [2, G4 * P])
        fxn = part(0, [G4, D])
        fxf = part(0, [G4 * P])
        wsum = part(0, [2, NA, G4 * P])
        fnm = sb("fnm", [P, G4])
        lg = sb("lg", [P, 12, G4, NE])
        g1 = sb("g1", [P, 6, G4])
        cwt = sb("cwt", [P, 2, G4, NX])
        cwT = sb("cwT", [NX, G4, P])
        sil = part(0, [2, G4 * P])
        gf = part(0, [2, G4 * P])

        PS = ctx.enter_context(nc.psum_tensor("PS", [P, 8, 512], f32))

        names = """ld_x ld_w ld_m ld_s su_w su_bc su_bcs su_rot su_mf su_m su_tp su_tpc su_dve su_fin su_n2
            a_bn a_ag a_ve a_rs a_xn a_tr a_kh a_kl a_xf a_qp a_qh a_ql a_vp a_vf a_S a_nm a_nb a_ex a_pt a_ptc
            a_pv a_oc a_ss a_nc a_cl a_pw a_fc a_x
            m_bn m_ag m_ve m_rs m_xn m_tr m_kh m_kl m_xf m_dp m_sp m_ex1 m_dt m_a m_al m_cs m_dec m_px m_pj m_t3 m_cn
            m_cv m_pz m_zc m_U m_L m_lx m_bt m_xb m_G m_gm m_mt m_xdt m_xw m_hc m_in m_ie m_y1 m_y2 m_y4 m_sq m_ms
            m_rr m_yt m_ytc m_o m_st m_h m_x m_h0 m_cn0 o_done""".split()
        for k in (0, 1):
            names += [n + str(k) for n in """f_bn f_ag f_ve f_rs f_nm f_xn f_tr f_xh f_xf f_xl f_gl f_lg f_th f_cw f_ct
                f_ctc f_h f_s f_g f_o f_x f_xa f_as f_xw""".split()]
        s = {n: sem(n) for n in names}

        x_dram = Q.rearrange("b (t p) d -> b p t d", p=P)
        o_dram = out.rearrange("b (t p) d -> (b t) p d", p=P)

        block = ctx.enter_context(nc.Block())

        def reached(eng, sm, value):
            if not (isinstance(value, int) and value <= 0):
                eng.wait_ge(sm, value)

        def output_read(eng, k, g, e):
            if e < 0:
                g, e = g - 1, e + NX
            if e in BY_ACT:
                reached(eng, s["f_xa%d" % k], g * NA + BY_ACT.index(e) + 1)
            else:
                reached(eng, s["f_x%d" % k], g * NV + BY_DVE.index(e) + 1)

        def mm3(pe, dst, ah, al, bh, bl, start=True, stop=True):
            pe.matmul(dst, ah, bh, start=start, stop=False)
            pe.matmul(dst, ah, bl, start=False, stop=False)
            return pe.matmul(dst, al, bh, start=False, stop=stop)

        @block.sync
        def _(sp_):
            sp_.dma_start(mk[:], masks).then_inc(s["ld_m"], 16)
            for n, src in ((R_SC, scale), (R_GB, gate_b), (R_D, D_skip), (R_DB, dt_bias), (R_AL, A_log)):
                sp_.dma_start(row[0:1, n:n + src.shape[0]], src.rearrange("(a n) -> a n", a=1)).then_inc(s["ld_s"], 16)
            sp_.dma_start(row[0:1, R_BI:R_BI + 1], bias).then_inc(s["ld_s"], 16)
            pairs = rot_w.rearrange("w (j two) -> j w two", two=2)
            for n in range(2):
                sp_.dma_start(rr[n::2], pairs).then_inc(s["ld_s"], 16)
            for b in range(B):
                sp_.dma_start(X[:, b * T:(b + 1) * T, :], x_dram[b]).then_inc(s["ld_x"], 16)
                sp_.wait_ge(s["ld_x"], 16 * (b + 1))
            with sp_.Fori(0, NG) as g:
                sp_.wait_ge(s["f_xw1"], g + 1)
                sp_.dma_start(o_dram[bass.ds(g * G4, G4)].rearrange("t p d -> p t d"),
                              X[:, bass.ds(g * G4, G4), :]).then_inc(s["o_done"], 16)
            sp_.wait_ge(s["o_done"], 16 * NG)

        @block.gpsimd
        def _(pool):
            pool.memset(ones[:], 1.0).then_inc(s["su_dve"], 1)
            pool.memset(half[:], -0.5).then_inc(s["su_dve"], 1)
            for e in range(NE):
                pool.memset(rank[:, :, e:e + 1], float(NE - e)).then_inc(s["su_dve"], 1)
            pool.memset(cwt[:], 1.0).then_inc(s["su_dve"], 1)
            pool.wait_ge(s["su_dve"], N_DVE)
            pool.wait_ge(s["su_n2"], 1)
            pool.tensor_tensor(rn[:, 3, :], rn[:, 2, :], half[:, 0:3], ALU.pow).then_inc(s["su_mf"], 1)
            def rows_power(b, k):
                pool.wait_ge(s[k + "_ve"], b + 1)
                pool.tensor_tensor(rstd[:], ve[:], half[:], ALU.pow).then_inc(s[k + "_rs"], 1)

            def norm_power(b, hf):
                h = slice(4 * hf, 4 * hf + 4)
                pool.wait_ge(s["a_cl"], b * 2 + hf + 1)
                pool.tensor_tensor(nrm[:, 4, h], nrm[:, 3, h], half[:, h], ALU.pow).then_inc(s["a_pw"], 1)

            def attend(b, last):
                if not last:
                    rows_power(b + 1, "a")
                norm_power(b, 0)
                norm_power(b, 1)

            rows_power(0, "a")
            attend(0, False)
            pool.wait_ge(s["ld_w"], 16 * N_W)
            pool.tensor_copy(w1h[:], w1s[:]).then_inc(s["su_w"], 1)
            pool.wait_ge(s["su_w"], 1)
            pool.tensor_tensor(w1l[:], w1s[:], fp(w1h[:]), ALU.subtract).then_inc(s["su_w"], 1)
            with pool.Fori(1, B - 1) as b:
                attend(b, False)
            attend(B - 1, True)

            def experts(k):
                def power(g):
                    pool.wait_ge(s["f_ve%d" % k], g + 1)
                    pool.tensor_tensor(frs[:], fve[:], half[:, 0:G4], ALU.pow).then_inc(s["f_rs%d" % k], 1)

                def rows_lo(g, par):
                    pool.wait_ge(s["f_xf%d" % k], g + 1)
                    pool.tensor_tensor(fxl[:, par, :], fxf, fp(fxh[:, par, :]), ALU.subtract).then_inc(s["f_xl%d" % k], 1)

                def sum_weighed(g, par, j):
                    pool.wait_ge(s["f_xa%d" % k], g * NA + j + 1)
                    if j > 1:
                        pool.wait_ge(s["f_as%d" % k], g * (NA - 1) + j - 1)
                    pool.tensor_tensor(wsum[:, par, 0, :], wsum[:, par, 0, :], wsum[:, par, j, :],
                                       ALU.add).then_inc(s["f_as%d" % k], 1)

                def group(g, par, late, last):
                    if not last:
                        rows_lo(g + 1, 1 - par)
                    for j in range(1, NA - 1):
                        sum_weighed(g, par, j)
                    if not late:
                        power(g + 2)
                    sum_weighed(g, par, NA - 1)

                power(0)
                rows_lo(0, 0)
                power(1)
                group(0, 0, False, False)
                group(1, 1, False, False)
                with pool.Fori(1, NG // 2 - 1) as i:
                    group(2 * i, 0, False, False)
                    group(2 * i + 1, 1, False, False)
                group(NG - 2, 0, True, False)
                group(NG - 1, 1, True, True)

            experts(0)

            def rows_power_half(b, hf):
                h = slice(hf * HT, (hf + 1) * HT)
                pool.wait_ge(s["m_ve"], b * 2 + hf + 1)
                pool.tensor_tensor(rstd[:, h], ve[:, h], half[:, 0:HT], ALU.pow).then_inc(s["m_rs"], 1)

            def steps_of_a(b, hf, c):
                q = b * 2 + hf
                pool.wait_ge(s["m_al"], q + 1)
                reached(pool, s["m_L"], q * HT + c - 1)
                up = upto.unsqueeze(1).broadcast_to([P, H, P])
                pool.tensor_tensor(Uh[:, c % 2], up, fp(ahr[:, hf, c, :]).unsqueeze(2).broadcast_to([P, H, P]),
                                   ALU.mult).then_inc(s["m_U"], 1)
                pool.tensor_tensor(Ul[:, c % 2], up, fp(alr[:, hf, c, :]).unsqueeze(2).broadcast_to([P, H, P]),
                                   ALU.mult).then_inc(s["m_U"], 1)

            def root(n, t):
                pool.wait_ge(s["m_ms"], n + 1)
                pool.tensor_tensor(yrs[:, t:t + 1], yms[:, t:t + 1], half[:, 0:1], ALU.pow).then_inc(s["m_rr"], 1)

            def sequence(b, first, last):
                for t in range(T):
                    hf, c = divmod(t, HT)
                    q, n = b * 2 + hf, b * T + t
                    x4 = xb[:, c % 2, 0:DI].rearrange("p (h e) -> p h e", h=H)
                    pool.wait_ge(s["m_xb"], n + 1)
                    reached(pool, s["m_ie"], n - 1)
                    pool.tensor_tensor(xdt[:, c % 2], x4, dtv[:, hf, c, :].unsqueeze(2).broadcast_to([P, H, HD]),
                                       ALU.mult).then_inc(s["m_xdt"], 1)
                    pool.wait_ge(s["m_dec"], q + 1)
                    pool.wait_ge(s["m_xdt"], n + 1)
                    reached(pool, s["m_st"], n - 1)
                    pool.tensor_tensor(xw[:, c % 2], xdt[:, c % 2], dec[:, hf, 1, c, :].unsqueeze(2).broadcast_to([P, H, HD]),
                                       ALU.mult).then_inc(s["m_xw"], 1)
                    if t == 0:
                        pool.wait_ge(s["m_h0"], b + 1)
                    reached(pool, s["m_h"], n)
                    pool.tensor_tensor(hc[:], hst[:, c % 2], dec[:, hf, 2, c, :].unsqueeze(2).broadcast_to([P, H, HD]),
                                       ALU.mult).then_inc(s["m_hc"], 1)
                    nb, nh = (b, 1) if hf == 0 else (b + 1, 0)
                    more = not (last and hf == 1)
                    if c + 2 < HT:
                        steps_of_a(b, hf, c + 2)
                    elif c == HT - 1 and more:
                        steps_of_a(nb, nh, 0)
                    if c == 1 and not last:
                        rows_power_half(b + 1, hf)
                    if not (first and t == 0):
                        root(n - 1, (t - 1) % T)
                    if c == HT - 1 and more:
                        steps_of_a(nb, nh, 1)
                if last:
                    root(b * T + T - 1, T - 1)

            rows_power_half(0, 0)
            rows_power_half(0, 1)
            steps_of_a(0, 0, 0)
            steps_of_a(0, 0, 1)
            sequence(0, True, False)
            with pool.Fori(1, B - 1) as b:
                sequence(b, False, False)
            sequence(B - 1, False, True)

            experts(1)

        @block.scalar
        def _(act):
            act.dma_start(wi, W_in[0:6 * P].rearrange("(k p) d -> p k d", p=P)).then_inc(s["ld_w"], 16)
            act.dma_start(wid[:], W_in[6 * P:6 * P + H]).then_inc(s["ld_w"], 16)
            act.dma_start(cw[:], conv_w.rearrange("(k p) w -> p k w", p=P)).then_inc(s["ld_w"], 16)
            act.dma_start(cols[2 * NX + 2:], conv_b.rearrange("(k p) -> k p", p=P)).then_inc(s["ld_w"], 16)
            act.dma_start(wos[:], W_out).then_inc(s["ld_w"], 16)
            act.dma_start(cols[2 * NX:2 * NX + 2], norm_w.rearrange("(k p) -> k p", p=P)).then_inc(s["ld_w"], 16)
            act.dma_start(w1s[:, NE, :], sw1[0]).then_inc(s["ld_w"], 16)
            act.dma_start(w1s[:, 0:NE, :], rw1.rearrange("e d f -> d e f")).then_inc(s["ld_w"], 16)
            act.dma_start(w2s[:, NE, :], sw2[0]).then_inc(s["ld_w"], 16)
            act.dma_start(w2s[:, 0:NE, :], rw2.rearrange("e f d -> f e d")).then_inc(s["ld_w"], 16)
            act.dma_start(cols[2 * NE:2 * NX], sb1.rearrange("e (k f) -> (e k) f", f=F)).then_inc(s["ld_w"], 16)
            act.dma_start(cols[0:2 * NE], rb1.rearrange("e (k f) -> (e k) f", f=F)).then_inc(s["ld_w"], 16)
            act.dma_start(b2[0:NE, :], rb2).then_inc(s["ld_w"], 16)
            act.dma_start(b2[NE:NX, :], sb2).then_inc(s["ld_w"], 16)
            act.dma_start(gws[:], gate_w).then_inc(s["ld_w"], 16)
            act.wait_ge(s["su_bcs"], 1)
            act.activation(negA[:], bc[:, R_AL:R_AL + H], ACT.Exp).then_inc(s["su_fin"], 1)

            def rows_hi(b, k, banks=(0, 1)):
                for h in range(2):
                    act.wait_ge(s[k + "_tr"], b * 2 + h + 1)
                    act.activation(kh[:, h * 512:(h + 1) * 512], PS[:, banks[h], :], ACT.Copy).then_inc(s[k + "_kh"], 1)

            def rows_full(b, k, banks=(0, 1)):
                for h in range(2):
                    act.activation(xTf[:, h * 512:(h + 1) * 512], PS[:, banks[h], :], ACT.Copy).then_inc(s[k + "_xf"], 1)

            def queries(b):
                for h in range(2):
                    act.wait_ge(s["a_qp"], b * 2 + h + 1)
                    act.activation(qh[:, h * 512:(h + 1) * 512], PS[:, 2 + h, :], ACT.Copy).then_inc(s["a_qh"], 1)

            def values(b):
                for h in range(2):
                    act.wait_ge(s["a_vp"], b * 2 + h + 1)
                    act.activation(vf[:, 4 * h:4 * h + 4, :], PS[:, 4 + h, :].rearrange("p (t d) -> p t d", t=4),
                                   ACT.Copy).then_inc(s["a_vf"], 1)

            def exps(b, t):
                act.wait_ge(s["a_nb"], b * T + t + 1)
                reached(act, s["a_pt"], b * T + t - 1)
                reached(act, s["a_cl"], b * 2 - 1 + (t >= 4))
                act.activation(Pr[:, t % 2, :], PS[:, 2 * (t % 2):2 * (t % 2) + 2, :], ACT.Exp,
                               bias=nbias[:, t:t + 1], accum_out=lsum[:, t:t + 1]).then_inc(s["a_ex"], 1)

            def attend(b, last):
                for t in range(T):
                    if t + 1 < T:
                        exps(b, t + 1)
                    act.wait_ge(s["a_pt"], b * T + t + 1)
                    reached(act, s["a_pv"], b * T + t - 1)
                    act.activation(PT[:, t % 2, :], PS[:, 4:6, :].rearrange("p a n -> p (a n)"),
                                   ACT.Copy).then_inc(s["a_ptc"], 1)
                    if t == T - 2 and not last:
                        rows_hi(b + 1, "a")
                        rows_full(b + 1, "a")
                if not last:
                    queries(b + 1)
                    values(b + 1)
                    exps(b + 1, 0)

            rows_hi(0, "a")
            rows_full(0, "a")
            queries(0)
            values(0)
            exps(0, 0)
            attend(0, False)
            with act.Fori(1, B - 1) as b:
                attend(b, False)
            attend(B - 1, True)

            def experts(k):
                def rows(g):
                    act.wait_ge(s["f_nm%d" % k], g + 1)
                    reached(act, s["f_tr%d" % k], g)
                    for t in range(G4):
                        act.activation(fxn[:, t, :], X[:, g * G4 + t, :], ACT.Identity, bias=fnm[:, t:t + 1],
                                       scale=frs[:, t:t + 1]).then_inc(s["f_xn%d" % k], 1)

                def rows_t(g, par):
                    act.wait_ge(s["f_tr%d" % k], g + 1)
                    act.activation(fxh[:, par, :], PS[:, 6, :], ACT.Copy).then_inc(s["f_xh%d" % k], 1)
                    reached(act, s["f_gl%d" % k], g)
                    reached(act, s["f_xl%d" % k], g)
                    act.wait_ge(s["f_xh%d" % k], g + 1)
                    act.activation(fxf, PS[:, 6, :], ACT.Copy).then_inc(s["f_xf%d" % k], 1)

                def gate(g):
                    act.wait_ge(s["f_lg%d" % k], g * GN + 3)
                    act.activation(lg[:, 2], lg[:, 1], ACT.Tanh, scale=0.5).then_inc(s["f_th%d" % k], 1)

                def gate_t(g):
                    act.wait_ge(s["f_ct%d" % k], g + 1)
                    reached(act, s["f_o%d" % k], g * NX)
                    act.activation(cwT[:], PS[0:NX, 7, :].rearrange("e (t p) -> e t p", t=G4),
                                   ACT.Copy).then_inc(s["f_ctc%d" % k], 1)

                def silu(g, e, o):
                    act.wait_ge(s["f_h%d" % k], g * NX + e + 1)
                    reached(act, s["f_g%d" % k], g * NX + e - 1)
                    act.activation(sil[:, o, :], PS[:, 2 * o, :], ACT.Silu,
                                   bias=b1[:, e, 0:1]).then_inc(s["f_s%d" % k], 1)

                def weigh(g, e, par, o):
                    j = BY_ACT.index(e)
                    act.wait_ge(s["f_o%d" % k], g * NX + e + 1)
                    if e == BY_ACT[0]:
                        reached(act, s["f_xw%d" % k], g - 1)
                    if e == NX - 1:
                        m = act.activation(wsum[:, par, j, :], PS[:, 4 + o, :], ACT.Copy)
                    else:
                        for t in range(G4):
                            c = slice(t * P, (t + 1) * P)
                            m = act.activation(wsum[:, par, j, c], PS[:, 4 + o, c], ACT.Copy,
                                               scale=cwt[:, par, t, e:e + 1])
                    m.then_inc(s["f_xa%d" % k], 1)

                rows(0)
                rows_t(0, 0)
                gate(0)
                silu(0, 0, 0)

                def group(g, par, first, last):
                    for e in range(NX):
                        o = (par * NX + e) % 2
                        if e + 1 < NX:
                            silu(g, e + 1, 1 - o)
                        elif not last:
                            silu(g + 1, 0, 1 - o)
                        if e == 0 and not first:
                            weigh(g - 1, NX - 1, 1 - par, 1 - o)
                        if e - 1 in BY_ACT:
                            weigh(g, e - 1, par, 1 - o)
                        if e == 2:
                            gate_t(g)
                        if not last:
                            if e == 1:
                                rows(g + 1)
                            if e == 3:
                                rows_t(g + 1, 1 - par)
                            if e == 6:
                                gate(g + 1)
                    if last:
                        weigh(g, NX - 1, par, o)

                group(0, 0, True, False)
                group(1, 1, False, False)
                with act.Fori(1, NG // 2 - 1) as i:
                    group(2 * i, 0, False, False)
                    group(2 * i + 1, 1, False, False)
                group(NG - 2, 0, False, False)
                group(NG - 1, 1, False, True)

            experts(0)

            def rows_both(b, hf):
                h = slice(hf * HS, (hf + 1) * HS)
                act.wait_ge(s["m_tr"], b * 2 + hf + 1)
                act.activation(kh[:, h], PS[:, 1, :], ACT.Copy).then_inc(s["m_kh"], 1)
                act.activation(xTf[:, h], PS[:, 1, :], ACT.Copy).then_inc(s["m_xf"], 1)

            def softplus_exp(b, hf):
                act.wait_ge(s["m_sp"], (b * 2 + hf) * SPN + 2)
                act.activation(sp[:, 2], sp[:, 1], ACT.Exp).then_inc(s["m_ex1"], 1)

            def decays(b, hf):
                act.wait_ge(s["m_cs"], b * 2 + hf + 1)
                act.activation(dec[:, hf], PS[:, 4, 2 * P:2 * P + 3 * HT * H].rearrange("p (k c h) -> p k c h", k=3, c=HT),
                               ACT.Exp).then_inc(s["m_dec"], 1)

            def projected(b, hf, c):
                j = (b * 2 + hf) * HT + c
                act.wait_ge(s["m_px"], j + 1)
                act.activation(pj[:, c, PAD + hf * HS:PAD + (hf + 1) * HS], PS[:, 0, :],
                               ACT.Copy).then_inc(s["m_pj"], 1)
                act.activation(cv[:, hf, c, :], PS[:, 0, :], ACT.Copy, scale=cw[:, c, PAD:TAPS]).then_inc(s["m_t3"], 1)
                act.wait_ge(s["m_pz"], j + 1)
                act.activation(zs[:, hf, c, :], PS[:, 1, 0:DI], ACT.Copy).then_inc(s["m_zc"], 1)

            def silus(b, hf):
                q = b * 2 + hf
                for k in range(4):
                    act.wait_ge(s["m_cn"], 3 * (q * HT + k + 1))
                    act.activation(cv[:, hf, k, :], cv[:, hf, k, :], ACT.Silu,
                                   bias=cb[:, k:k + 1]).then_inc(s["m_cv"], 1)
                channels(q * HT, 0)
                act.wait_ge(s["m_zc"], (q + 1) * HT)
                act.activation(zs[:, hf], zs[:, hf], ACT.Silu).then_inc(s["m_cv"], 1)

            def turned(n):
                act.wait_ge(s["m_yt"], n + 1)
                act.activation(yT[:], PS[:, 7, 0:2 * P].rearrange("p (k n) -> p k n", k=2),
                               ACT.Copy).then_inc(s["m_ytc"], 1)

            def channels(n, c):
                act.wait_ge(s["m_bt"], n + 1)
                reached(act, s["m_ie"], n - 1)
                reached(act, s["m_st"], n - 1)
                act.activation(xb[:, c % 2, :], PS[:, 3, 0:3 * P], ACT.Copy).then_inc(s["m_xb"], 1)

            def square(n, t):
                act.wait_ge(s["m_y4"], n + 1)
                act.activation(yq[:], yb[:, 2, :], ACT.Square, accum_out=ysq[:, t:t + 1]).then_inc(s["m_sq"], 1)

            def sequence(b, first, last):
                for t in range(T):
                    hf, c = divmod(t, HT)
                    n = b * T + t
                    nb, nh = (b, 1) if hf == 0 else (b + 1, 0)
                    if c > 0:
                        channels(n, c)
                    act.wait_ge(s["m_L"], n + 1)
                    reached(act, s["m_mt"], n)
                    act.activation(Lx, PS[:, 2, :].rearrange("p (h t) -> p h t", h=H),
                                   ACT.Exp).then_inc(s["m_lx"], 1)
                    if c == 2 and not last:
                        rows_both(b + 1, hf)
                    if not (last and hf == 1):
                        if c == 1:
                            softplus_exp(nb, nh)
                        projected(nb, nh, c)
                    if not (first and t == 0):
                        square(n - 1, (t - 1) % T)
                        turned(n - 1)
                    if c == HT - 1 and not (last and hf == 1):
                        decays(nb, nh)
                        silus(nb, nh)
                if last:
                    square(b * T + T - 1, T - 1)
                    turned(b * T + T - 1)

            rows_both(0, 0)
            rows_both(0, 1)
            softplus_exp(0, 0)
            for c in range(HT):
                projected(0, 0, c)
            decays(0, 0)
            silus(0, 0)
            sequence(0, True, False)
            with act.Fori(1, B - 1) as b:
                sequence(b, False, False)
            sequence(B - 1, False, True)

            experts(1)

        @block.tensor
        def _(pe):
            pe.wait_ge(s["ld_s"], 16 * 8)
            pe.wait_ge(s["su_dve"], 1)
            pe.matmul(PS[:, 7, 0:NR], ones[0:1, :], row[:], start=True, stop=True).then_inc(s["su_bc"], 1)
            pe.wait_ge(s["ld_m"], 16)
            pe.wait_ge(s["ld_w"], 16 * N_W)
            for k in range(4):
                m = pe.transpose(PS[:, 0, k * P:(k + 1) * P], wi[:, 2 + k, :], ident)
            m.then_inc(s["su_tp"], 1)
            pe.transpose(PS[:, 2, 0:P], wi[:, 0, :], ident)
            pe.transpose(PS[:, 2, P:2 * P], wi[:, 1, :], ident)
            pe.transpose(PS[:, 2, 2 * P:2 * P + H], wid[:], ident[0:H, 0:H]).then_inc(s["su_tp"], 1)
            pe.transpose(PS[:, 3, 0:P], wos[:, 0:P], ident)
            pe.transpose(PS[:, 3, P:2 * P], wos[:, P:2 * P], ident)
            pe.transpose(PS[:, 3, 2 * P:2 * P + NC], cols[:], ident[0:NC, 0:NC]).then_inc(s["su_tp"], 1)

            pe.wait_ge(s["su_m"], 2)
            pe.wait_ge(s["su_tpc"], N_TPC)
            pe.wait_ge(s["su_bcs"], 1)
            def rows_t(b):
                for t in range(T):
                    pe.wait_ge(s["a_xn"], b * T + t + 1)
                    if t == 0:
                        reached(pe, s["a_ex"], b * T - 1)
                    m = pe.transpose(PS[:, t // 4, (t % 4) * P:(t % 4 + 1) * P], xn[:, t, :], ident)
                    if t % 4 == 3:
                        m.then_inc(s["a_tr"], 1)

            def queries(b):
                reached(pe, s["a_ex"], b * T)
                for h in range(2):
                    pe.wait_ge(s["a_kh"], b * 2 + h + 1)
                    pe.wait_ge(s["a_kl"], b * 2 + h + 1)
                    c = slice(h * 512, (h + 1) * 512)
                    mm3(pe, PS[:, 2 + h, :], Mh[:], Ml[:], kh[:, c], kl[:, c]).then_inc(s["a_qp"], 1)

            def values(b):
                pe.wait_ge(s["a_xf"], b * 2 + 2)
                reached(pe, s["a_ptc"], b * T)
                for t in range(T):
                    m = pe.matmul(PS[:, 4 + t // 4, (t % 4) * P:(t % 4 + 1) * P], xTf[:, t * P:(t + 1) * P],
                                  Mf[:, 1, :], start=True, stop=True)
                    if t % 4 == 3:
                        m.then_inc(s["a_vp"], 1)

            def scores(b, t):
                q = slice(t * P, (t + 1) * P)
                for h in range(2):
                    c = slice(h * 512, (h + 1) * 512)
                    m = mm3(pe, PS[:, 2 * (t % 2) + h, :], qh[:, q], ql[:, q], kh[:, c], kl[:, c])
                m.then_inc(s["a_S"], 1)

            def first_scores(b):
                pe.wait_ge(s["a_qh"], b * 2 + 2)
                pe.wait_ge(s["a_ql"], b * 2 + 2)
                scores(b, 0)
                values(b)
                scores(b, 1)

            def weigh(b, t):
                pe.wait_ge(s["a_ptc"], b * T + t + 1)
                reached(pe, s["a_oc"], b * T + t - 1)
                for k in range(T):
                    m = pe.matmul(PS[:, 6 + t % 2, 0:D], PT[:, t % 2, k * P:(k + 1) * P], vf[:, k, :],
                                  start=(k == 0), stop=(k == T - 1))
                m.then_inc(s["a_pv"], 1)

            def attend(b, last):
                for t in range(T):
                    pe.wait_ge(s["a_ex"], b * T + t + 1)
                    if t == 0:
                        pe.wait_ge(s["a_vf"], b * 2 + 2)
                    else:
                        pe.wait_ge(s["a_ptc"], b * T + t)
                    for k in range(T):
                        m = pe.transpose(PS[:, 4 + k // 4, (k % 4) * P:(k % 4 + 1) * P],
                                         Pr[:, t % 2, k * P:(k + 1) * P], ident)
                    m.then_inc(s["a_pt"], 1)
                    if t + 2 < T:
                        scores(b, t + 2)
                    elif t == T - 2 and not last:
                        rows_t(b + 1)
                    if t >= 1:
                        weigh(b, t - 1)
                if not last:
                    queries(b + 1)
                weigh(b, T - 1)
                if not last:
                    first_scores(b + 1)

            rows_t(0)
            queries(0)
            first_scores(0)
            attend(0, False)
            with pe.Fori(1, B - 1) as b:
                attend(b, False)
            attend(B - 1, True)

            def experts(k):
                def rows_t(g):
                    reached(pe, s["f_xf%d" % k], g)
                    for t in range(G4):
                        pe.wait_ge(s["f_xn%d" % k], g * G4 + t + 1)
                        m = pe.transpose(PS[:, 6, t * P:(t + 1) * P], fxn[:, t, :], ident)
                    m.then_inc(s["f_tr%d" % k], 1)

                def gate(g):
                    pe.wait_ge(s["f_xf%d" % k], g + 1)
                    reached(pe, s["f_ctc%d" % k], g)
                    for t in range(G4):
                        m = pe.matmul(PS[:, 7, t * NE:(t + 1) * NE], fxf[:, t * P:(t + 1) * P], gws[:],
                                      start=True, stop=True)
                    m.then_inc(s["f_gl%d" % k], 1)

                def gate_t(g, par):
                    pe.wait_ge(s["f_cw%d" % k], g + 1)
                    for t in range(G4):
                        m = pe.transpose(PS[0:NX, 7, t * P:(t + 1) * P], cwt[:, par, t, :], ident)
                    m.then_inc(s["f_ct%d" % k], 1)

                def hidden(g, e, par, o):
                    reached(pe, s["f_g%d" % k], g * NX + e - 1)
                    if e == 0:
                        pe.wait_ge(s["f_xh%d" % k], g + 1)
                        pe.wait_ge(s["f_xl%d" % k], g + 1)
                    for j in range(2):
                        w = slice(j * F, (j + 1) * F)
                        m = mm3(pe, PS[:, 2 * o + j, :], w1h[:, e, w], w1l[:, e, w], fxh[:, par, :], fxl[:, par, :])
                    m.then_inc(s["f_h%d" % k], 1)

                def output(g, e, o):
                    pe.wait_ge(s["f_g%d" % k], g * NX + e + 1)
                    output_read(pe, k, g, e - 2)
                    if e == NX - 1:
                        pe.wait_ge(s["f_ctc%d" % k], g + 1)
                    for t in range(G4):
                        c = slice(t * P, (t + 1) * P)
                        if e == NX - 1:
                            pe.matmul(PS[:, 4 + o, c], cwT[:, t, :], b2[:], start=True, stop=False)
                        m = pe.matmul(PS[:, 4 + o, c], gf[:, o, c], w2s[:, e, :], start=(e != NX - 1), stop=True)
                    m.then_inc(s["f_o%d" % k], 1)

                if k == 0:
                    pe.wait_ge(s["su_w"], 2)
                    pe.wait_ge(s["a_x"], 2 * B)
                else:
                    pe.wait_ge(s["m_x"], NT)
                rows_t(0)
                gate(0)
                hidden(0, 0, 0, 0)

                def group(g, par, last):
                    for e in range(NX):
                        o = (par * NX + e) % 2
                        if e + 1 < NX:
                            hidden(g, e + 1, par, 1 - o)
                        elif not last:
                            hidden(g + 1, 0, 1 - par, 1 - o)
                        output(g, e, o)
                        if e == 2:
                            gate_t(g, par)
                        if not last:
                            if e == 2:
                                rows_t(g + 1)
                            if e == 4:
                                gate(g + 1)

                group(0, 0, False)
                group(1, 1, False)
                with pe.Fori(1, NG // 2 - 1) as i:
                    group(2 * i, 0, False)
                    group(2 * i + 1, 1, False)
                group(NG - 2, 0, False)
                group(NG - 1, 1, True)

            experts(0)

            pe.wait_ge(s["f_x0"], NG * NV)
            pe.wait_ge(s["f_xa0"], NG * NA)
            pe.wait_ge(s["f_xw0"], NG)
            def rows_t2(b, hf):
                q = b * 2 + hf
                pe.wait_ge(s["m_xn"], (q + 1) * HT)
                reached(pe, s["m_xf"], q)
                if not (isinstance(q, int) and q < 2):
                    pe.wait_ge(s["m_zc"], (q - 1) * HT + 2)
                for t in range(HT):
                    m = pe.transpose(PS[:, 1, t * P:(t + 1) * P], xn[:, hf * HT + t, :], ident)
                m.then_inc(s["m_tr"], 1)

            def steps(b, hf):
                q = b * 2 + hf
                pe.wait_ge(s["m_xf"], q + 1)
                reached(pe, s["m_gm"], (q - 1) * HT + 1)
                for c in range(HT):
                    x0 = (hf * HT + c) * P
                    m = pe.matmul(PS[:, 4, P + c * H:P + (c + 1) * H], xTf[:, x0:x0 + P], wdt[:],
                                  start=True, stop=True)
                m.then_inc(s["m_dp"], 1)

            def sums(b, hf):
                q = b * 2 + hf
                pe.wait_ge(s["m_dt"], q * 2 + 2)
                reached(pe, s["m_gm"], q * HT)
                a_all = av[:, hf].rearrange("p c h -> p (c h)")
                for j, w in enumerate((upto, after, ones[:])):
                    m = pe.matmul(PS[:, 4, 2 * P + j * HT * H:2 * P + (j + 1) * HT * H], w, a_all, start=True, stop=True)
                m.then_inc(s["m_cs"], 1)

            def project(b, hf, c):
                q = b * 2 + hf
                j = q * HT + c
                if c == 0:
                    pe.wait_ge(s["m_kl"], q + 1)
                    pe.wait_ge(s["m_kh"], q + 1)
                reached(pe, s["m_t3"], j)
                h, w = slice(hf * HS, (hf + 1) * HS), slice(c * P, (c + 1) * P)
                mm3(pe, PS[:, 0, :], wxh[:, w], wxl[:, w], kh[:, h], kl[:, h]).then_inc(s["m_px"], 1)
                reached(pe, s["m_zc"], j)
                if c == (0 if isinstance(q, int) and q == 0 else 2):
                    pe.wait_ge(s["m_xf"], min(q + 2, 2 * B) if isinstance(q, int) else q + 2)
                x0 = hf * HS + c * P
                mm3(pe, PS[:, 1, 0:DI], kh[:, x0:x0 + P], kl[:, x0:x0 + P], wzh[:], wzl[:]).then_inc(s["m_pz"], 1)

            def turn(n):
                pe.wait_ge(s["m_y4"], n + 1)
                pe.transpose(PS[:, 7, 0:P], yb[:, 2, 0:P], ident)
                pe.transpose(PS[:, 7, P:2 * P], yb[:, 2, P:2 * P], ident).then_inc(s["m_yt"], 1)

            def leave(n):
                pe.wait_ge(s["m_ytc"], n + 1)
                pe.matmul(PS[:, 7, 0:D], yT[:, 0, :], woT[:, 0, :], start=True, stop=False)
                pe.matmul(PS[:, 7, 0:D], yT[:, 1, :], woT[:, 1, :], start=False, stop=True).then_inc(s["m_o"], 1)

            def front(b, hf, c):
                q = b * 2 + hf
                n = q * HT + c
                pe.wait_ge(s["m_U"], n * 2 + 2)
                reached(pe, s["m_lx"], n)
                pe.matmul(PS[:, 2, :], after_r[:], Uh[:, c % 2], start=True, stop=False)
                pe.matmul(PS[:, 2, :], after_r[:], Ul[:, c % 2], start=False, stop=True).then_inc(s["m_L"], 1)
                if c == 0:
                    pe.wait_ge(s["m_cv"], q * 5 + 3)
                reached(pe, s["m_xb"], n)
                for m in range(3):
                    p = pe.transpose(PS[:, 3, m * P:(m + 1) * P], cv[:, hf, m, c * P:(c + 1) * P], ident)
                p.then_inc(s["m_bt"], 1)

            def sequence(b, first, last):
                for t in range(T):
                    hf, c = divmod(t, HT)
                    q, n = b * 2 + hf, b * T + t
                    nb, nh = (b, 1) if hf == 0 else (b + 1, 0)
                    more = not (last and hf == 1)
                    k = slice(c * P, (c + 1) * P)
                    if c == 0:
                        pe.wait_ge(s["m_cv"], q * 5 + 4)
                        pe.wait_ge(s["m_dec"], q + 1)
                    if c == 1 and more:
                        pe.wait_ge(s["m_sp"], (q + 1) * SPN + 1)
                    reached(pe, s["m_gm"], n)
                    pe.matmul(PS[:, 4, 0:P], cv[:, hf, 2, k], cv[:, hf, 3, k], start=True, stop=True).then_inc(s["m_G"], 1)
                    if t == 0:
                        pe.wait_ge(s["m_h0"], b + 1)
                    reached(pe, s["m_h"], n)
                    pe.matmul(PS[:, 6, 0:DI], cv[:, hf, 3, k], hst[:, c % 2].rearrange("p h e -> p (h e)"),
                              start=True, stop=True).then_inc(s["m_in"], 1)
                    if c == 2 and not last:
                        rows_t2(b + 1, hf)
                    if more:
                        project(nb, nh, c)
                        if c == 0:
                            steps(nb, nh)
                    if c < HT - 1:
                        front(b, hf, c + 1)
                    pe.wait_ge(s["m_xw"], n + 1)
                    pe.wait_ge(s["m_xb"], n + 1)
                    pe.wait_ge(s["m_y1"], n + 1)
                    pe.matmul(PS[:, 6, DI:2 * DI], xb[:, c % 2, DI:DI + P], xw[:, c % 2].rearrange("p h e -> p (h e)"),
                              start=True, stop=True).then_inc(s["m_st"], 1)
                    if not (first and t == 0):
                        reached(pe, s["m_x"], n - 1)
                        turn(n - 1)
                    if c == HT - 1 and more:
                        sums(nb, nh)
                    reached(pe, s["m_y2"], n)
                    pe.wait_ge(s["m_mt"], n + 1)
                    pe.wait_ge(s["m_xdt"], n + 1)
                    for h in range(H):
                        e = slice(h * HD, (h + 1) * HD)
                        pe.matmul(PS[:, 5, e], Ddiag[:, h, :], xb[:, c % 2, e], start=True, stop=False)
                        m = pe.matmul(PS[:, 5, e], MT[:, h, :], xdt[:, c % 2, h, :], start=False, stop=True)
                    m.then_inc(s["m_ie"], 1)
                    if not (first and t == 0):
                        leave(n - 1)
                    if c == HT - 1 and more:
                        front(nb, nh, 0)
                if last:
                    n = b * T + T - 1
                    pe.wait_ge(s["m_x"], n)
                    turn(n)
                    leave(n)

            rows_t2(0, 0)
            rows_t2(0, 1)
            steps(0, 0)
            for c in range(HT):
                project(0, 0, c)
            sums(0, 0)
            front(0, 0, 0)
            sequence(0, True, False)
            with pe.Fori(1, B - 1) as b:
                sequence(b, False, False)
            sequence(B - 1, False, True)

            experts(1)

        @block.vector
        def _(dve):
            def norm_rows(b, k):
                for t in range(T):
                    dve.bn_stats(stats[:, t, :], X[:, b * T + t, :]).then_inc(s[k + "_bn"], 1)
                dve.wait_ge(s[k + "_bn"], b * (T + 1) + T)
                dve.memset(turn[:], 0.0).then_inc(s[k + "_bn"], 1)
                for t in range(T):
                    dve.bn_aggr(mv[:, t, :], stats[:, t, :]).then_inc(s[k + "_ag"], 1)
                dve.wait_ge(s[k + "_ag"], b * T + T)
                dve.tensor_scalar(ve[:], mv[:, :, 1], EPS, None, ALU.add).then_inc(s[k + "_ve"], 1)

            dve.wait_ge(s["su_bc"], 1)
            dve.tensor_copy(bc[:], PS[:, 7, 0:NR]).then_inc(s["su_bcs"], 1)
            chain = [0]

            def link(ins):
                chain[0] += 1
                ins.then_inc(s["su_rot"], 1)
                dve.wait_ge(s["su_rot"], chain[0])

            dve.wait_ge(s["su_bcs"], 1)
            dve.wait_ge(s["ld_s"], 16 * 8)
            dve.wait_ge(s["ld_m"], 16)
            link(dve.reciprocal(s2[:, 1:2], bc[:, R_SC:R_SC + 1]))
            link(dve.tensor_scalar(s2[:, 0:1], s2[:, 1:2], 2.0, None, ALU.mult))
            link(dve.tensor_scalar(s2[:, 1:2], s2[:, 0:1], bc[:, R_BI:R_BI + 1], None, ALU.add))
            link(dve.tensor_tensor(rn[:, 0, :], rr[:, :, 0], rr[:, :, 0], ALU.mult))
            link(dve.tensor_tensor(rn[:, 1, :], rr[:, :, 1], rr[:, :, 1], ALU.mult))
            dve.tensor_tensor(rn[:, 2, :], rn[:, 0, :], rn[:, 1, :], ALU.add).then_inc(s["su_n2"], 1)
            dve.wait_ge(s["su_mf"], 1)
            cs, sn = rn[:, 4, :], rn[:, 5, :]
            link(dve.tensor_tensor(cs, rr[:, :, 0], rn[:, 3, :], ALU.mult))
            link(dve.tensor_tensor(sn, rr[:, :, 1], rn[:, 3, :], ALU.mult))
            link(dve.tensor_tensor(rn[:, 6, 0:1], sn[:, 0:1], sn[:, 1:2], ALU.mult))
            link(dve.tensor_tensor(rn[:, 6, 1:2], cs[:, 0:1], sn[:, 1:2], ALU.mult))
            link(dve.scalar_tensor_tensor(rn[:, 7, 0:1], cs[:, 0:1], cs[:, 1:2], rn[:, 6, 0:1], ALU.mult, ALU.add))
            link(dve.scalar_tensor_tensor(rn[:, 7, 1:2], sn[:, 0:1], cs[:, 1:2], rn[:, 6, 1:2], ALU.mult, ALU.subtract))
            link(dve.tensor_scalar(rn[:, 7, 0:2], rn[:, 7, 0:2], s2[:, 0:1], None, ALU.mult))
            for j, (c1, s1) in enumerate(((rn[:, 7, 0:1], rn[:, 7, 1:2]), (cs[:, 2:3], sn[:, 2:3]))):
                link(dve.tensor_scalar(Mt[:, j, :], ident, c1, None, ALU.mult))
                link(dve.scalar_tensor_tensor(Mf[:, j, :], swap, s1, Mt[:, j, :], ALU.mult, ALU.add))
            dve.tensor_copy(Mh[:], Mf[:, 0, :]).then_inc(s["su_m"], 1)
            dve.wait_ge(s["su_m"], 1)
            dve.tensor_tensor(Ml[:], Mf[:, 0, :], fp(Mh[:]), ALU.subtract).then_inc(s["su_m"], 1)
            dve.tensor_copy(after_r[:], after).then_inc(s["su_rot"], 1)
            chain[0] += 1
            dve.wait_ge(s["su_fin"], 1)
            link(dve.tensor_scalar(negA[:], negA[:], -1.0, None, ALU.mult))
            dve.wait_ge(s["su_dve"], N_DVE)
            dve.wait_ge(s["ld_x"], 16)
            norm_rows(0, "a")
            for k, (hi, lo, w) in enumerate(((wxh, wxl, CC), (wzh, wzl, DI))):
                dve.wait_ge(s["su_tp"], k + 1)
                src = PS[:, 2 * k, 0:w]
                dve.tensor_copy(hi[:], src).then_inc(s["su_tpc"], 1)
                dve.wait_ge(s["su_tpc"], 2 * k + 1)
                dve.tensor_tensor(lo[:], src, fp(hi[:]), ALU.subtract).then_inc(s["su_tpc"], 1)
            dve.tensor_copy(wdt[:], PS[:, 2, DI:DI + H]).then_inc(s["su_tpc"], 1)
            dve.wait_ge(s["su_tp"], 3)
            dve.tensor_copy(b1n[:], PS[:, 3, 2 * P:2 * P + NC]).then_inc(s["su_tpc"], 1)
            dve.wait_ge(s["su_tpc"], 6)
            for j in range(2):
                dve.tensor_scalar(woT[:, j, :], PS[:, 3, j * P:(j + 1) * P], nw[:, j:j + 1], None,
                                  ALU.mult).then_inc(s["su_tpc"], 1)

            def norm_rows_2(b, hf):
                dve.wait_ge(s["a_rs"], b + 1)
                reached(dve, s["a_tr"], b * 2)
                for t in range(4 * hf, 4 * hf + 4):
                    dve.tensor_scalar(xn[:, t, :], X[:, b * T + t, :], mv[:, t, 0:1], rstd[:, t:t + 1],
                                      ALU.subtract, ALU.mult).then_inc(s["a_xn"], 1)

            def rows_lo(b, k):
                for h in range(2):
                    c = slice(h * 512, (h + 1) * 512)
                    dve.wait_ge(s[k + "_kh"], b * 2 + h + 1)
                    dve.wait_ge(s[k + "_xf"], b * 2 + h + 1)
                    dve.tensor_tensor(kl[:, c], xTf[:, c], fp(kh[:, c]), ALU.subtract).then_inc(s[k + "_kl"], 1)

            def queries_lo(b):
                for h in range(2):
                    c = slice(h * 512, (h + 1) * 512)
                    dve.wait_ge(s["a_qh"], b * 2 + h + 1)
                    dve.tensor_tensor(ql[:, c], PS[:, 2 + h, :], fp(qh[:, c]), ALU.subtract).then_inc(s["a_ql"], 1)

            def row_max(b, t):
                dve.wait_ge(s["a_S"], b * T + t + 1)
                dve.tensor_reduce(nmx[:, t:t + 1], PS[:, 2 * (t % 2):2 * (t % 2) + 2, :], AX.XY, ALU.max,
                                  negate=True).then_inc(s["a_nm"], 1)
                dve.wait_ge(s["a_nm"], b * T + t + 1)
                dve.tensor_scalar(nbias[:, t:t + 1], nmx[:, t:t + 1], s2[:, 1:2], s2[:, 1:2],
                                  ALU.subtract, ALU.add).then_inc(s["a_nb"], 1)

            def o_copy(b, t):
                dve.wait_ge(s["a_pv"], b * T + t + 1)
                reached(dve, s["a_x"], b * 2 - 1 + (t >= 4))
                dve.tensor_copy(Osb[:, t, :], PS[:, 6 + t % 2, 0:D]).then_inc(s["a_oc"], 1)
                dve.wait_ge(s["a_oc"], b * T + t + 1)
                reached(dve, s["a_ss"], b * T + t)
                dve.tensor_tensor_reduce(osq[:], Osb[:, t, :], Osb[:, t, :], 1.0, 0.0, ALU.mult, ALU.add,
                                         nrm[:, 0, t:t + 1]).then_inc(s["a_ss"], 1)

            def norm_1(b, hf):
                h = slice(4 * hf, 4 * hf + 4)
                n = b * 6 + 3 * hf
                dve.reciprocal(nrm[:, 1, h], lsum[:, h]).then_inc(s["a_nc"], 1)
                dve.wait_ge(s["a_nc"], n + 1)
                dve.wait_ge(s["a_ss"], b * T + 4 * hf + 4)
                dve.tensor_tensor(nrm[:, 2, h], nrm[:, 0, h], nrm[:, 1, h], ALU.mult).then_inc(s["a_nc"], 1)
                dve.wait_ge(s["a_nc"], n + 2)
                dve.tensor_tensor(nrm[:, 2, h], nrm[:, 2, h], nrm[:, 1, h], ALU.mult).then_inc(s["a_nc"], 1)
                dve.wait_ge(s["a_nc"], n + 3)
                dve.tensor_scalar(nrm[:, 3, h], nrm[:, 2, h], SMALL, None, ALU.max).then_inc(s["a_cl"], 1)

            def norm_2(b, hf):
                h = slice(4 * hf, 4 * hf + 4)
                dve.wait_ge(s["a_pw"], b * 2 + hf + 1)
                dve.tensor_tensor(nrm[:, 5, h], nrm[:, 4, h], nrm[:, 1, h], ALU.mult).then_inc(s["a_fc"], 1)
                dve.wait_ge(s["a_fc"], b * 2 + hf + 1)
                for t in range(4 * hf, 4 * hf + 4):
                    xt = X[:, b * T + t, :]
                    m = dve.scalar_tensor_tensor(xt, Osb[:, t, :], nrm[:, 5, t:t + 1], xt, ALU.mult, ALU.add)
                m.then_inc(s["a_x"], 1)

            def attend(b, first, last):
                for t in range(T):
                    if t + 2 < T:
                        row_max(b, t + 2)
                    if t == T - 1 and not last:
                        rows_lo(b + 1, "a")
                    if t >= 1:
                        o_copy(b, t - 1)
                    if t == 1 and not first:
                        norm_2(b - 1, 1)
                    if t == 2 and not last:
                        dve.wait_ge(s["ld_x"], 16 * (b + 2))
                        norm_rows(b + 1, "a")
                    if t in (3, 4) and not last:
                        norm_rows_2(b + 1, t - 3)
                    if t == 5:
                        norm_1(b, 0)
                    if t == 6:
                        norm_2(b, 0)
                if not last:
                    queries_lo(b + 1)
                o_copy(b, T - 1)
                if not last:
                    row_max(b + 1, 0)
                norm_1(b, 1)
                if not last:
                    row_max(b + 1, 1)

            norm_rows_2(0, 0)
            norm_rows_2(0, 1)
            dve.tensor_tensor(Ddiag[:], ident.unsqueeze(1).broadcast_to([P, H, P]),
                              bc[:, R_D:R_D + H].unsqueeze(2).broadcast_to([P, H, P]), ALU.mult).then_inc(s["su_rot"], 1)
            chain[0] += 1
            rows_lo(0, "a")
            queries_lo(0)
            row_max(0, 0)
            row_max(0, 1)
            attend(0, True, False)
            with dve.Fori(1, B - 1) as b:
                attend(b, False, False)
            attend(B - 1, False, True)
            norm_2(B - 1, 1)

            def experts(k):
                def rows(g, gate_g=None, par=0, n=0):
                    if isinstance(g, int) and g == 0:
                        dve.wait_ge(s["a_x"], 2 * B) if k == 0 else dve.wait_ge(s["m_x"], NT)
                    for t in range(G4):
                        dve.bn_stats(fst[:, t, :], X[:, g * G4 + t, :]).then_inc(s["f_bn%d" % k], 1)
                        if gate_g is not None:
                            gate(gate_g, par, n + t, n + t + 1)
                    reached(dve, s["f_xn%d" % k], g * G4)
                    dve.wait_ge(s["f_bn%d" % k], g * (G4 + 1) + G4)
                    dve.memset(turn[:], 0.0).then_inc(s["f_bn%d" % k], 1)
                    for t in range(G4):
                        dve.bn_aggr(fmv[:, t, :], fst[:, t, :]).then_inc(s["f_ag%d" % k], 1)

                def rows_2(g):
                    dve.wait_ge(s["f_ag%d" % k], (g + 1) * G4)
                    dve.tensor_scalar(fve[:], fmv[:, :, 1], EPS, None, ALU.add).then_inc(s["f_ve%d" % k], 1)

                def rows_3(g):
                    dve.wait_ge(s["f_rs%d" % k], g + 1)
                    dve.scalar_tensor_tensor(fnm[:], fmv[:, :, 0], -1.0, frs[:], ALU.mult,
                                             ALU.mult).then_inc(s["f_nm%d" % k], 1)

                def gate(g, par, n, upto_n):
                    def each(v):
                        return v.unsqueeze(2).broadcast_to([P, G4, NE])

                    for n in range(n, upto_n):
                        reached(dve, s["f_lg%d" % k], g * GN + n)
                        if n == 0:
                            dve.wait_ge(s["f_gl%d" % k], g + 1)
                            m = dve.tensor_tensor(lg[:, 0], PS[:, 7, 0:G4 * NE].rearrange("p (t e) -> p t e", t=G4),
                                                  bc[:, R_GB:R_GB + NE].unsqueeze(1).broadcast_to([P, G4, NE]), ALU.add)
                        elif n == 1:
                            m = dve.tensor_reduce(g1[:, 0, :], lg[:, 0], AX.X, ALU.max)
                        elif n == 2:
                            m = dve.tensor_tensor(lg[:, 1], lg[:, 0], each(g1[:, 0, :]), ALU.subtract)
                        elif n == 3:
                            m = dve.scalar_tensor_tensor(lg[:, 3], lg[:, 1], 0.0, rank[:], ALU.is_ge, ALU.mult)
                        elif n == 4:
                            m = dve.tensor_reduce(g1[:, 1, :], lg[:, 3], AX.X, ALU.max)
                        elif n == 5:
                            m = dve.tensor_tensor(lg[:, 4], lg[:, 3], each(g1[:, 1, :]), ALU.is_equal)
                        elif n == 6:
                            m = dve.scalar_tensor_tensor(lg[:, 5], lg[:, 4], -BIG, lg[:, 1], ALU.mult, ALU.add)
                        elif n == 7:
                            m = dve.tensor_reduce(g1[:, 2, :], lg[:, 5], AX.X, ALU.max)
                        elif n == 8:
                            m = dve.tensor_tensor(lg[:, 6], lg[:, 5], each(g1[:, 2, :]), ALU.is_ge)
                        elif n == 9:
                            m = dve.tensor_tensor(lg[:, 7], lg[:, 6], rank[:], ALU.mult)
                        elif n == 10:
                            m = dve.tensor_reduce(g1[:, 3, :], lg[:, 7], AX.X, ALU.max)
                        elif n == 11:
                            m = dve.tensor_tensor(lg[:, 8], lg[:, 7], each(g1[:, 3, :]), ALU.is_equal)
                        elif n == 12:
                            m = dve.tensor_tensor(lg[:, 9], lg[:, 8], lg[:, 4], ALU.add)
                        elif n == 13:
                            dve.wait_ge(s["f_th%d" % k], g + 1)
                            m = dve.tensor_scalar(lg[:, 10], lg[:, 2], -1.0, 1.0, ALU.mult, ALU.add)
                        elif n == 14:
                            m = dve.reciprocal(lg[:, 11], lg[:, 10])
                        elif n == 15:
                            m = dve.scalar_tensor_tensor(lg[:, 10], lg[:, 2], 1.0, lg[:, 11], ALU.add, ALU.mult)
                        elif n == 16:
                            m = dve.tensor_reduce(g1[:, 4, :], lg[:, 10], AX.X, ALU.add)
                        elif n == 17:
                            m = dve.reciprocal(g1[:, 5, :], g1[:, 4, :])
                        elif n == 18:
                            m = dve.tensor_tensor(lg[:, 11], lg[:, 10], lg[:, 9], ALU.mult)
                        else:
                            m = dve.tensor_tensor(cwt[:, par, :, 0:NE], lg[:, 11], each(g1[:, 5, :]), ALU.mult)
                        m.then_inc(s["f_lg%d" % k] if n < GN else s["f_cw%d" % k], 1)

                def multiply(g, e, o):
                    dve.wait_ge(s["f_s%d" % k], g * NX + e + 1)
                    reached(dve, s["f_o%d" % k], g * NX + e - 1)
                    dve.scalar_tensor_tensor(gf[:, o, :], PS[:, 2 * o + 1, :], b1[:, e, 1:2], sil[:, o, :],
                                             ALU.add, ALU.mult).then_inc(s["f_g%d" % k], 1)

                def add(g, e, par, o, n=None):
                    dve.wait_ge(s["f_o%d" % k], g * NX + e + 1)
                    dve.wait_ge(s["f_cw%d" % k], g + 1)
                    reached(dve, s["f_x%d" % k], g * NV + BY_DVE.index(e))
                    for t in range(G4):
                        xt = X[:, g * G4 + t, :]
                        m = dve.scalar_tensor_tensor(xt, PS[:, 4 + o, t * P:(t + 1) * P],
                                                     cwt[:, par, t, e:e + 1], xt, ALU.mult, ALU.add)
                        if t == G4 - 1:
                            m.then_inc(s["f_x%d" % k], 1)
                        if n is not None:
                            gate(g + 1, 1 - par, n + t, n + t + 1)

                def add_weighed(g, par):
                    dve.wait_ge(s["f_as%d" % k], (g + 1) * (NA - 1))
                    dve.wait_ge(s["f_x%d" % k], (g + 1) * NV)
                    xg = X[:, bass.ds(g * G4, G4), :]
                    dve.tensor_tensor(xg, wsum[:, par, 0, :].rearrange("p (t d) -> p t d", t=G4), xg,
                                      ALU.add).then_inc(s["f_xw%d" % k], 1)

                rows(0)
                rows_2(0)
                rows_3(0)
                rows(1)
                gate(0, 0, 0, GN + 1)

                def group(g, par, first, late, last):
                    for e in range(NX):
                        o = (par * NX + e) % 2
                        multiply(g, e, o)
                        if e == 0 and not last:
                            rows_2(g + 1)
                        if e == 0 and not first:
                            gate(g, par, 17, GN + 1)
                        if e == 1 and not last:
                            rows_3(g + 1)
                        if e - 1 in BY_DVE:
                            add(g, e - 1, par, 1 - o, {5: 0, 7: 9}.get(e) if not last else None)
                        if e == 2 and not first:
                            add_weighed(g - 1, 1 - par)
                        if e == 6 and not last:
                            gate(g + 1, 1 - par, 4, 9)
                        if e == 8 and not last:
                            if late:
                                gate(g + 1, 1 - par, 13, 17)
                            else:
                                rows(g + 2, g + 1, 1 - par, 13)
                    if last:
                        add_weighed(g, par)

                group(0, 0, True, False, False)
                group(1, 1, False, False, False)
                with dve.Fori(1, NG // 2 - 1) as i:
                    group(2 * i, 0, False, False, False)
                    group(2 * i + 1, 1, False, False, False)
                group(NG - 2, 0, False, True, False)
                group(NG - 1, 1, False, True, True)

            experts(0)

            def norm_half(b, hf):
                q = b * 2 + hf
                for t in range(hf * HT, (hf + 1) * HT):
                    dve.bn_stats(stats[:, t, :], X[:, b * T + t, :]).then_inc(s["m_bn"], 1)
                dve.wait_ge(s["m_bn"], q * (HT + 1) + HT)
                dve.memset(turn[:], 0.0).then_inc(s["m_bn"], 1)
                for t in range(hf * HT, (hf + 1) * HT):
                    dve.bn_aggr(mv[:, t, :], stats[:, t, :]).then_inc(s["m_ag"], 1)
                h = slice(hf * HT, (hf + 1) * HT)
                dve.wait_ge(s["m_ag"], (q + 1) * HT)
                dve.tensor_scalar(ve[:, h], mv[:, h, 1], EPS, None, ALU.add).then_inc(s["m_ve"], 1)

            def norm_half_2(b, hf, between):
                q = b * 2 + hf
                dve.wait_ge(s["m_rs"], q + 1)
                reached(dve, s["m_tr"], q - 1)
                for t in range(hf * HT, (hf + 1) * HT):
                    dve.tensor_scalar(xn[:, t, :], X[:, b * T + t, :], mv[:, t, 0:1], rstd[:, t:t + 1],
                                      ALU.subtract, ALU.mult).then_inc(s["m_xn"], 1)
                    if between is not None:
                        n = between[2] + t - hf * HT
                        softplus(between[0], between[1], n, n + 1)

            def rows_lo_half(b, hf):
                q = b * 2 + hf
                h = slice(hf * HS, (hf + 1) * HS)
                dve.wait_ge(s["m_xf"], q + 1)
                dve.wait_ge(s["m_kh"], q + 1)
                dve.tensor_tensor(kl[:, h], xTf[:, h], fp(kh[:, h]), ALU.subtract).then_inc(s["m_kl"], 1)

            def softplus(b, hf, first, end):
                q = b * 2 + hf
                for n in range(first, end):
                    if n <= SPN:
                        reached(dve, s["m_sp"], q * SPN + n)
                    if n == 0:
                        dve.wait_ge(s["m_dp"], q + 1)
                        m = dve.tensor_tensor(sp[:, 0], PS[:, 4, P:P + HT * H].rearrange("p (c h) -> p c h", c=HT),
                                              bc[:, R_DB:R_DB + H].unsqueeze(1).broadcast_to([P, HT, H]), ALU.add)
                    elif n == 1:
                        m = dve.scalar_tensor_tensor(sp[:, 1], sp[:, 0], -1.0, sp[:, 0], ALU.mult, ALU.min)
                    elif n == 2:
                        dve.wait_ge(s["m_ex1"], q + 1)
                        m = dve.tensor_scalar(sp[:, 3], sp[:, 2], 2.0, None, ALU.add)
                    elif n == 3:
                        m = dve.reciprocal(sp[:, 4], sp[:, 3])
                    elif n == 4:
                        m = dve.tensor_tensor(sp[:, 5], sp[:, 2], sp[:, 4], ALU.mult)
                    elif n == 5:
                        m = dve.tensor_tensor(sp[:, 6], sp[:, 5], sp[:, 5], ALU.mult)
                    elif n == 6:
                        m = dve.tensor_scalar(sp[:, 7], sp[:, 6], 2.0 / 17, None, ALU.mult)
                    elif n < SPN - 1:
                        m = dve.scalar_tensor_tensor(sp[:, 7], sp[:, 7], 2.0 / (29 - 2 * n), sp[:, 6], ALU.add, ALU.mult)
                    elif n == SPN - 1:
                        m = dve.scalar_tensor_tensor(sp[:, 7], sp[:, 7], 2.0, sp[:, 5], ALU.add, ALU.mult)
                    elif n == SPN:
                        dve.scalar_tensor_tensor(dtv[:, hf], sp[:, 0], 0.0, sp[:, 7], ALU.max,
                                                 ALU.add).then_inc(s["m_dt"], 1)
                    elif n == SPN + 1:
                        dve.wait_ge(s["m_dt"], q * 2 + 1)
                        dve.tensor_tensor(av[:, hf], dtv[:, hf], negA[:].unsqueeze(1).broadcast_to([P, HT, H]),
                                          ALU.mult).then_inc(s["m_dt"], 1)
                    elif n == SPN + 2:
                        dve.wait_ge(s["m_dt"], q * 2 + 2)
                        dve.tensor_copy(ahr[:, hf], av[:, hf]).then_inc(s["m_a"], 1)
                    else:
                        dve.wait_ge(s["m_a"], q + 1)
                        dve.tensor_tensor(alr[:, hf], av[:, hf], fp(ahr[:, hf]), ALU.subtract).then_inc(s["m_al"], 1)
                    if n < SPN:
                        m.then_inc(s["m_sp"], 1)

            def tap(b, hf, c, w):
                j = (b * 2 + hf) * HT + c
                if w == 0:
                    dve.wait_ge(s["m_pj"], j + 1)
                    dve.wait_ge(s["m_t3"], j + 1)
                reached(dve, s["m_cn"], j * 3 + w)
                dve.scalar_tensor_tensor(cv[:, hf, c, :], pj[:, c, hf * HS + w:hf * HS + w + HS], cw[:, c, w:w + 1],
                                         cv[:, hf, c, :], ALU.mult, ALU.add).then_inc(s["m_cn"], 1)

            def heads(v):
                return v.rearrange("p (h e) -> p h e", h=H)

            def state_0(b):
                reached(dve, s["m_hc"], b * T)
                reached(dve, s["m_in"], b * T)
                reached(dve, s["m_h"], b * T)
                dve.memset(hst[:, 0], 0.0).then_inc(s["m_h0"], 1)

            def leave(n, t):
                dve.wait_ge(s["m_rr"], n + 1)
                dve.wait_ge(s["m_o"], n + 1)
                xt = X[:, n, :]
                dve.scalar_tensor_tensor(xt, PS[:, 7, 0:D], yrs[:, t:t + 1], xt, ALU.mult,
                                         ALU.add).then_inc(s["m_x"], 1)

            def mean_square(n, t):
                dve.wait_ge(s["m_sq"], n + 1)
                dve.tensor_scalar(yms[:, t:t + 1], ysq[:, t:t + 1], 1.0 / DI, EPS, ALU.mult,
                                  ALU.add).then_inc(s["m_ms"], 1)

            def sequence(b, first, last):
                for t in range(T):
                    hf, c = divmod(t, HT)
                    q, n = b * 2 + hf, b * T + t
                    nb, nh = (b, 1) if hf == 0 else (b + 1, 0)
                    more = not (last and hf == 1)
                    dve.wait_ge(s["m_G"], n + 1)
                    reached(dve, s["m_mt"], n)
                    dve.tensor_tensor(Gm, PS[:, 4, 0:P], upto, ALU.mult).then_inc(s["m_gm"], 1)
                    if more and c == 3:
                        softplus(nb, nh, SPN, SPN + 1)
                    dve.wait_ge(s["m_in"], n + 1)
                    dve.wait_ge(s["m_dec"], q + 1)
                    dve.tensor_tensor(heads(yb[:, 0, :]), heads(PS[:, 6, 0:DI]),
                                      dec[:, hf, 0, c, :].unsqueeze(2).broadcast_to([P, H, HD]),
                                      ALU.mult).then_inc(s["m_y1"], 1)
                    if more and c == 3:
                        softplus(nb, nh, SPN + 1, SPN + 2)
                    dve.wait_ge(s["m_gm"], n + 1)
                    dve.wait_ge(s["m_lx"], n + 1)
                    reached(dve, s["m_ie"], n)
                    dve.tensor_tensor(MT, Lx, Gm.unsqueeze(1).broadcast_to([P, H, P]), ALU.mult).then_inc(s["m_mt"], 1)
                    if more and c == 3:
                        softplus(nb, nh, SPN + 2, SPN + 3)
                    first_step = (None, 2, 9, SPN + 3)[c] if more else None

                    def fill(n):
                        if first_step is not None and not (c == 3 and n > 0):
                            softplus(nb, nh, first_step + n, first_step + n + 1)

                    if more:
                        tap(nb, nh, c, 0)
                    fill(0)
                    dve.wait_ge(s["m_st"], n + 1)
                    dve.wait_ge(s["m_hc"], n + 1)
                    dve.tensor_tensor(hst[:, 1 - c % 2], heads(PS[:, 6, DI:2 * DI]), hc[:],
                                      ALU.add).then_inc(s["m_h"], 1)
                    if t == T - 1 and not last:
                        state_0(b + 1)
                    fill(1)
                    if not (first and t == 0):
                        mean_square(n - 1, (t - 1) % T)
                    if more:
                        tap(nb, nh, c, 1)
                    fill(2)
                    if more and c == 0:
                        softplus(nb, nh, 0, 2)
                    if not last:
                        if c == 0:
                            norm_half(b + 1, hf)
                        if c == 1:
                            norm_half_2(b + 1, hf, (nb, nh, 5))
                        if c == 3:
                            rows_lo_half(b + 1, hf)
                    elif more and c == 1:
                        softplus(nb, nh, 5, 9)
                    dve.wait_ge(s["m_y1"], n + 1)
                    dve.wait_ge(s["m_ie"], n + 1)
                    dve.tensor_tensor(yb[:, 1, :], PS[:, 5, 0:DI], yb[:, 0, :], ALU.add).then_inc(s["m_y2"], 1)
                    if c == 2:
                        fill(3)
                    if more:
                        tap(nb, nh, c, 2)
                    if c == 2:
                        fill(4)
                    dve.wait_ge(s["m_y2"], n + 1)
                    if c == 0:
                        dve.wait_ge(s["m_cv"], q * 5 + 5)
                    reached(dve, s["m_yt"], n)
                    reached(dve, s["m_sq"], n)
                    dve.tensor_tensor(yb[:, 2, :], yb[:, 1, :], zs[:, hf, c, :], ALU.mult).then_inc(s["m_y4"], 1)
                    if c == 2:
                        fill(5)
                    if not (first and t == 0):
                        leave(n - 1, (t - 1) % T)
                if last:
                    mean_square(b * T + T - 1, T - 1)
                    leave(b * T + T - 1, T - 1)

            dve.wait_ge(s["f_x0"], NG * NV)
            dve.wait_ge(s["f_xw0"], NG)
            for k in range(4):
                dve.memset(pj[:, k, 0:PAD], 0.0).then_inc(s["m_cn0"], 1)
            dve.wait_ge(s["m_cn0"], 4)
            norm_half(0, 0)
            norm_half(0, 1)
            norm_half_2(0, 0, None)
            norm_half_2(0, 1, None)
            rows_lo_half(0, 0)
            rows_lo_half(0, 1)
            softplus(0, 0, 0, SPN + 4)
            for c in range(HT):
                for w in range(PAD):
                    tap(0, 0, c, w)
            state_0(0)
            sequence(0, True, False)
            with dve.Fori(1, B - 1) as b:
                sequence(b, False, False)
            sequence(B - 1, False, True)

            experts(1)


_INS = ['L0_attn_a_Q', 'L0_attn_a_rot_w', 'L0_attn_a_scale', 'L0_attn_a_bias', 'L0_attn_b_W_in',
        'L0_attn_b_conv_w', 'L0_attn_b_conv_b', 'L0_attn_b_dt_bias', 'L0_attn_b_A_log', 'L0_attn_b_D',
        'L0_attn_b_norm_w', 'L0_attn_b_W_out', 'L0_ffn_gate_w', 'L0_ffn_gate_b', 'L0_ffn_sw1', 'L0_ffn_sb1',
        'L0_ffn_sw2', 'L0_ffn_sb2', 'L0_ffn_rw1', 'L0_ffn_rb1', 'L0_ffn_rw2', 'L0_ffn_rb2']


def kernel(**inputs):
    import numpy as _np
    import concourse.bacc as _bacc
    from concourse import mybir as _mybir
    from concourse.bass_utils import run_bass_kernel_spmd as _run

    nc = _bacc.Bacc("TRN2", target_bir_lowering=False, num_devices=1)
    arrays, args = {}, []

    def give(name, a):
        arrays[name] = a
        args.append(nc.dram_tensor(name, a.shape, _mybir.dt.from_np(a.dtype), kind="ExternalInput").ap())

    for name in _INS:
        a = _np.ascontiguousarray(inputs[name])
        give(f"in_{name}_dram", a.reshape(1, 1) if a.ndim == 0 else a)
    n = 128
    r, c = _np.arange(n)[:, None], _np.arange(n)[None, :]
    swap = _np.where((r % 2 == 0) & (c == r + 1), 1.0, 0.0) - _np.where((r % 2 == 1) & (c == r - 1), 1.0, 0.0)
    give("in_masks_dram", _np.ascontiguousarray(
        _np.stack([_np.eye(n), swap, r <= c, r > c], axis=1).astype(_np.float32)))
    shape = inputs['L0_attn_a_Q'].shape
    args.append(nc.dram_tensor("out_0_dram", shape, _mybir.dt.float32, kind="ExternalOutput").ap())
    hybrid_block_kernel(nc, *args)
    return _run(nc, [arrays], core_ids=[0]).results[0]["out_0_dram"]
```
